# Optimizing a Trainium2 kernel written in Bass

```python
import numpy as np
import jax
import jax.numpy as jnp

def _softmax(x, axis=-1):
    return jax.nn.softmax(x, axis=axis)
def _gelu(x):
    return jax.nn.gelu(x, approximate=True)
def _silu(x):
    return jax.nn.silu(x)
def _sigmoid(x):
    return jax.nn.sigmoid(x)
def _layernorm(x, axis=-1, eps=1e-5):
    m = jnp.mean(x, axis=axis, keepdims=True)
    v = jnp.var(x, axis=axis, keepdims=True)
    return (x - m) / jnp.sqrt(v + eps)
def _scatter_add(tgt, idx, src, axis=0):
    return tgt.at[idx].add(src)
def _segment_sum(src, seg, n):
    return jax.ops.segment_sum(src, seg, n)

kernel_name = 'mk_dlrm_tower_d1_rec_57109d'

def setup_inputs(seed: int = 0):
    np.random.seed(seed)
    _w = jnp.asarray
    def _rec_inputs():
        import jax
        import jax.numpy as jnp
        _tk = jax.random.key(seed)
        ids = jnp.stack([jax.random.randint(jax.random.fold_in(_tk, 200 + f), (1024,), 0, v, jnp.int32) for f, v in enumerate([1000, 1000000, 1000, 1000000])], axis=1)
        tbl_0 = 0.05 * jax.random.normal(jax.random.fold_in(_tk, 500 + 0), (1000, 4), jnp.float32)
        tbl_1 = 0.05 * jax.random.normal(jax.random.fold_in(_tk, 500 + 1), (1000000, 4), jnp.float32)
        tbl_2 = 0.05 * jax.random.normal(jax.random.fold_in(_tk, 500 + 2), (1000, 4), jnp.float32)
        tbl_3 = 0.05 * jax.random.normal(jax.random.fold_in(_tk, 500 + 3), (1000000, 4), jnp.float32)
        _rk = jax.random.fold_in(_tk, 7)
        r_x = 7.22013e-05 + 1.00017 * jax.random.normal(jax.random.fold_in(_rk, 101), (1024, 2048), jnp.float32)
        W_top1 = 0.0197642 * jax.random.normal(jax.random.fold_in(_tk, 801), (2560, 512), jnp.float32)
        W_top2 = 0.0441942 * jax.random.normal(jax.random.fold_in(_tk, 802), (512, 256), jnp.float32)
        W_top3 = 0.0625 * jax.random.normal(jax.random.fold_in(_tk, 803), (256, 1), jnp.float32)
        b_top1 = jnp.zeros((512,), jnp.float32)
        b_top2 = jnp.zeros((256,), jnp.float32)
        return r_x, ids, tbl_0, tbl_1, tbl_2, tbl_3, W_top1, b_top1, W_top2, b_top2, W_top3
    r_x, ids, tbl_0, tbl_1, tbl_2, tbl_3, W_top1, b_top1, W_top2, b_top2, W_top3 = _rec_inputs()
    def _L0_rec_setup():
        import jax, jax.numpy as jnp
        import numpy as np
        B, IN, HID, D, N, OUT = (4096, 2048, 2048, 512, 4, 512)
        H = 8
        HD = D // H

        def _ln(x, g, b):
            m = x.mean(-1, keepdims=True)
            v = ((x - m) ** 2).mean(-1, keepdims=True)
            return (x - m) / jnp.sqrt(v + 1e-05) * g + b
        key = jax.random.key(seed)
        ks = jax.random.split(key, 32)

        def nrm(k, shape, scale=0.02):
            return jax.random.normal(k, shape, jnp.float32) * scale
        inp = {}
        inp['x'] = jax.random.normal(ks[0], (B, IN), jnp.float32)
        inp['strength'] = jax.random.uniform(ks[1], (B, N, N), jnp.float32)
        for t, i in (('er', 2), ('ei', 4)):
            inp[t + '_W1'] = nrm(ks[i], (HID, IN))
            inp[t + '_b1'] = jnp.zeros((HID,), jnp.float32)
            inp[t + '_g1'] = jnp.ones((HID,), jnp.float32)
            inp[t + '_be1'] = jnp.zeros((HID,), jnp.float32)
            inp[t + '_W2'] = nrm(ks[i + 1], (N * D, HID))
            inp[t + '_b2'] = jnp.zeros((N * D,), jnp.float32)
        names = ['Wq_r', 'Wq_i', 'Wk_r', 'Wk_i', 'Wv_r', 'Wv_i', 'Wo_r', 'Wo_i']
        for j, nm in enumerate(names):
            inp[nm] = nrm(ks[6 + j], (D, D))
            inp['b' + nm[1:]] = jnp.zeros((D,), jnp.float32)
        inp['int_Wr'] = jnp.tile(jnp.eye(D, dtype=jnp.float32)[None], (N, 1, 1))
        inp['int_Wi'] = jnp.zeros((N, D, D), jnp.float32)
        inp['meas_Mr'] = nrm(ks[20], (OUT, D), 1.0 / np.sqrt(D))
        inp['meas_Mi'] = nrm(ks[21], (OUT, D), 1.0 / np.sqrt(D))
        inp['post_W'] = nrm(ks[22], (OUT, OUT))
        inp['post_b'] = jnp.zeros((OUT,), jnp.float32)
        inp['post_g'] = jnp.ones((OUT,), jnp.float32)
        inp['post_be'] = jnp.zeros((OUT,), jnp.float32)
        return inp
    _L0_rec_all = _L0_rec_setup()
    _L0_rec_in = {k: v for k, v in _L0_rec_all.items() if k in ('er_W1', 'er_b1', 'er_g1', 'er_be1', 'er_W2', 'er_b2', 'ei_W1', 'ei_b1', 'ei_g1', 'ei_be1', 'ei_W2', 'ei_b2', 'Wq_r', 'bq_r', 'Wq_i', 'bq_i', 'Wk_r', 'bk_r', 'Wk_i', 'bk_i', 'Wv_r', 'bv_r', 'Wv_i', 'bv_i', 'Wo_r', 'bo_r', 'Wo_i', 'bo_i', 'int_Wr', 'int_Wi', 'meas_Mr', 'meas_Mi', 'post_W', 'post_b', 'post_g', 'post_be', )}
    del _L0_rec_all

    return {
        "r_x": r_x,
        "ids": ids,
        "tbl_0": tbl_0,
        "tbl_1": tbl_1,
        "tbl_2": tbl_2,
        "tbl_3": tbl_3,
        "W_top1": W_top1,
        "b_top1": b_top1,
        "W_top2": W_top2,
        "b_top2": b_top2,
        "W_top3": W_top3,
        "L0_rec_er_W1": _L0_rec_in["er_W1"],
        "L0_rec_er_b1": _L0_rec_in["er_b1"],
        "L0_rec_er_g1": _L0_rec_in["er_g1"],
        "L0_rec_er_be1": _L0_rec_in["er_be1"],
        "L0_rec_er_W2": _L0_rec_in["er_W2"],
        "L0_rec_er_b2": _L0_rec_in["er_b2"],
        "L0_rec_ei_W1": _L0_rec_in["ei_W1"],
        "L0_rec_ei_b1": _L0_rec_in["ei_b1"],
        "L0_rec_ei_g1": _L0_rec_in["ei_g1"],
        "L0_rec_ei_be1": _L0_rec_in["ei_be1"],
        "L0_rec_ei_W2": _L0_rec_in["ei_W2"],
        "L0_rec_ei_b2": _L0_rec_in["ei_b2"],
        "L0_rec_Wq_r": _L0_rec_in["Wq_r"],
        "L0_rec_bq_r": _L0_rec_in["bq_r"],
        "L0_rec_Wq_i": _L0_rec_in["Wq_i"],
        "L0_rec_bq_i": _L0_rec_in["bq_i"],
        "L0_rec_Wk_r": _L0_rec_in["Wk_r"],
        "L0_rec_bk_r": _L0_rec_in["bk_r"],
        "L0_rec_Wk_i": _L0_rec_in["Wk_i"],
        "L0_rec_bk_i": _L0_rec_in["bk_i"],
        "L0_rec_Wv_r": _L0_rec_in["Wv_r"],
        "L0_rec_bv_r": _L0_rec_in["bv_r"],
        "L0_rec_Wv_i": _L0_rec_in["Wv_i"],
        "L0_rec_bv_i": _L0_rec_in["bv_i"],
        "L0_rec_Wo_r": _L0_rec_in["Wo_r"],
        "L0_rec_bo_r": _L0_rec_in["bo_r"],
        "L0_rec_Wo_i": _L0_rec_in["Wo_i"],
        "L0_rec_bo_i": _L0_rec_in["bo_i"],
        "L0_rec_int_Wr": _L0_rec_in["int_Wr"],
        "L0_rec_int_Wi": _L0_rec_in["int_Wi"],
        "L0_rec_meas_Mr": _L0_rec_in["meas_Mr"],
        "L0_rec_meas_Mi": _L0_rec_in["meas_Mi"],
        "L0_rec_post_W": _L0_rec_in["post_W"],
        "L0_rec_post_b": _L0_rec_in["post_b"],
        "L0_rec_post_g": _L0_rec_in["post_g"],
        "L0_rec_post_be": _L0_rec_in["post_be"],
    }

def reference(r_x, ids, tbl_0, tbl_1, tbl_2, tbl_3, W_top1, b_top1, W_top2, b_top2, W_top3, L0_rec_er_W1, L0_rec_er_b1, L0_rec_er_g1, L0_rec_er_be1, L0_rec_er_W2, L0_rec_er_b2, L0_rec_ei_W1, L0_rec_ei_b1, L0_rec_ei_g1, L0_rec_ei_be1, L0_rec_ei_W2, L0_rec_ei_b2, L0_rec_Wq_r, L0_rec_bq_r, L0_rec_Wq_i, L0_rec_bq_i, L0_rec_Wk_r, L0_rec_bk_r, L0_rec_Wk_i, L0_rec_bk_i, L0_rec_Wv_r, L0_rec_bv_r, L0_rec_Wv_i, L0_rec_bv_i, L0_rec_Wo_r, L0_rec_bo_r, L0_rec_Wo_i, L0_rec_bo_i, L0_rec_int_Wr, L0_rec_int_Wi, L0_rec_meas_Mr, L0_rec_meas_Mi, L0_rec_post_W, L0_rec_post_b, L0_rec_post_g, L0_rec_post_be):
    import jax
    import jax.numpy as jnp
    def _L0_rec_ref(x, strength, er_W1, er_b1, er_g1, er_be1, er_W2, er_b2, ei_W1, ei_b1, ei_g1, ei_be1, ei_W2, ei_b2, Wq_r, bq_r, Wq_i, bq_i, Wk_r, bk_r, Wk_i, bk_i, Wv_r, bv_r, Wv_i, bv_i, Wo_r, bo_r, Wo_i, bo_i, int_Wr, int_Wi, meas_Mr, meas_Mi, post_W, post_b, post_g, post_be):
        import jax, jax.numpy as jnp
        import numpy as np
        B, IN, HID, D, N, OUT = (4096, 2048, 2048, 512, 4, 512)
        H = 8
        HD = D // H

        def _ln(x, g, b):
            m = x.mean(-1, keepdims=True)
            v = ((x - m) ** 2).mean(-1, keepdims=True)
            return (x - m) / jnp.sqrt(v + 1e-05) * g + b
        Bsz = x.shape[0]

        def enc(W1, b1, g, be, W2, b2):
            h = jax.nn.gelu(_ln(x @ W1.T + b1, g, be), approximate=False)
            return (h @ W2.T + b2).reshape(Bsz, N, D)
        sr = enc(er_W1, er_b1, er_g1, er_be1, er_W2, er_b2)
        si = enc(ei_W1, ei_b1, ei_g1, ei_be1, ei_W2, ei_b2)

        def heads(t):
            return t.reshape(Bsz, N, H, HD).transpose(0, 2, 1, 3)
        qr = heads(sr @ Wq_r.T + bq_r)
        qi = heads(si @ Wq_i.T + bq_i)
        kr = heads(sr @ Wk_r.T + bk_r)
        ki = heads(si @ Wk_i.T + bk_i)
        vr = heads(sr @ Wv_r.T + bv_r)
        vi = heads(si @ Wv_i.T + bv_i)
        ar = jnp.einsum('bhnd,bhmd->bhnm', qr, kr) + jnp.einsum('bhnd,bhmd->bhnm', qi, ki)
        ai = jnp.einsum('bhnd,bhmd->bhnm', qi, kr) - jnp.einsum('bhnd,bhmd->bhnm', qr, ki)
        mag = jnp.sqrt(ar ** 2 + ai ** 2 + 1e-08) * HD ** (-0.5)
        w = jax.nn.softmax(mag, axis=-1)
        out_r = jnp.einsum('bhnm,bhmd->bhnd', w, vr).transpose(0, 2, 1, 3).reshape(Bsz, N, D)
        out_i = jnp.einsum('bhnm,bhmd->bhnd', w, vi).transpose(0, 2, 1, 3).reshape(Bsz, N, D)
        attn_r = out_r @ Wo_r.T + bo_r
        attn_i = out_i @ Wo_i.T + bo_i
        R = jnp.einsum('bnd,ned->bne', attn_r, int_Wr) - jnp.einsum('bnd,ned->bne', attn_i, int_Wi)
        I = jnp.einsum('bnd,ned->bne', attn_r, int_Wi) + jnp.einsum('bnd,ned->bne', attn_i, int_Wr)
        Ri, Ii = (R[:, :, None, :], I[:, :, None, :])
        Rj, Ij = (R[:, None, :, :], I[:, None, :, :])
        phase = jnp.arctan2(Ii * Rj - Ri * Ij, Ri * Rj + Ii * Ij)
        f = jnp.cos(phase) * strength[..., None]
        sup_r = jnp.einsum('bijd,bjd->bd', f, R)
        sup_i = jnp.einsum('bijd,bjd->bd', f, I)
        norm = jnp.sqrt(jnp.sum(sup_r ** 2 + sup_i ** 2, axis=-1, keepdims=True) + 1e-08)
        sup_r = sup_r / norm
        sup_i = sup_i / norm
        mr = sup_r @ meas_Mr.T - sup_i @ meas_Mi.T
        mi = sup_r @ meas_Mi.T + sup_i @ meas_Mr.T
        amp = jnp.sqrt(mr ** 2 + mi ** 2)
        out = jax.nn.gelu(_ln(amp @ post_W.T + post_b, post_g, post_be), approximate=False)
        return out

    e = jnp.stack([tbl_0[ids[:, 0]], tbl_1[ids[:, 1]], tbl_2[ids[:, 2]], tbl_3[ids[:, 3]]], axis=1)
    z = _L0_rec_ref(r_x, e, L0_rec_er_W1, L0_rec_er_b1, L0_rec_er_g1, L0_rec_er_be1, L0_rec_er_W2, L0_rec_er_b2, L0_rec_ei_W1, L0_rec_ei_b1, L0_rec_ei_g1, L0_rec_ei_be1, L0_rec_ei_W2, L0_rec_ei_b2, L0_rec_Wq_r, L0_rec_bq_r, L0_rec_Wq_i, L0_rec_bq_i, L0_rec_Wk_r, L0_rec_bk_r, L0_rec_Wk_i, L0_rec_bk_i, L0_rec_Wv_r, L0_rec_bv_r, L0_rec_Wv_i, L0_rec_bv_i, L0_rec_Wo_r, L0_rec_bo_r, L0_rec_Wo_i, L0_rec_bo_i, L0_rec_int_Wr, L0_rec_int_Wi, L0_rec_meas_Mr, L0_rec_meas_Mi, L0_rec_post_W, L0_rec_post_b, L0_rec_post_g, L0_rec_post_be)
    z = z.reshape(z.shape[0], -1)
    h = jnp.concatenate([z, r_x], axis=1)
    h = jnp.maximum(h @ W_top1 + b_top1, 0.0)
    h = jnp.maximum(h @ W_top2 + b_top2, 0.0)
    y = h @ W_top3
    return y


_drawn_inputs = setup_inputs


def setup_inputs(seed=0):
    import zlib

    import numpy as np

    out = dict(_drawn_inputs(seed))
    spreads = {'b_top1': (0.0, 0.1),
     'b_top2': (0.0, 0.1),
     'L0_rec_er_b1': (0.0, 0.8),
     'L0_rec_er_g1': (1.0, 0.6),
     'L0_rec_er_be1': (0.0, 0.8),
     'L0_rec_er_b2': (0.0, 0.8),
     'L0_rec_ei_b1': (0.0, 0.8),
     'L0_rec_ei_g1': (1.0, 0.6),
     'L0_rec_ei_be1': (0.0, 0.8),
     'L0_rec_ei_b2': (0.0, 0.8),
     'L0_rec_bq_r': (0.0, 0.8),
     'L0_rec_bq_i': (0.0, 0.8),
     'L0_rec_bk_r': (0.0, 0.8),
     'L0_rec_bk_i': (0.0, 0.8),
     'L0_rec_bv_r': (0.0, 0.1),
     'L0_rec_bv_i': (0.0, 0.1),
     'L0_rec_bo_r': (0.0, 0.1),
     'L0_rec_bo_i': (0.0, 0.1),
     'L0_rec_int_Wi': (0.0, 0.1),
     'L0_rec_post_b': (0.0, 0.1),
     'L0_rec_post_g': (1.0, 0.2),
     'L0_rec_post_be': (0.0, 0.1)}
    factors = {'L0_rec_Wq_r': 8.0, 'L0_rec_Wq_i': 8.0, 'L0_rec_Wk_r': 8.0, 'L0_rec_Wk_i': 8.0}
    for name, (base, spread) in spreads.items():
        noise = np.random.default_rng([zlib.crc32(name.encode()), seed]).standard_normal(out[name].shape)
        drawn = base * np.exp(spread * noise) if base else spread * noise
        out[name] = jnp.asarray(drawn.astype(out[name].dtype))
    for name, factor in factors.items():
        out[name] = (out[name] * factor).astype(out[name].dtype)
    return out
```

```python
from contextlib import ExitStack

import concourse.bass as bass
from concourse import mybir

F32 = mybir.dt.float32
F32R = mybir.dt.float32r
BF16 = mybir.dt.bfloat16
I32 = mybir.dt.int32
U32 = mybir.dt.uint32
ACT = mybir.ActivationFunctionType
ALU = mybir.AluOpType
AX_X = mybir.AxisListType.X

P = 128
B = 1024
IN = 2048
D = 512
NT = 4
H = 8
HD = D // H
BANK = 512
KT = IN // P
DK = D // P
GROUP = 4
CB = 128
CHUNKS = B // CB
TOK = CB * NT
LN_EPS = 1e-5
EPS = 1e-8


class Mem:

    def __init__(self, nc, ctx, prefix):
        self.nc, self.ctx, self.prefix = nc, ctx, prefix

    def sb(self, name, shape, dt=F32):
        return self.ctx.enter_context(self.nc.sbuf_tensor(self.prefix + name, shape, dt))

    def psum(self, name, shape):
        return self.ctx.enter_context(self.nc.psum_tensor(self.prefix + name, shape, F32))

    def sem(self, name):
        return self.ctx.enter_context(self.nc.semaphore(self.prefix + name))


def encoders(nc, io, scratch, keep):
    W1_GROUPS, TOP, GROUPS = 8, 8, 17
    RING = 4
    HALF = B // 2
    with ExitStack() as ctx:
        m = Mem(nc, ctx, "enc_")
        src_hi = m.sb("src_hi", [P, KT, B], F32R)
        src_lo = m.sb("src_lo", [P, KT, B], F32R)
        src_stage = m.sb("src_stage", [P, 2, B])
        w_stage = m.sb("w_stage", [P, RING, D])
        w_hi = m.sb("w_hi", [P, RING, D], F32R)
        w_lo = m.sb("w_lo", [P, RING, D], F32R)
        out_stage = m.sb("out_stage", [P, 8, BANK])
        square = m.sb("square", [P, 2, BANK])
        stats = m.sb("stats", [P, 2, 2, B])
        bias = m.sb("bias", [P, GROUPS * GROUP])
        group_bias = m.sb("group_bias", [P, GROUP])
        ln_g = m.sb("ln_g", [P, 2 * KT])
        ln_b = m.sb("ln_b", [P, 2 * KT])
        mean_w = m.sb("mean_w", [P, P])
        acc = m.psum("acc", [P, 8, BANK])

        consts_in = m.sem("consts_in")
        w_in = [m.sem(f"w_in{i}") for i in range(RING)]
        src_in = [m.sem(f"src_in{i}") for i in range(2)]
        w_hi_done = m.sem("w_hi_done")
        w_ready = m.sem("w_ready")
        w_used = m.sem("w_used")
        bank_ready = m.sem("bank_ready")
        bank_free = m.sem("bank_free")
        norm_done = m.sem("norm_done")
        src_hi_done = m.sem("src_hi_done")
        src_ready = m.sem("src_ready")
        bias_set = m.sem("bias_set")
        gelu_done = m.sem("gelu_done")
        centred = m.sem("centred")
        squared = m.sem("squared")
        summed = m.sem("summed")
        stored = m.sem("stored")
        zeroed = m.sem("zeroed")
        stats_mm = m.sem("stats_mm")
        stats_dve = m.sem("stats_dve")
        stats_std = m.sem("stats_std")
        stats_read = m.sem("stats_read")
        pool_set = m.sem("pool_set")
        ids_in = m.sem("ids_in")
        gathered = m.sem("gathered")

        block = ctx.enter_context(nc.Block())

        w_all = io["w_enc"]
        pre = scratch["pre"]
        used_before = lambda g, k: (w_used, 15 * g + k - 3) if k >= 4 else (
            (bank_ready, 8 * g) if k == 3 else (w_used, 15 * g + k - 2))

        @block.sync
        def _(sp):
            sp.dma_start(bias[:, :], io["b_enc"]).then_inc(consts_in, 16)
            sp.dma_start(ln_g[:, :], io["ln_g"]).then_inc(consts_in, 16)
            sp.dma_start(ln_b[:, :], io["ln_b"]).then_inc(consts_in, 16)

            def load(g, k):
                sp.dma_start(w_stage[:, k % RING, :], w_all[g, k]).then_inc(w_in[k % RING], 16)

            for k in range(RING):
                load(0, k)
            for k in range(RING, KT):
                sp.wait_ge(w_ready, k - RING + 1)
                load(0, k)
            with sp.Fori(1, GROUPS) as g:
                for k in range(KT):
                    sp.wait_ge(w_ready, 16 * g + k - RING + 1)
                    load(g, k)

        @block.gpsimd
        def _(pool):
            for k in range(2):
                pool.dma_start(src_stage[:, k, :], io["xT"][k]).then_inc(src_in[k], 16)
            nc.gpsimd.memset(mean_w[:, :], 1.0 / IN).then_inc(pool_set, 1)
            nc.gpsimd.memset(keep["ident"][:, :], 0.0).then_inc(pool_set, 1)
            pool.wait_ge(pool_set, 2)
            nc.gpsimd.affine_select(out=keep["ident"][:, :], in_=keep["ident"][:, :],
                                    compare_op=ALU.not_equal, fill=1.0, base=0,
                                    pattern=[[-1, P]], channel_multiplier=1).then_inc(pool_set, 1)
            for k in range(2, KT):
                pool.wait_ge(src_ready, k - 1)
                pool.dma_start(src_stage[:, k % 2, :], io["xT"][k]).then_inc(src_in[k % 2], 16)
            pool.dma_start(keep["ids"][:, :, :], io["ids"]).then_inc(ids_in, 16)
            pool.wait_ge(ids_in, 16)
            for i in range(NT):
                for c in range(CHUNKS):
                    pool.indirect_dma_start(
                        keep["strength"][:, (c * NT + i) * NT:(c * NT + i + 1) * NT], None, io[f"tbl_{i}"],
                        bass.IndirectOffsetOnAxis(ap=keep["ids"][:, c, i:i + 1], axis=0)).then_inc(gathered, 16)

            def store(g):
                for b in range(8):
                    pool.wait_ge(bank_free, 8 * g + 8 + b + 1)
                    pool.dma_start(pre[g, b // 2, :, (b % 2) * HALF:(b % 2 + 1) * HALF],
                                   out_stage[:, b, :]).then_inc(stored, 16)

            def load_h(e):
                for k in range(KT):
                    pool.wait_ge(src_ready, KT * (e + 1) + k - 1)
                    pool.dma_start(src_stage[:, k % 2, :], pre[4 * e + k // 4, k % 4]).then_inc(src_in[k % 2], 16)

            with pool.Fori(0, W1_GROUPS) as g:
                store(g)
            pool.wait_ge(stored, 16 * 8 * W1_GROUPS)
            pool.wait_ge(stats_dve, 10)
            load_h(0)
            with pool.Fori(TOP, TOP + 4) as g:
                store(g)
            load_h(1)
            with pool.Fori(TOP + 4, GROUPS) as g:
                store(g)
            pool.wait_ge(stored, 16 * 8 * GROUPS)
            pool.wait_ge(gathered, 16 * NT * CHUNKS)

        @block.scalar
        def _(act):
            act.sem_inc(bank_free, 8)
            act.wait_ge(consts_in, 48)

            def split_w(g, k):
                act.wait_ge(w_in[k % RING], 16 * (4 * g + k // RING + 1))
                act.activation(w_hi[:, k % RING, :], w_stage[:, k % RING, :],
                               ACT.Identity).then_inc(w_hi_done, 1)

            def split_w_later(g, k):
                act.wait_ge(*used_before(g, k))
                split_w(g, k)

            def split_src(s, k):
                act.activation(src_hi[:, k, :], src_stage[:, k % 2, :], ACT.Identity).then_inc(src_hi_done, 1)

            def evacuate(g, with_stats):
                act.activation(group_bias[:, :], bias[:, bass.ds(g * GROUP, GROUP)], ACT.Copy).then_inc(bias_set, 1)
                act.wait_ge(bias_set, g + 1)
                for b in range(8):
                    act.wait_ge(bank_ready, 8 * g + b + 1)
                    if with_stats:
                        if not isinstance(g, int) or b >= 2:
                            act.wait_ge(summed, 16 * g + 2 * b - 3)
                        act.activation(square[:, b % 2, :], acc[:, b, :], ACT.Square,
                                       bias=group_bias[:, b // 2:b // 2 + 1]).then_inc(squared, 1)
                    if not isinstance(g, int) or g > 0:
                        act.wait_ge(stored, 128 * g)
                    act.activation(out_stage[:, b, :], acc[:, b, :], ACT.Identity,
                                   bias=group_bias[:, b // 2:b // 2 + 1]).then_inc(bank_free, 1)

            def make_h(e, k):
                act.wait_ge(norm_done, KT * e + k + 1)
                if k < 15:
                    act.wait_ge(w_used, 15 * (8 + 4 * e) + k + 1)
                else:
                    act.wait_ge(bank_ready, 8 * (9 + 4 * e))
                act.activation(src_stage[:, k % 2, :], src_stage[:, k % 2, :], ACT.Gelu,
                               scale=ln_g[:, e * KT + k:e * KT + k + 1],
                               bias=ln_b[:, e * KT + k:e * KT + k + 1]).then_inc(gelu_done, 1)
                act.wait_ge(gelu_done, KT * e + k + 1)
                split_src(e + 1, k)

            for k in range(KT):
                act.wait_ge(src_in[k % 2], 16 * (k // 2 + 1))
                split_src(0, k)
                if k < RING:
                    split_w(0, k)
                else:
                    act.wait_ge(w_used, k - 3)
                    split_w(0, k)
            for k in range(RING):
                split_w_later(1, k)
            evacuate(0, True)
            with act.Fori(1, W1_GROUPS) as g:
                for k in range(RING, KT):
                    split_w_later(g, k)
                for k in range(RING):
                    split_w_later(g + 1, k)
                evacuate(g, True)
            act.wait_ge(summed, 16 * W1_GROUPS)
            for e in range(2):
                act.wait_ge(stats_dve, 4 * e + 4)
                act.activation(stats[:, e, 1, :], stats[:, e, 1, :], ACT.Sqrt).then_inc(stats_std, 1)
            for e in range(2):
                g = TOP + 4 * e
                for k in range(RING, KT):
                    split_w_later(g, k)
                    make_h(e, k - RING)
                for k in range(RING):
                    split_w_later(g + 1, k)
                    make_h(e, KT - RING + k)
                evacuate(g, False)
                with act.Fori(g + 1, g + 4) as g:
                    for k in range(RING, KT):
                        split_w_later(g, k)
                    for k in range(RING):
                        split_w_later(g + 1, k)
                    evacuate(g, False)
            for k in range(RING, KT):
                split_w_later(GROUPS - 1, k)
            evacuate(GROUPS - 1, False)

        @block.vector
        def _(dve):
            def split_w(g, k):
                dve.wait_ge(w_hi_done, 16 * g + k + 1)
                dve.tensor_tensor(w_lo[:, k % RING, :], w_stage[:, k % RING, :],
                                  w_hi[:, k % RING, :].bitcast(F32), ALU.subtract).then_inc(w_ready, 1)

            def split_src(s, k):
                dve.wait_ge(src_hi_done, KT * s + k + 1)
                dve.tensor_tensor(src_lo[:, k, :], src_stage[:, k % 2, :], src_hi[:, k, :].bitcast(F32),
                                  ALU.subtract).then_inc(src_ready, 1)

            def add_stats(g, e):
                for b in range(8):
                    half = slice((b % 2) * HALF, (b % 2 + 1) * HALF)
                    dve.wait_ge(squared, 8 * g + b + 1)
                    if not isinstance(g, int) or b >= 2:
                        dve.wait_ge(summed, 16 * g + 2 * b - 3)
                    dve.tensor_tensor(stats[:, e, 1, half], stats[:, e, 1, half], square[:, b % 2, :],
                                      ALU.add).then_inc(summed, 1)
                    dve.wait_ge(bank_free, 8 + 8 * g + b + 1)
                    if not isinstance(g, int) or b >= 2:
                        dve.wait_ge(summed, 16 * g + 2 * b - 2)
                    dve.tensor_tensor(stats[:, e, 0, half], stats[:, e, 0, half], out_stage[:, b, :],
                                      ALU.add).then_inc(summed, 1)

            def normalise(e, k):
                dve.wait_ge(src_in[k % 2], 16 * (8 * (e + 1) + k // 2 + 1))
                dve.tensor_tensor(src_stage[:, k % 2, :], src_stage[:, k % 2, :], stats[:, e, 0, :],
                                  ALU.subtract).then_inc(centred, 1)
                dve.wait_ge(centred, KT * e + k + 1)
                dve.tensor_tensor(src_stage[:, k % 2, :], src_stage[:, k % 2, :], stats[:, e, 1, :],
                                  ALU.mult).then_inc(norm_done, 1)

            dve.memset(stats[:, :, :, :], 0.0).then_inc(zeroed, 1)
            for k in range(KT):
                split_src(0, k)
                split_w(0, k)
            for k in range(RING):
                split_w(1, k)
            dve.wait_ge(zeroed, 1)
            add_stats(0, 0)
            for e in range(2):
                with dve.Fori(max(4 * e, 1), 4 * e + 4) as g:
                    for k in range(RING, KT):
                        split_w(g, k)
                    for k in range(RING):
                        split_w(g + 1, k)
                    add_stats(g, e)
            for e in range(2):
                both = lambda i: acc[:, 4 * e + 2 * i:4 * e + 2 * i + 2, :].rearrange("p h n -> p (h n)")
                dve.wait_ge(stats_mm, 4 * e + 4)
                dve.tensor_copy(stats[:, e, 0, :], both(0)).then_inc(stats_dve, 1)
                dve.wait_ge(stats_dve, 4 * e + 1)
                dve.tensor_tensor(src_stage[:, e, :], stats[:, e, 0, :], stats[:, e, 0, :],
                                  ALU.mult).then_inc(stats_dve, 1)
                dve.wait_ge(stats_dve, 4 * e + 2)
                dve.tensor_tensor(stats[:, e, 1, :], both(1), src_stage[:, e, :],
                                  ALU.subtract).then_inc(stats_dve, 1)
                dve.wait_ge(stats_dve, 4 * e + 3)
                dve.tensor_scalar(stats[:, e, 1, :], stats[:, e, 1, :], 0.0, LN_EPS, ALU.max,
                                  ALU.add).then_inc(stats_dve, 1)
            for e in range(2):
                dve.wait_ge(stats_std, e + 1)
                dve.reciprocal(stats[:, e, 1, :], stats[:, e, 1, :]).then_inc(stats_dve, 1)
            dve.wait_ge(stats_dve, 10)

            for e in range(2):
                g = TOP + 4 * e
                for k in range(RING, KT):
                    split_w(g, k)
                    normalise(e, k - RING)
                    split_src(e + 1, k - RING)
                for k in range(RING):
                    split_w(g + 1, k)
                    normalise(e, KT - RING + k)
                    split_src(e + 1, KT - RING + k)
                with dve.Fori(g + 1, g + 4) as g:
                    for k in range(RING, KT):
                        split_w(g, k)
                    for k in range(RING):
                        split_w(g + 1, k)
            for k in range(RING, KT):
                split_w(GROUPS - 1, k)

        @block.tensor
        def _(pe):
            def gemm(g, source):
                for k in range(KT):
                    if not isinstance(g, int):
                        pe.wait_ge(w_ready, KT * g + k + 1)
                    else:
                        pe.wait_ge(w_ready, KT * g + k + 1)
                    pe.wait_ge(src_ready, KT * source + k + 1)
                    for mt in range(GROUP):
                        hi = w_hi[:, k % RING, mt * P:(mt + 1) * P]
                        lo = w_lo[:, k % RING, mt * P:(mt + 1) * P]
                        for h in range(2):
                            if k == 0:
                                pe.wait_ge(bank_free, 8 * g + 2 * mt + h + 1)
                            cols = slice(h * HALF, (h + 1) * HALF)
                            pe.matmul(acc[:, 2 * mt + h, :], hi, src_hi[:, k, cols], start=k == 0, stop=False)
                            pe.matmul(acc[:, 2 * mt + h, :], hi, src_lo[:, k, cols], start=False, stop=False)
                        for h in range(2):
                            cols = slice(h * HALF, (h + 1) * HALF)
                            last = pe.matmul(acc[:, 2 * mt + h, :], lo, src_hi[:, k, cols],
                                             start=False, stop=k == KT - 1)
                            if k == KT - 1:
                                last.then_inc(bank_ready, 1)
                    if k < KT - 1:
                        last.then_inc(w_used, 1)

            with pe.Fori(0, W1_GROUPS) as g:
                gemm(g, 0)
            pe.wait_ge(summed, 16 * W1_GROUPS)
            pe.wait_ge(bank_free, 8 * W1_GROUPS + 8)
            pe.wait_ge(pool_set, 1)
            for e in range(2):
                for i in range(2):
                    for h in range(2):
                        pe.matmul(acc[:, 4 * e + 2 * i + h, :], mean_w[:, :],
                                  stats[:, e, i, h * HALF:(h + 1) * HALF], start=True, stop=True
                                  ).then_inc(stats_mm, 1)
            pe.wait_ge(stats_dve, 7)
            gemm(TOP, 0)
            with pe.Fori(TOP + 1, TOP + 5) as g:
                gemm(g, 1)
            with pe.Fori(TOP + 5, GROUPS) as g:
                gemm(g, 2)


def attention(nc, io, scratch, keep):
    QR, QI, KR, KI, VR, VI = range(6)
    BLK = TOK // P
    SB = P // NT
    W_TILES = 6 * DK
    with ExitStack() as ctx:
        m = Mem(nc, ctx, "att_")
        stage = m.sb("stage", [P, 4, D])
        w_hi = m.sb("w_hi", [P, 6, DK, D], F32R)
        w_lo = m.sb("w_lo", [P, 6, DK, D], F32R)
        s_hi = m.sb("s_hi", [P, 2, DK, TOK], F32R)
        s_lo = m.sb("s_lo", [P, 2, DK, TOK], F32R)
        q1 = m.sb("q1", [P, 2, 2, TOK])
        q2 = m.sb("q2", [P, 2, 2, TOK])
        kk = m.sb("kk", [P, 2, 2, TOK])
        val = m.sb("val", [P, BLK, H, 2, HD])
        sq_r = m.sb("sq_r", [P, 2 * BLK, P])
        sq_i = m.sb("sq_i", [P, 2 * BLK, P])
        mask = m.sb("mask", [P, SB, NT])
        prob = m.sb("prob", [P, H, BLK, NT])
        peak = m.sb("peak", [P, H * BLK])
        total = m.sb("total", [P, H * BLK])
        wide = m.sb("wide", [P, H, P])
        wide_t = m.sb("wide_t", [P, H, P])
        out_st = m.sb("out_st", [P, 2, H, P])
        qk_bias = m.sb("qk_bias", [P, 4, DK])
        v_bias = m.sb("v_bias", [P, H])
        ps = m.psum("ps", [P, 8, BANK])

        w_bias_in = m.sem("w_bias_in")
        tile_in = [m.sem(f"tile_in{i}") for i in range(4)]
        hi_done = m.sem("hi_done")
        split_done = m.sem("split_done")
        gemm_ready = m.sem("gemm_ready")
        even_free = m.sem("even_free")
        odd_free = m.sem("odd_free")
        scores_done = m.sem("scores_done")
        score_free = m.sem("score_free")
        extracted = m.sem("extracted")
        chain = m.sem("chain")
        root_done = m.sem("root_done")
        shifted = m.sem("shifted")
        exp_done = m.sem("exp_done")
        prob_ready = m.sem("prob_ready")
        wide_ready = m.sem("wide_ready")
        turned = m.sem("turned")
        turned_out = m.sem("turned_out")
        mixed = m.sem("mixed")
        mixed_out = m.sem("mixed_out")
        stored = [m.sem(f"stored{i}") for i in range(2)]
        mask_set = m.sem("mask_set")

        block = ctx.enter_context(nc.Block())
        s_src = scratch["pre"]
        out = scratch["mixed"]

        @block.sync
        def _(sp):
            sp.sem_inc(stored[0], 16)
            sp.sem_inc(stored[1], 16)
            sp.dma_start(qk_bias[:, :, :], io["b_qk"]).then_inc(w_bias_in, 16)
            sp.dma_start(v_bias[:, :], io["b_v"]).then_inc(w_bias_in, 16)
            for t in range(W_TILES):
                if t >= 4:
                    sp.wait_ge(split_done, t - 3)
                sp.dma_start(stage[:, t % 4, :], io["w_qkv"][t]).then_inc(tile_in[t % 4], 16)

            def load(c, tiles):
                for t in tiles:
                    e, kt = t // DK, t % DK
                    sp.wait_ge(split_done, W_TILES + 8 * c + t - 3)
                    src = s_src[9 + 4 * e:13 + 4 * e, kt, :, bass.ds(c * CB, CB)].rearrange("n p b -> p n b")
                    sp.dma_start(stage[:, t % 4, :].rearrange("p (n b) -> p n b", n=NT),
                                 src).then_inc(tile_in[t % 4], 16)

            def store(c, blk):
                sp.wait_ge(mixed_out, BLK * c + blk + 2)
                sp.dma_start(out[c, blk], out_st[:, blk % 2, :, :]).then_inc(stored[blk % 2], 16)

            load(0, range(8))
            with sp.Fori(0, CHUNKS - 1) as c:
                load(c + 1, range(0, 6))
                store(c, 0)
                load(c + 1, range(6, 8))
                for blk in range(1, BLK):
                    store(c, blk)
            for blk in range(BLK):
                store(CHUNKS - 1, blk)
            for i in range(2):
                sp.wait_ge(stored[i], 16 * (1 + CHUNKS * BLK // 2))

        @block.gpsimd
        def _(pool):
            pool.sem_inc(wide_ready, 1)
            nc.gpsimd.memset(mask[:, :, :], 1.0).then_inc(mask_set, 1)
            pool.wait_ge(mask_set, 1)
            nc.gpsimd.affine_select(out=mask[:, :, :], in_=mask[:, :, :], compare_op=ALU.is_ge, fill=0.0,
                                    base=0, pattern=[[-NT, SB], [0, NT]], channel_multiplier=1).then_inc(mask_set, 1)
            pool.wait_ge(mask_set, 2)
            nc.gpsimd.affine_select(out=mask[:, :, :], in_=mask[:, :, :], compare_op=ALU.is_ge, fill=0.0,
                                    base=NT - 1, pattern=[[NT, SB], [0, NT]], channel_multiplier=-1
                                    ).then_inc(mask_set, 1)
            pool.wait_ge(mask_set, 3)
            with pool.Fori(0, CHUNKS) as c:
                for blk in range(BLK):
                    pool.wait_ge(prob_ready, c + 1)
                    pool.wait_ge(turned, BLK * c + blk + 1)
                    nc.gpsimd.tensor_tensor(
                        wide[:, :, :].rearrange("p h (b n) -> p h b n", n=NT),
                        prob[:, :, blk, :].unsqueeze(2).broadcast_to([P, H, SB, NT]),
                        mask[:, :, :].unsqueeze(1).broadcast_to([P, H, SB, NT]), ALU.mult).then_inc(wide_ready, 1)

        @block.scalar
        def _(act):
            act.sem_inc(odd_free, 2)
            act.sem_inc(turned_out, 1)
            act.wait_ge(w_bias_in, 32)

            def split_s(c, t):
                act.wait_ge(tile_in[t % 4], 16 * (W_TILES // 4 + 2 * c + t // 4 + 1))
                act.activation(s_hi[:, t // DK, t % DK, :].rearrange("p (b n) -> p b n", n=NT),
                               stage[:, t % 4, :].rearrange("p (n b) -> p b n", n=NT),
                               ACT.Identity).then_inc(hi_done, 1)

            def evacuate(c, mt):
                act.wait_ge(gemm_ready, 24 * c + 4 * mt + 2)
                act.wait_ge(scores_done, 4 * c + mt + 1)
                slot = mt % 2
                for h in range(2):
                    rows = slice(h * HD, (h + 1) * HD)
                    b = qk_bias[rows, QI, mt:mt + 1]
                    act.activation(q1[HD:P, slot, h, :], ps[rows, QI, :], ACT.Identity, bias=b)
                for h in range(2):
                    rows = slice(h * HD, (h + 1) * HD)
                    b = qk_bias[rows, QI, mt:mt + 1]
                    last = act.activation(q2[0:HD, slot, h, :], ps[rows, QI, :], ACT.Identity, bias=b)
                last.then_inc(odd_free, 1)
                act.wait_ge(gemm_ready, 24 * c + 4 * mt + 4)
                for h in range(2):
                    rows = slice(h * HD, (h + 1) * HD)
                    last = act.activation(kk[HD:P, slot, h, :], ps[rows, KI, :], ACT.Identity,
                                          bias=qk_bias[rows, KI, mt:mt + 1])
                last.then_inc(odd_free, 1)

            def square(c, mt):
                act.wait_ge(scores_done, 4 * c + mt + 3)
                act.wait_ge(extracted, 4 * c + mt + 1)
                act.activation(sq_r[:, :, :], ps[:, 4:6, :].rearrange("p a (k n) -> p (a k) n", k=BLK), ACT.Square)
                act.activation(sq_i[:, :, :], ps[:, 6:8, :].rearrange("p a (k n) -> p (a k) n", k=BLK),
                               ACT.Square).then_inc(score_free, 1)

            def evacuate_v(c, blk):
                act.wait_ge(gemm_ready, 24 * c + 16 + 2 * blk + 2)
                act.activation(val[:, blk, :, 1, :],
                               ps[:, (2 * blk + 1) % 4, :].rearrange("p (h d) -> p h d", h=H),
                               ACT.Copy).then_inc(odd_free, 1)

            def chunk(c, last_chunk):
                evacuate(c, 0)
                for mt in range(1, 4):
                    evacuate(c, mt)
                    square(c, mt - 1)
                act.wait_ge(mixed, BLK * c + 1)
                evacuate_v(c, 0)
                square(c, 3)
                act.wait_ge(shifted, 2 * c + 1)
                act.activation(prob[:, :, :, :], prob[:, :, :, :], ACT.Sqrt).then_inc(root_done, 1)
                evacuate_v(c, 1)
                act.wait_ge(shifted, 2 * c + 2)
                act.activation(prob[:, :, :, :], prob[:, :, :, :], ACT.Exp, scale=HD ** -0.5).then_inc(exp_done, 1)
                evacuate_v(c, 2)
                evacuate_v(c, 3)
                for blk in range(BLK):
                    act.wait_ge(turned, BLK * c + blk + 2)
                    act.wait_ge(mixed, BLK * c + blk + 1)
                    act.activation(wide_t[:, :, :], ps[:, 4:6, :].rearrange("p a (h n) -> p (a h) n", n=P),
                                   ACT.Copy).then_inc(turned_out, 1)
                    if not last_chunk:
                        for t in range(2 * blk, 2 * blk + 2):
                            split_s(c + 1, t)

            for t in range(W_TILES):
                act.wait_ge(tile_in[t % 4], 16 * (t // 4 + 1))
                act.activation(w_hi[:, t // DK, t % DK, :], stage[:, t % 4, :], ACT.Identity).then_inc(hi_done, 1)
            for t in range(8):
                split_s(0, t)
            with act.Fori(0, CHUNKS - 1) as c:
                chunk(c, False)
            chunk(CHUNKS - 1, True)

        @block.vector
        def _(dve):
            dve.sem_inc(even_free, 2)
            dve.sem_inc(extracted, 1)
            dve.sem_inc(mixed_out, 1)
            dve.wait_ge(w_bias_in, 32)
            dve.wait_ge(mask_set, 3)

            def split_s(c, t):
                dve.wait_ge(hi_done, W_TILES + 8 * c + t + 1)
                dve.tensor_tensor(s_lo[:, t // DK, t % DK, :].rearrange("p (b n) -> p b n", n=NT),
                                  stage[:, t % 4, :].rearrange("p (n b) -> p b n", n=NT),
                                  s_hi[:, t // DK, t % DK, :].bitcast(F32).rearrange("p (b n) -> p b n", n=NT),
                                  ALU.subtract).then_inc(split_done, 1)

            def evacuate(c, mt):
                dve.wait_ge(gemm_ready, 24 * c + 4 * mt + 1)
                dve.wait_ge(scores_done, 4 * c + mt + 1)
                slot = mt % 2
                for h in range(2):
                    rows = slice(h * HD, (h + 1) * HD)
                    dve.tensor_scalar(q1[0:HD, slot, h, :], ps[rows, QR, :], qk_bias[rows, QR, mt:mt + 1],
                                      None, ALU.add)
                for h in range(2):
                    rows = slice(h * HD, (h + 1) * HD)
                    last = dve.tensor_scalar(q2[HD:P, slot, h, :], ps[rows, QR, :], qk_bias[rows, QR, mt:mt + 1],
                                             -1.0, ALU.add, ALU.mult)
                last.then_inc(even_free, 1)
                dve.wait_ge(gemm_ready, 24 * c + 4 * mt + 3)
                for h in range(2):
                    rows = slice(h * HD, (h + 1) * HD)
                    last = dve.tensor_scalar(kk[0:HD, slot, h, :], ps[rows, KR, :], qk_bias[rows, KR, mt:mt + 1],
                                             None, ALU.add)
                last.then_inc(even_free, 1)

            def extract(c, mt):
                dve.wait_ge(score_free, 4 * c + mt + 1)
                dve.tensor_tensor(sq_r[:, :, :], sq_r[:, :, :], sq_i[:, :, :], ALU.add).then_inc(chain, 1)
                dve.wait_ge(chain, 11 * c + 2 * mt + 1)
                dve.tensor_tensor(sq_r[:, :, :], sq_r[:, :, :],
                                  mask[:, :, :].rearrange("p b n -> p (b n)").unsqueeze(1).broadcast_to(
                                      [P, 2 * BLK, P]), ALU.mult).then_inc(chain, 1)
                dve.wait_ge(chain, 11 * c + 2 * mt + 2)
                if mt == 0:
                    dve.wait_ge(wide_ready, BLK * c + 1)
                dve.tensor_reduce(prob[:, 2 * mt:2 * mt + 2, :, :].rearrange("p h k n -> p (h k) n"),
                                  sq_r[:, :, :].rearrange("p x (b n) -> p x n b", n=NT),
                                  AX_X, ALU.add).then_inc(extracted, 1)

            def evacuate_v(c, blk):
                dve.wait_ge(gemm_ready, 24 * c + 16 + 2 * blk + 1)
                dve.tensor_copy(val[:, blk, :, 0, :],
                                ps[:, (2 * blk) % 4, :].rearrange("p (h d) -> p h d", h=H)).then_inc(even_free, 1)

            def chunk(c, last_chunk):
                flat = prob[:, :, :, :].rearrange("p h k n -> p (h k) n")
                wide_peak = peak[:, :].unsqueeze(2).broadcast_to([P, H * BLK, NT])
                wide_total = total[:, :].unsqueeze(2).broadcast_to([P, H * BLK, NT])
                evacuate(c, 0)
                for mt in range(1, 4):
                    evacuate(c, mt)
                    extract(c, mt - 1)
                dve.wait_ge(mixed, BLK * c + 1)
                evacuate_v(c, 0)
                extract(c, 3)
                dve.wait_ge(extracted, 4 * c + 5)
                dve.tensor_scalar(flat, flat, EPS, None, ALU.add).then_inc(shifted, 1)
                evacuate_v(c, 1)
                dve.wait_ge(root_done, c + 1)
                dve.tensor_reduce(peak[:, :], flat, AX_X, ALU.max).then_inc(chain, 1)
                dve.wait_ge(chain, 11 * c + 9)
                dve.tensor_tensor(flat, flat, wide_peak, ALU.subtract).then_inc(shifted, 1)
                evacuate_v(c, 2)
                dve.wait_ge(exp_done, c + 1)
                dve.tensor_reduce(total[:, :], flat, AX_X, ALU.add).then_inc(chain, 1)
                dve.wait_ge(chain, 11 * c + 10)
                dve.reciprocal(total[:, :], total[:, :]).then_inc(chain, 1)
                dve.wait_ge(chain, 11 * c + 11)
                dve.tensor_tensor(flat, flat, wide_total, ALU.mult).then_inc(prob_ready, 1)
                evacuate_v(c, 3)
                for blk in range(BLK):
                    if not last_chunk:
                        for t in range(2 * blk, 2 * blk + 2):
                            split_s(c + 1, t)
                    dve.wait_ge(mixed, BLK * c + blk + 2)
                    dve.wait_ge(stored[blk % 2], 16 * (2 * c + blk // 2 + 1))
                    dve.tensor_tensor(out_st[:, blk % 2, :, :], ps[:, 6:8, :].rearrange("p a (h n) -> p (a h) n", n=P),
                                      v_bias[:, :].unsqueeze(2).broadcast_to([P, H, P]),
                                      ALU.add).then_inc(mixed_out, 1)

            for t in range(W_TILES):
                dve.wait_ge(hi_done, t + 1)
                dve.tensor_tensor(w_lo[:, t // DK, t % DK, :], stage[:, t % 4, :],
                                  w_hi[:, t // DK, t % DK, :].bitcast(F32), ALU.subtract).then_inc(split_done, 1)
            for t in range(8):
                split_s(0, t)
            with dve.Fori(0, CHUNKS - 1) as c:
                chunk(c, False)
            chunk(CHUNKS - 1, True)

        @block.tensor
        def _(pe):
            pe.sem_inc(scores_done, 2)
            pe.sem_inc(turned, 1)
            pe.sem_inc(mixed, 1)

            def bank_wait(c, i):
                pe.wait_ge(odd_free if i % 2 else even_free, 12 * c + i // 2 + 1)

            def project(c, mt):
                for j in (QR, QI, KR, KI):
                    bank_wait(c, 4 * mt + j)
                    e = j % 2
                    for kt in range(DK):
                        if mt == 0:
                            pe.wait_ge(split_done, W_TILES + 8 * c + DK * e + kt + 1)
                        hi = w_hi[:, j, kt, mt * P:(mt + 1) * P]
                        lo = w_lo[:, j, kt, mt * P:(mt + 1) * P]
                        pe.matmul(ps[:, j, :], hi, s_hi[:, e, kt, :], start=kt == 0, stop=False)
                        pe.matmul(ps[:, j, :], hi, s_lo[:, e, kt, :], start=False, stop=False)
                        last = pe.matmul(ps[:, j, :], lo, s_hi[:, e, kt, :], start=False, stop=kt == DK - 1)
                    last.then_inc(gemm_ready, 1)

            def values(c, blk):
                for e in range(2):
                    i = 2 * blk + e
                    bank_wait(c, 16 + i)
                    cols = slice(blk * P, (blk + 1) * P)
                    for kt in range(DK):
                        hi, lo = s_hi[:, e, kt, cols], s_lo[:, e, kt, cols]
                        pe.matmul(ps[:, i % 4, :], hi, w_hi[:, VR + e, kt, :], start=kt == 0, stop=False)
                        pe.matmul(ps[:, i % 4, :], hi, w_lo[:, VR + e, kt, :], start=False, stop=False)
                        last = pe.matmul(ps[:, i % 4, :], lo, w_hi[:, VR + e, kt, :], start=False,
                                         stop=kt == DK - 1)
                    last.then_inc(gemm_ready, 1)

            def scores(c, mt):
                pe.wait_ge(even_free, 12 * c + 2 * mt + 4)
                pe.wait_ge(odd_free, 12 * c + 2 * mt + 4)
                if mt == 0:
                    pe.wait_ge(turned_out, BLK * c + 1)
                    pe.wait_ge(mixed_out, BLK * c + 1)
                else:
                    pe.wait_ge(score_free, 4 * c + mt)
                slot = mt % 2
                for h in range(2):
                    for blk in range(BLK):
                        cols = slice(blk * P, (blk + 1) * P)
                        pe.matmul(ps[:, 4 + h, cols], q1[:, slot, h, cols], kk[:, slot, h, cols],
                                  start=True, stop=True)
                        last = pe.matmul(ps[:, 6 + h, cols], q2[:, slot, h, cols], kk[:, slot, h, cols],
                                         start=True, stop=True)
                last.then_inc(scores_done, 1)

            def turn(c, blk):
                pe.wait_ge(wide_ready, BLK * c + blk + 2)
                if blk == 0:
                    pe.wait_ge(score_free, 4 * c + 4)
                else:
                    pe.wait_ge(turned_out, BLK * c + blk + 1)
                for h in range(H):
                    last = pe.transpose(ps[:, 4 + h // 4, (h % 4) * P:(h % 4 + 1) * P], wide[:, h, :],
                                        keep["ident"][:, :])
                last.then_inc(turned, 1)

            def mix(c, blk):
                pe.wait_ge(turned_out, BLK * c + blk + 2)
                if blk == 0:
                    pe.wait_ge(even_free, 12 * c + 14)
                    pe.wait_ge(odd_free, 12 * c + 14)
                else:
                    pe.wait_ge(mixed_out, BLK * c + blk + 1)
                for h in range(H):
                    last = pe.matmul(ps[:, 6 + h // 4, (h % 4) * P:(h % 4 + 1) * P],
                                     val[:, blk, h, :, :].rearrange("p r d -> p (r d)"), wide_t[:, h, :],
                                     start=True, stop=True)
                last.then_inc(mixed, 1)

            with pe.Fori(0, CHUNKS) as c:
                project(c, 0)
                for mt in range(1, 4):
                    project(c, mt)
                    scores(c, mt - 1)
                values(c, 0)
                scores(c, 3)
                for blk in range(1, BLK):
                    values(c, blk)
                turn(c, 0)
                for blk in range(1, BLK):
                    turn(c, blk)
                    mix(c, blk - 1)
                mix(c, BLK - 1)


def out_proj(nc, io, scratch, keep):
    STEPS = 2 * CHUNKS
    with ExitStack() as ctx:
        m = Mem(nc, ctx, "out_")
        stage = m.sb("stage", [P, 2, DK, TOK])
        w_hi = m.sb("w_hi", [P, 2, DK, D], F32R)
        w_lo = m.sb("w_lo", [P, 2, DK, D], F32R)
        x_hi = m.sb("x_hi", [P, 2, DK, TOK], F32R)
        x_lo = m.sb("x_lo", [P, 2, DK, TOK], F32R)
        out_st = m.sb("out_st", [P, 2, NT, DK, CB])
        bias = m.sb("bias", [P, 2, DK])
        ps = m.psum("ps", [P, 8, BANK])
        bias_in = m.sem("bias_in")
        tile_in = [m.sem(f"tile_in{i}") for i in range(2)]
        hi_done = m.sem("hi_done")
        split_done = m.sem("split_done")
        ready = m.sem("ready")
        free = m.sem("free")
        stored = [m.sem(f"stored{i}") for i in range(2)]
        block = ctx.enter_context(nc.Block())
        src, dst = scratch["mixed"], scratch["attn"]

        @block.sync
        def _(sp):
            sp.dma_start(bias[:, :, :], io["b_o"]).then_inc(bias_in, 16)
            for r in range(2):
                sp.dma_start(stage[:, r, :, :], io["w_o"][r]).then_inc(tile_in[r], 16)

            def load(c):
                for r in range(2):
                    sp.wait_ge(split_done, 2 * c + r + 1)
                    for odd in range(2):
                        for blk in range(NT):
                            sp.dma_start(stage[odd * HD:(odd + 1) * HD, r, :, blk * P:(blk + 1) * P],
                                         src[c, blk, r * HD:(r + 1) * HD, odd::2, :]).then_inc(tile_in[r], 16)

            def store(c):
                for r in range(2):
                    sp.wait_ge(free, 8 * c + 4 * r + 12)
                    sp.dma_start(dst[c, r].rearrange("n p x -> p n x"),
                                 out_st[:, r, :, :, :].rearrange("p n k b -> p n (k b)")).then_inc(stored[r], 16)

            sp.sem_inc(stored[0], 16)
            sp.sem_inc(stored[1], 16)
            load(0)
            with sp.Fori(0, CHUNKS - 1) as c:
                load(c + 1)
                store(c)
            store(CHUNKS - 1)
            for r in range(2):
                sp.wait_ge(stored[r], 16 * (CHUNKS + 1))

        @block.scalar
        def _(act):
            act.sem_inc(free, 8)
            act.wait_ge(bias_in, 16)
            for r in range(2):
                act.wait_ge(tile_in[r], 16)
                act.activation(w_hi[:, r, :, :], stage[:, r, :, :], ACT.Identity).then_inc(hi_done, 1)

            def split_x(c, r):
                act.wait_ge(tile_in[r], 16 + 128 * (c + 1))
                act.activation(x_hi[:, r, :, :], stage[:, r, :, :], ACT.Identity).then_inc(hi_done, 1)

            def evacuate(c, r):
                act.wait_ge(stored[r], 16 * (c + 1))
                for mt in range(DK):
                    act.wait_ge(ready, 8 * c + 4 * r + mt + 1)
                    act.activation(out_st[:, r, :, mt, :],
                                   ps[:, 4 * r + mt, :].rearrange("p (b n) -> p n b", n=NT),
                                   ACT.Identity, bias=bias[:, r, mt:mt + 1]).then_inc(free, 1)

            for r in range(2):
                split_x(0, r)
            with act.Fori(0, CHUNKS - 1) as c:
                for r in range(2):
                    evacuate(c, r)
                    split_x(c + 1, r)
            for r in range(2):
                evacuate(CHUNKS - 1, r)

        @block.vector
        def _(dve):
            for r in range(2):
                dve.wait_ge(hi_done, r + 1)
                dve.tensor_tensor(w_lo[:, r, :, :], stage[:, r, :, :], w_hi[:, r, :, :].bitcast(F32),
                                  ALU.subtract).then_inc(split_done, 1)
            with dve.Fori(0, CHUNKS) as c:
                for r in range(2):
                    dve.wait_ge(hi_done, 2 * c + r + 3)
                    dve.tensor_tensor(x_lo[:, r, :, :], stage[:, r, :, :], x_hi[:, r, :, :].bitcast(F32),
                                      ALU.subtract).then_inc(split_done, 1)

        @block.tensor
        def _(pe):
            with pe.Fori(0, CHUNKS) as c:
                for r in range(2):
                    pe.wait_ge(split_done, 2 * c + r + 3)
                    for mt in range(DK):
                        pe.wait_ge(free, 8 * c + 4 * r + mt + 1)
                        for kt in range(DK):
                            hi = w_hi[:, r, kt, mt * P:(mt + 1) * P]
                            lo = w_lo[:, r, kt, mt * P:(mt + 1) * P]
                            pe.matmul(ps[:, 4 * r + mt, :], hi, x_hi[:, r, kt, :], start=kt == 0, stop=False)
                            pe.matmul(ps[:, 4 * r + mt, :], hi, x_lo[:, r, kt, :], start=False, stop=False)
                            last = pe.matmul(ps[:, 4 * r + mt, :], lo, x_hi[:, r, kt, :], start=False,
                                             stop=kt == DK - 1)
                        last.then_inc(ready, 1)


def interference(nc, io, scratch, keep):
    RE, IM, NEG = range(3)
    W_LOADS = 16
    TINY = 1e-30
    with ExitStack() as ctx:
        m = Mem(nc, ctx, "int_")
        stage = m.sb("stage", [P, 2, 2, D])
        w_hi = m.sb("w_hi", [P, NT, 2, DK, D], F32R)
        w_lo = m.sb("w_lo", [P, NT, 2, DK, D], F32R)
        a_hi = m.sb("a_hi", [P, 2, 3, D], F32R)
        a_lo = m.sb("a_lo", [P, 2, 3, D], F32R)
        unit = m.sb("unit", [P, 2, NT, D])
        mag = m.sb("mag", [P, NT, D])
        inv = m.sb("inv", [P, NT, D])
        is_zero = m.sb("is_zero", [P, NT, D], BF16)
        s_now = m.sb("s_now", [P, NT, NT])
        sums = m.sb("sums", [P, 2, D])
        sup = m.sb("sup", [P, 2, D])
        norm = m.sb("norm", [P, 1])
        ps = m.psum("ps", [P, 8, BANK])
        zero_sum, tmp, dots = inv[:, 0, :], inv[:, 1, :], [inv[:, 2, :], inv[:, 3, :]]

        tile_in = [m.sem(f"tile_in{i}") for i in range(2)]
        hi_done = m.sem("hi_done")
        w_split = m.sem("w_split")
        a_split = m.sem("a_split")
        neg_done = m.sem("neg_done")
        ready = m.sem("ready")
        free = m.sem("free")
        squares = m.sem("squares")
        sq_sum = m.sem("sq_sum")
        rooted = m.sem("rooted")
        inverting = m.sem("inverting")
        units = m.sem("units")
        chain = m.sem("chain")
        dot_ready = m.sem("dot_ready")
        pool_chain = m.sem("pool_chain")
        strength_set = m.sem("strength_set")
        sup_added = m.sem("sup_added")
        sup_done = m.sem("sup_done")
        norm_sum = m.sem("norm_sum")
        norm_root = m.sem("norm_root")
        norm_inv = m.sem("norm_inv")
        sup_scaled = m.sem("sup_scaled")
        stored = m.sem("stored")
        block = ctx.enter_context(nc.Block())
        src, dst = scratch["attn"], scratch["sup"]
        strength = keep["strength"]

        @block.sync
        def _(sp):
            sp.sem_inc(stored, 16)
            for t in range(W_LOADS):
                if t >= 2:
                    sp.wait_ge(w_split, t - 1)
                sp.dma_start(stage[:, t % 2, :, :], io["w_int"][t]).then_inc(tile_in[t % 2], 16)

            def load(c, n):
                sp.dma_start(stage[:, n % 2, :, :], src[c, :, n].rearrange("r p x -> p r x")
                             ).then_inc(tile_in[n % 2], 16)

            def store(c):
                sp.wait_ge(sup_scaled, c + 1)
                sp.dma_start(dst[c], sup[:, :, :]).then_inc(stored, 16)

            sp.wait_ge(w_split, W_LOADS - 1)
            load(0, 0)
            sp.wait_ge(w_split, W_LOADS)
            load(0, 1)
            for n in range(2, NT):
                sp.wait_ge(neg_done, n - 1)
                load(0, n)

            def chunk(s, loads):
                for c, n in loads:
                    sp.wait_ge(neg_done, NT * c + n - 1)
                    load(c, n)
                store(s)

            load_ahead = lambda s: [(s + 1, 2), (s + 1, 3), (s + 2, 0), (s + 2, 1)]
            for n in range(2):
                sp.wait_ge(neg_done, NT + n - 1)
                load(1, n)
            with sp.Fori(0, CHUNKS - 2) as s:
                chunk(s, load_ahead(s))
            chunk(CHUNKS - 2, load_ahead(CHUNKS - 2)[:2])
            chunk(CHUNKS - 1, [])
            sp.wait_ge(stored, 16 * (CHUNKS + 1))

        @block.gpsimd
        def _(pool):
            pool.sem_inc(pool_chain, 20)
            pool.sem_inc(sup_done, 1)

            def split_attn(c, n):
                pool.wait_ge(hi_done, W_LOADS + NT * c + n + 1)
                nc.gpsimd.tensor_tensor(a_lo[:, n % 2, 0:2, :], stage[:, n % 2, :, :],
                                        a_hi[:, n % 2, 0:2, :].bitcast(F32), ALU.subtract).then_inc(a_split, 1)

            def add_squares(c, n):
                pool.wait_ge(squares, NT * c + n + 1)
                nc.gpsimd.tensor_tensor(mag[:, n, :], mag[:, n, :], inv[:, n, :], ALU.add).then_inc(sq_sum, 1)

            def superpose(c, j):
                count = 0

                def link(ins):
                    nonlocal count
                    count += 1
                    ins.then_inc(pool_chain, 1)
                    pool.wait_ge(pool_chain, 20 + 10 * NT * c + 10 * j + count)

                pool.wait_ge(units, 2 * NT * c + 2 * NT)
                for i in range(NT):
                    z = tmp if i else zero_sum
                    link(nc.gpsimd.tensor_tensor(z, is_zero[:, i, :], s_now[:, i, j:j + 1].broadcast_to([P, D]),
                                                 ALU.mult))
                    if i:
                        link(nc.gpsimd.tensor_tensor(zero_sum, zero_sum, tmp, ALU.add))
                dot = dots[j % 2]
                pool.wait_ge(dot_ready, NT * c + j + 1)
                link(nc.gpsimd.tensor_tensor(dot, dot, zero_sum, ALU.add))
                link(nc.gpsimd.tensor_tensor(dot, dot, mag[:, j, :], ALU.mult))
                if j == 0:
                    pool.wait_ge(stored, 16 * c + 16)
                    nc.gpsimd.tensor_tensor(sup[:, 0, :], dot, unit[:, 0, j, :], ALU.mult)
                    link(nc.gpsimd.tensor_tensor(sup[:, 1, :], dot, unit[:, 1, j, :], ALU.mult))
                else:
                    nc.gpsimd.tensor_tensor(zero_sum, dot, unit[:, 0, j, :], ALU.mult)
                    link(nc.gpsimd.tensor_tensor(tmp, dot, unit[:, 1, j, :], ALU.mult))
                    nc.gpsimd.tensor_tensor(sup[:, 0, :], sup[:, 0, :], zero_sum, ALU.add)
                    last = nc.gpsimd.tensor_tensor(sup[:, 1, :], sup[:, 1, :], tmp, ALU.add)
                    last.then_inc(sup_done if j == NT - 1 else sup_added, 1)
                    if j < NT - 1:
                        pool.wait_ge(sup_added, 2 * c + j)

            def chunk(s, splits):
                for n in range(NT):
                    add_squares(s, n)
                for j in range(NT):
                    superpose(s, j)
                    if j < len(splits):
                        split_attn(*splits[j])

            for n in range(NT + 2):
                split_attn(n // NT, n % NT)
            split_ahead = lambda s: [(s + 1, 2), (s + 1, 3), (s + 2, 0), (s + 2, 1)]
            with pool.Fori(0, CHUNKS - 2) as s:
                chunk(s, split_ahead(s))
            chunk(CHUNKS - 2, split_ahead(CHUNKS - 2)[:2])
            chunk(CHUNKS - 1, [])

        @block.scalar
        def _(act):
            act.sem_inc(free, NT)

            def split_attn(c, n):
                act.wait_ge(tile_in[n % 2], 16 * (W_LOADS // 2 + 2 * c + n // 2 + 1))
                if not isinstance(c, int) or NT * c + n >= 2:
                    act.wait_ge(ready, NT * c + n - 1)
                act.activation(a_hi[:, n % 2, 0:2, :], stage[:, n % 2, :, :], ACT.Identity).then_inc(hi_done, 1)
                act.activation(a_hi[:, n % 2, NEG, :], stage[:, n % 2, IM, :], ACT.Identity, scale=-1.0)
                act.wait_ge(a_split, NT * c + n + 1)
                act.activation(a_lo[:, n % 2, NEG, :], a_lo[:, n % 2, IM, :].bitcast(F32), ACT.Identity,
                               scale=-1.0).then_inc(neg_done, 1)

            def root(c, n):
                act.wait_ge(sq_sum, NT * c + n + 1)
                act.activation(mag[:, n, :], mag[:, n, :], ACT.Sqrt).then_inc(rooted, 1)

            def chunk(s, splits):
                for n in range(NT):
                    act.wait_ge(ready, NT * s + n + 1)
                    act.wait_ge(sup_done, s + 1)
                    act.activation(mag[:, n, :], ps[:, 2 * n, :], ACT.Square)
                    act.activation(inv[:, n, :], ps[:, 2 * n + 1, :], ACT.Square).then_inc(squares, 1)
                    act.activation(unit[:, 0, n, :], ps[:, 2 * n, :], ACT.Copy)
                    act.activation(unit[:, 1, n, :], ps[:, 2 * n + 1, :], ACT.Copy).then_inc(free, 1)
                    if n:
                        root(s, n - 1)
                root(s, NT - 1)
                for c, n in splits:
                    split_attn(c, n)
                act.wait_ge(norm_sum, s + 1)
                act.activation(norm[:, :], norm[:, :], ACT.Sqrt).then_inc(norm_root, 1)

            for t in range(W_LOADS):
                act.wait_ge(tile_in[t % 2], 16 * (t // 2 + 1))
                act.activation(w_hi[:, t // 4, t // 2 % 2, 2 * (t % 2):2 * (t % 2) + 2, :], stage[:, t % 2, :, :],
                               ACT.Identity).then_inc(hi_done, 1)
            for n in range(NT + 2):
                split_attn(n // NT, n % NT)
            split_ahead = lambda s: [(s + 1, 2), (s + 1, 3), (s + 2, 0), (s + 2, 1)]
            with act.Fori(0, CHUNKS - 2) as s:
                chunk(s, split_ahead(s))
            chunk(CHUNKS - 2, split_ahead(CHUNKS - 2)[:2])
            chunk(CHUNKS - 1, [])

        @block.vector
        def _(dve):
            for t in range(W_LOADS):
                dve.wait_ge(hi_done, t + 1)
                part = (slice(None), t // 4, t // 2 % 2, slice(2 * (t % 2), 2 * (t % 2) + 2), slice(None))
                dve.tensor_tensor(w_lo[part], stage[:, t % 2, :, :], w_hi[part].bitcast(F32),
                                  ALU.subtract).then_inc(w_split, 1)

            with dve.Fori(0, CHUNKS) as c:
                dve.wait_ge(sup_done, c + 1)
                dve.tensor_scalar(s_now[:, :, :].rearrange("p i j -> p (i j)"),
                                  strength[:, bass.ds(c * NT * NT, NT * NT)], 1.0, None, ALU.mult
                                  ).then_inc(strength_set, 1)
                for n in range(NT):
                    dve.wait_ge(rooted, NT * c + n + 1)
                    dve.tensor_scalar(is_zero[:, n, :], mag[:, n, :], 0.0, None, ALU.is_equal)
                    dve.tensor_scalar(inv[:, n, :], mag[:, n, :], TINY, None, ALU.max).then_inc(inverting, 1)
                    dve.wait_ge(inverting, 2 * NT * c + 2 * n + 1)
                    dve.reciprocal(inv[:, n, :], inv[:, n, :]).then_inc(inverting, 1)
                    dve.wait_ge(inverting, 2 * NT * c + 2 * n + 2)
                    dve.wait_ge(free, NT * c + n + NT + 1)
                    for part in range(2):
                        dve.tensor_tensor(unit[:, part, n, :], unit[:, part, n, :], inv[:, n, :],
                                          ALU.mult).then_inc(units, 1)
                dve.wait_ge(units, 2 * NT * c + 2 * NT)
                dve.wait_ge(strength_set, c + 1)
                for j in range(NT):
                    base = 10 * NT * c + 10 * j
                    for i in range(NT):
                        for part in range(2):
                            if i:
                                dve.wait_ge(chain, base + 2 * i + part - 1)
                                dve.scalar_tensor_tensor(out=sums[:, part, :], in0=unit[:, part, i, :],
                                                         scalar=s_now[:, i, j:j + 1], in1=sums[:, part, :],
                                                         op0=ALU.mult, op1=ALU.add).then_inc(chain, 1)
                            else:
                                dve.tensor_scalar(sums[:, part, :], unit[:, part, i, :], s_now[:, i, j:j + 1],
                                                  None, ALU.mult).then_inc(chain, 1)
                    for part in range(2):
                        dve.wait_ge(chain, base + 7 + part)
                        dve.tensor_tensor(sums[:, part, :], sums[:, part, :], unit[:, part, j, :],
                                          ALU.mult).then_inc(chain, 1)
                    dve.wait_ge(chain, base + 10)
                    dve.wait_ge(pool_chain, base + 10)
                    dve.tensor_tensor(dots[j % 2], sums[:, 0, :], sums[:, 1, :], ALU.add).then_inc(dot_ready, 1)
                    if j < NT - 1:
                        dve.wait_ge(dot_ready, NT * c + j + 1)
                dve.wait_ge(sup_done, c + 2)
                dve.tensor_tensor_reduce(out=sums[:, :, :], in0=sup[:, :, :], in1=sup[:, :, :], scale=1.0,
                                         scalar=EPS, op0=ALU.mult, op1=ALU.add,
                                         accum_out=norm[:, :]).then_inc(norm_sum, 1)
                dve.wait_ge(norm_root, c + 1)
                dve.reciprocal(norm[:, :], norm[:, :]).then_inc(norm_inv, 1)
                dve.wait_ge(norm_inv, c + 1)
                dve.tensor_scalar(sup[:, :, :], sup[:, :, :], norm[:, 0:1], None, ALU.mult).then_inc(sup_scaled, 1)

        @block.tensor
        def _(pe):
            pe.wait_ge(w_split, W_LOADS)
            with pe.Fori(0, CHUNKS) as c:
                for n in range(NT):
                    pe.wait_ge(neg_done, NT * c + n + 1)
                    pe.wait_ge(free, NT * c + n + 1)
                    R, I = ps[:, 2 * n, :], ps[:, 2 * n + 1, :]
                    for kt in range(DK):
                        cols = slice(kt * CB, (kt + 1) * CB)
                        for out, comp, w in ((R, RE, 0), (I, RE, 1), (I, IM, 0), (R, NEG, 1)):
                            first = kt == 0 and comp == RE
                            end = kt == DK - 1 and comp in (IM, NEG)
                            hi, lo = a_hi[:, n % 2, comp, cols], a_lo[:, n % 2, comp, cols]
                            pe.matmul(out, hi, w_hi[:, n, w, kt, :], start=first, stop=False)
                            pe.matmul(out, hi, w_lo[:, n, w, kt, :], start=False, stop=False)
                            last = pe.matmul(out, lo, w_hi[:, n, w, kt, :], start=False, stop=end)
                    last.then_inc(ready, 1)


def head(nc, io, scratch, keep):
    HALF = B // 2
    HC = HALF // CB
    RE, IM, NEG = range(3)
    MEAS, POST, TOP1, TOP2, W_TILES = 0, 8, 12, 16, 18
    with ExitStack() as ctx:
        m = Mem(nc, ctx, "head_")
        w_stage = m.sb("w_stage", [P, 6, D])
        w_hi = m.sb("w_hi", [P, W_TILES, D], F32R)
        w_lo = m.sb("w_lo", [P, W_TILES, D], F32R)
        sup = m.sb("sup", [P, HC, 2, D])
        top_x = m.sb("top_x", [P, DK, HALF])
        x_hi = m.sb("x_hi", [P, 3, DK, HALF], F32R)
        x_lo = m.sb("x_lo", [P, 3, DK, HALF], F32R)
        act_a = m.sb("act_a", [P, DK, HALF])
        act_b = m.sb("act_b", [P, DK, HALF])
        stat = m.sb("stat", [P, 4, HALF])
        h2 = m.sb("h2", [P, 2, HALF])
        y, y2 = m.sb("y", [1, HALF]), m.sb("y2", [1, HALF])
        bias = m.sb("bias", [P, 5, DK])
        mean_w = m.sb("mean_w", [P, P])
        ps = m.psum("ps", [P, 8, BANK])

        bias_in = m.sem("bias_in")
        w_in = [m.sem(f"w_in{i}") for i in range(3)]
        w_hi_done = m.sem("w_hi_done")
        w_split = m.sem("w_split")
        sup_in = m.sem("sup_in")
        top_x_in = m.sem("top_x_in")
        mean_set = m.sem("mean_set")
        supT = m.sem("supT")
        x_hi_done = m.sem("x_hi_done")
        x_split = m.sem("x_split")
        x_neg = m.sem("x_neg")
        measured = m.sem("measured")
        meas_sq = m.sem("meas_sq")
        amp_sq = m.sem("amp_sq")
        amp = m.sem("amp")
        posted = m.sem("posted")
        post_out = m.sem("post_out")
        col_sum = m.sem("col_sum")
        col_mean = m.sem("col_mean")
        var = m.sem("var")
        std = m.sem("std")
        normed = m.sem("normed")
        gelu = m.sem("gelu")
        top1 = m.sem("top1")
        top1_sum = m.sem("top1_sum")
        top1_out = m.sem("top1_out")
        top2 = m.sem("top2")
        top2_out = m.sem("top2_out")
        top3 = m.sem("top3")
        top3_out = m.sem("top3_out")
        stored = m.sem("stored")
        block = ctx.enter_context(nc.Block())
        src, top_part, out = scratch["sup"], scratch["pre"], io["out"]

        @block.sync
        def _(sp):
            sp.dma_start(bias[:, :, :], io["b_head"]).then_inc(bias_in, 16)
            for hb in range(2):
                if hb:
                    sp.wait_ge(supT, 2)
                for c in range(HC):
                    sp.dma_start(sup[:, c, :, :], src[hb * HC + c]).then_inc(sup_in, 16)
                if hb == 0:
                    for t in range(W_TILES // 2):
                        if t >= 3:
                            sp.wait_ge(w_split, t - 2)
                        s = 2 * (t % 3)
                        sp.dma_start(w_stage[:, s:s + 2, :], io["w_head"][t]).then_inc(w_in[t % 3], 16)
                if hb:
                    sp.wait_ge(top1_sum, 1)
                sp.dma_start(top_x[:, :, :], top_part[8, :, :, hb * HALF:(hb + 1) * HALF].rearrange("k p b -> p k b")
                             ).then_inc(top_x_in, 16)
            for hb in range(2):
                sp.wait_ge(top3_out, hb + 1)
                sp.dma_start(out[hb], y[0:1, :] if hb == 0 else y2[0:1, :]).then_inc(stored, 16)
            sp.wait_ge(stored, 32)

        @block.gpsimd
        def _(pool):
            nc.gpsimd.memset(mean_w[:, :], 1.0 / D).then_inc(mean_set, 1)

        flat = lambda t: t.rearrange("p k n -> p (k n)")

        @block.scalar
        def _(act):
            def split_w(t):
                act.wait_ge(w_in[t % 3], 16 * (t // 3 + 1))
                s = 2 * (t % 3)
                act.activation(w_hi[:, 2 * t:2 * t + 2, :], w_stage[:, s:s + 2, :], ACT.Identity).then_inc(w_hi_done, 1)

            for t in range(4):
                split_w(t)
            act.wait_ge(bias_in, 16)
            for hb in range(2):
                if hb:
                    act.wait_ge(top2, 2)
                for part in range(2):
                    act.wait_ge(supT, 2 * hb + part + 1)
                    act.activation(x_hi[:, part, :, :], ps[:, 4 * part:4 * part + 4, :],
                                   ACT.Identity).then_inc(x_hi_done, 1)
                act.wait_ge(x_hi_done, 6 * hb + 2)
                act.activation(x_hi[:, NEG, :, :], x_hi[:, IM, :, :].bitcast(F32), ACT.Identity,
                               scale=-1.0).then_inc(x_hi_done, 1)
                act.wait_ge(x_split, 5 * hb + 2)
                act.activation(x_lo[:, NEG, :, :], x_lo[:, IM, :, :].bitcast(F32), ACT.Identity,
                               scale=-1.0).then_inc(x_neg, 1)
                if hb == 0:
                    for t in range(4, W_TILES // 2):
                        split_w(t)
                act.wait_ge(measured, 8 * hb + 4)
                act.activation(act_a[:, :, :], ps[:, 0:4, :], ACT.Square).then_inc(meas_sq, 1)
                act.wait_ge(measured, 8 * hb + 8)
                act.activation(act_b[:, :, :], ps[:, 4:8, :], ACT.Square).then_inc(meas_sq, 1)
                act.wait_ge(amp_sq, hb + 1)
                act.activation(act_a[:, :, :], act_a[:, :, :], ACT.Sqrt).then_inc(amp, 1)
                act.wait_ge(amp, hb + 1)
                act.activation(x_hi[:, 0, :, :], act_a[:, :, :], ACT.Identity).then_inc(x_hi_done, 1)
                act.wait_ge(x_split, 5 * hb + 3)
                for mt in range(DK):
                    act.wait_ge(posted, 4 * hb + mt + 1)
                    last = act.activation(act_a[:, mt, :], ps[:, mt, :], ACT.Identity, bias=bias[:, 0, mt:mt + 1])
                last.then_inc(post_out, 1)
                act.wait_ge(post_out, 2 * hb + 1)
                act.activation(act_b[:, :, :], act_a[:, :, :], ACT.Square).then_inc(post_out, 1)
                act.wait_ge(var, 4 * hb + 4)
                act.activation(stat[:, 1, :], stat[:, 1, :], ACT.Sqrt).then_inc(std, 1)
                act.wait_ge(normed, 3 * hb + 3)
                for mt in range(DK):
                    last = act.activation(act_a[:, mt, :], act_a[:, mt, :], ACT.Gelu, scale=bias[:, 1, mt:mt + 1],
                                          bias=bias[:, 2, mt:mt + 1])
                last.then_inc(gelu, 1)
                act.wait_ge(gelu, hb + 1)
                act.activation(x_hi[:, 1, :, :], act_a[:, :, :], ACT.Identity).then_inc(x_hi_done, 1)
                act.wait_ge(top1_sum, hb + 1)
                act.activation(act_b[:, :, :], act_b[:, :, :], ACT.Relu).then_inc(top1_out, 1)
                act.wait_ge(top1_out, hb + 1)
                act.activation(x_hi[:, 2, :, :], act_b[:, :, :], ACT.Identity).then_inc(x_hi_done, 1)
                for mt in range(2):
                    act.wait_ge(top2, 2 * hb + mt + 1)
                    last = act.activation(h2[:, mt, :], ps[:, 4 + mt, :], ACT.Relu, bias=bias[:, 3, mt:mt + 1])
                last.then_inc(top2_out, 1)
                act.wait_ge(top3, hb + 1)
                act.activation((y if hb == 0 else y2)[0:1, :], ps[0:1, 6, :], ACT.Copy).then_inc(top3_out, 1)

        @block.vector
        def _(dve):
            def split_w(t):
                dve.wait_ge(w_hi_done, t + 1)
                s = 2 * (t % 3)
                dve.tensor_tensor(w_lo[:, 2 * t:2 * t + 2, :], w_stage[:, s:s + 2, :],
                                  w_hi[:, 2 * t:2 * t + 2, :].bitcast(F32), ALU.subtract).then_inc(w_split, 1)

            for t in range(4):
                split_w(t)
            for hb in range(2):
                for part in range(2):
                    dve.wait_ge(x_hi_done, 6 * hb + part + 1)
                    dve.tensor_tensor(x_lo[:, part, :, :], ps[:, 4 * part:4 * part + 4, :],
                                      x_hi[:, part, :, :].bitcast(F32), ALU.subtract).then_inc(x_split, 1)
                if hb == 0:
                    for t in range(4, W_TILES // 2):
                        split_w(t)
                dve.wait_ge(meas_sq, 2 * hb + 2)
                dve.tensor_tensor(act_a[:, :, :], act_a[:, :, :], act_b[:, :, :], ALU.add).then_inc(amp_sq, 1)
                dve.wait_ge(x_hi_done, 6 * hb + 4)
                dve.tensor_tensor(x_lo[:, 0, :, :], act_a[:, :, :], x_hi[:, 0, :, :].bitcast(F32),
                                  ALU.subtract).then_inc(x_split, 1)
                for i, t in enumerate((act_a, act_b)):
                    dve.wait_ge(post_out, 2 * hb + i + 1)
                    dve.tensor_reduce(stat[:, i, :], t[:, :, :].rearrange("p k n -> p n k"), AX_X,
                                      ALU.add).then_inc(col_sum, 1)
                dve.wait_ge(col_mean, 2 * hb + 2)
                dve.tensor_copy(stat[:, 0, :], ps[:, 4, :]).then_inc(var, 1)
                dve.wait_ge(var, 4 * hb + 1)
                dve.tensor_tensor(stat[:, 2, :], stat[:, 0, :], stat[:, 0, :], ALU.mult).then_inc(var, 1)
                dve.wait_ge(var, 4 * hb + 2)
                dve.tensor_tensor(stat[:, 1, :], ps[:, 5, :], stat[:, 2, :], ALU.subtract).then_inc(var, 1)
                dve.wait_ge(var, 4 * hb + 3)
                dve.tensor_scalar(stat[:, 1, :], stat[:, 1, :], 0.0, LN_EPS, ALU.max, ALU.add).then_inc(var, 1)
                wide = lambda i: stat[:, i, :].unsqueeze(1).broadcast_to([P, DK, HALF])
                dve.tensor_tensor(act_a[:, :, :], act_a[:, :, :], wide(0), ALU.subtract).then_inc(normed, 1)
                dve.wait_ge(std, hb + 1)
                dve.reciprocal(stat[:, 3, :], stat[:, 1, :]).then_inc(normed, 1)
                dve.wait_ge(normed, 3 * hb + 2)
                dve.tensor_tensor(act_a[:, :, :], act_a[:, :, :], wide(3), ALU.mult).then_inc(normed, 1)
                dve.wait_ge(x_hi_done, 6 * hb + 5)
                dve.tensor_tensor(x_lo[:, 1, :, :], act_a[:, :, :], x_hi[:, 1, :, :].bitcast(F32),
                                  ALU.subtract).then_inc(x_split, 1)
                dve.wait_ge(top1, 4 * hb + 4)
                dve.wait_ge(top_x_in, 16 * (hb + 1))
                dve.tensor_tensor(act_b[:, :, :], ps[:, 0:4, :], top_x[:, :, :], ALU.add).then_inc(top1_sum, 1)
                dve.wait_ge(x_hi_done, 6 * hb + 6)
                dve.tensor_tensor(x_lo[:, 2, :, :], act_b[:, :, :], x_hi[:, 2, :, :].bitcast(F32),
                                  ALU.subtract).then_inc(x_split, 1)

        @block.tensor
        def _(pe):
            def product(bank, w, wcols, comp, first, end):
                for kt in range(DK):
                    hi, lo = w_hi[:, w[kt], wcols[kt]], w_lo[:, w[kt], wcols[kt]]
                    pe.matmul(ps[:, bank, :], hi, x_hi[:, comp, kt, :], start=first and kt == 0, stop=False)
                    pe.matmul(ps[:, bank, :], hi, x_lo[:, comp, kt, :], start=False, stop=False)
                    last = pe.matmul(ps[:, bank, :], lo, x_hi[:, comp, kt, :], start=False,
                                     stop=end and kt == DK - 1)
                return last

            def tiles(base, mt):
                return [base + kt for kt in range(DK)], [slice(mt * P, (mt + 1) * P)] * DK

            for hb in range(2):
                pe.wait_ge(sup_in, 16 * HC * (hb + 1))
                if hb:
                    pe.wait_ge(top3_out, 1)
                for part in range(2):
                    for kt in range(DK):
                        for c in range(HC):
                            last = pe.transpose(ps[:, 4 * part + kt, c * P:(c + 1) * P],
                                                sup[:, c, part, kt * P:(kt + 1) * P], keep["ident"][:, :])
                    last.then_inc(supT, 1)
                pe.wait_ge(w_split, 4)
                pe.wait_ge(x_split, 5 * hb + 2)
                pe.wait_ge(x_neg, hb + 1)
                for mt in range(DK):
                    product(mt, *tiles(MEAS, mt), RE, True, False)
                    product(mt, *tiles(MEAS + 4, mt), NEG, False, True).then_inc(measured, 1)
                for mt in range(DK):
                    product(4 + mt, *tiles(MEAS + 4, mt), RE, True, False)
                    product(4 + mt, *tiles(MEAS, mt), IM, False, True).then_inc(measured, 1)
                pe.wait_ge(w_split, W_TILES // 2)
                pe.wait_ge(x_split, 5 * hb + 3)
                for mt in range(DK):
                    product(mt, *tiles(POST, mt), 0, True, True).then_inc(posted, 1)
                pe.wait_ge(mean_set, 1)
                for i in range(2):
                    pe.wait_ge(col_sum, 2 * hb + i + 1)
                    pe.matmul(ps[:, 4 + i, :], mean_w[:, :], stat[:, i, :], start=True, stop=True).then_inc(col_mean, 1)
                pe.wait_ge(x_split, 5 * hb + 4)
                for mt in range(DK):
                    product(mt, *tiles(TOP1, mt), 1, True, True).then_inc(top1, 1)
                pe.wait_ge(x_split, 5 * hb + 5)
                pe.wait_ge(var, 4 * hb + 3)
                for mt in range(2):
                    w = [TOP2 + kt // 2 for kt in range(DK)]
                    cols = [slice((kt % 2) * 256 + mt * P, (kt % 2) * 256 + (mt + 1) * P) for kt in range(DK)]
                    product(4 + mt, w, cols, 2, True, True).then_inc(top2, 1)
                pe.wait_ge(top2_out, hb + 1)
                for mt in range(2):
                    last = pe.matmul(ps[0:1, 6, :], bias[:, 4, mt:mt + 1], h2[:, mt, :], start=mt == 0, stop=mt == 1)
                last.then_inc(top3, 1)


def build(nc, io):
    scratch = {
        "pre": nc.dram_tensor("pre", (17, GROUP, P, B), F32).ap(),
        "mixed": nc.dram_tensor("mixed", (CHUNKS, NT, P, H, P), F32).ap(),
        "attn": nc.dram_tensor("attn", (CHUNKS, 2, NT, P, DK * CB), F32).ap(),
        "sup": nc.dram_tensor("sup", (CHUNKS, P, 2, D), F32).ap(),
    }
    with ExitStack() as ctx:
        m = Mem(nc, ctx, "keep_")
        keep = {
            "ident": m.sb("ident", [P, P]),
            "ids": m.sb("ids", [P, CHUNKS, NT], I32),
            "strength": m.sb("strength", [P, CHUNKS * NT * NT]),
        }
        encoders(nc, io, scratch, keep)
        attention(nc, io, scratch, keep)
        out_proj(nc, io, scratch, keep)
        interference(nc, io, scratch, keep)
        head(nc, io, scratch, keep)


def kernel(**inputs):
    import numpy as np
    import concourse.bacc as bacc
    from concourse.bass_utils import run_bass_kernel_spmd as run

    v = {k.replace("L0_rec_", ""): np.asarray(a) for k, a in inputs.items()}

    def rows(w):
        return w.reshape(-1, P, w.shape[1])

    def cols(*vectors):
        return np.concatenate([x.reshape(-1, P) for x in vectors]).T

    w_enc = np.concatenate([v["er_W1"].T, v["ei_W1"].T, v["W_top1"][D:], v["er_W2"].T, v["ei_W2"].T], axis=1)
    head_w = np.concatenate([
        rows(v["meas_Mr"].T), rows(v["meas_Mi"].T), rows(v["post_W"].T), rows(v["W_top1"][:D]),
        rows(v["W_top2"]).reshape(2, 2, P, 256).transpose(0, 2, 1, 3).reshape(2, P, D)])
    int_w = np.stack([v["int_Wr"], v["int_Wi"]], axis=1).transpose(0, 1, 3, 2)
    zero = np.zeros(256, np.float32)
    arrays = {
        "xT": v["r_x"].T.reshape(KT, P, B),
        "w_enc": w_enc.reshape(KT, P, 17, D).transpose(2, 0, 1, 3),
        "b_enc": cols(v["er_b1"], v["ei_b1"], v["b_top1"], v["er_b2"], v["ei_b2"]),
        "ln_g": cols(v["er_g1"], v["ei_g1"]),
        "ln_b": cols(v["er_be1"], v["ei_be1"]),
        "ids": v["ids"].reshape(CHUNKS, P, NT).transpose(1, 0, 2),
        "tbl_0": v["tbl_0"], "tbl_1": v["tbl_1"], "tbl_2": v["tbl_2"], "tbl_3": v["tbl_3"],
        "w_qkv": np.concatenate([rows(v[w].T) for w in ("Wq_r", "Wq_i", "Wk_r", "Wk_i", "Wv_r", "Wv_i")]),
        "b_qk": cols(v["bq_r"], v["bq_i"], v["bk_r"], v["bk_i"]).reshape(P, 4, DK),
        "b_v": np.stack([v["bv_r"].reshape(H, HD), v["bv_i"].reshape(H, HD)]).transpose(0, 2, 1).reshape(P, H),
        "w_o": np.stack([v["Wo_r"].T, v["Wo_i"].T]).reshape(2, DK, P, D).transpose(0, 2, 1, 3),
        "b_o": cols(v["bo_r"], v["bo_i"]).reshape(P, 2, DK),
        "w_int": int_w.reshape(16, 2, P, D).transpose(0, 2, 1, 3),
        "w_head": head_w.reshape(9, 2, P, D).transpose(0, 2, 1, 3),
        "b_head": cols(v["post_b"], v["post_g"], v["post_be"], v["b_top2"], zero, v["W_top3"][:, 0], zero
                       ).reshape(P, 5, DK),
    }
    arrays = {name: np.ascontiguousarray(a) for name, a in arrays.items()}
    nc = bacc.Bacc("TRN2", target_bir_lowering=False, num_devices=1)
    io = {name: nc.dram_tensor(name, a.shape, mybir.dt.from_np(a.dtype), kind="ExternalInput").ap()
          for name, a in arrays.items()}
    y = nc.dram_tensor("y", (2, 1, B // 2), F32, kind="ExternalOutput").ap()
    io["out"] = y
    build(nc, io)
    result = run(nc, [arrays], core_ids=[0])
    return result.results[0]["y"].reshape(B, 1)
```

```python
from contextlib import ExitStack

import concourse.bass as bass
from concourse import mybir

F32 = mybir.dt.float32
F32R = mybir.dt.float32r
BF16 = mybir.dt.bfloat16
I32 = mybir.dt.int32
U32 = mybir.dt.uint32
ACT = mybir.ActivationFunctionType
ALU = mybir.AluOpType
AX_X = mybir.AxisListType.X

P = 128
B = 1024
IN = 2048
D = 512
NT = 4
H = 8
HD = D // H
BANK = 512
KT = IN // P
DK = D // P
GROUP = 4
CB = 128
CHUNKS = B // CB
TOK = CB * NT
LN_EPS = 1e-5
EPS = 1e-8


class Mem:

    def __init__(self, nc, ctx, prefix):
        self.nc, self.ctx, self.prefix = nc, ctx, prefix

    def sb(self, name, shape, dt=F32):
        return self.ctx.enter_context(self.nc.sbuf_tensor(self.prefix + name, shape, dt))

    def psum(self, name, shape):
        return self.ctx.enter_context(self.nc.psum_tensor(self.prefix + name, shape, F32))

    def sem(self, name):
        return self.ctx.enter_context(self.nc.semaphore(self.prefix + name))


def encoders(nc, io, scratch, keep):
    W1_GROUPS, TOP, GROUPS = 8, 8, 17
    RING = 4
    HALF = B // 2
    with ExitStack() as ctx:
        m = Mem(nc, ctx, "enc_")
        src_hi = m.sb("src_hi", [P, KT, B], F32R)
        src_lo = m.sb("src_lo", [P, KT, B], F32R)
        src_stage = m.sb("src_stage", [P, 2, B])
        w_stage = m.sb("w_stage", [P, RING, D])
        w_hi = m.sb("w_hi", [P, RING, D], F32R)
        w_lo = m.sb("w_lo", [P, RING, D], F32R)
        out_stage = m.sb("out_stage", [P, 8, BANK])
        square = m.sb("square", [P, 2, BANK])
        stats = m.sb("stats", [P, 2, 2, B])
        bias = m.sb("bias", [P, GROUPS * GROUP])
        group_bias = m.sb("group_bias", [P, GROUP])
        ln_g = m.sb("ln_g", [P, 2 * KT])
        ln_b = m.sb("ln_b", [P, 2 * KT])
        mean_w = m.sb("mean_w", [P, P])
        acc = m.psum("acc", [P, 8, BANK])

        consts_in = m.sem("consts_in")
        w_in = [m.sem(f"w_in{i}") for i in range(RING)]
        src_in = [m.sem(f"src_in{i}") for i in range(2)]
        w_hi_done = m.sem("w_hi_done")
        w_ready = m.sem("w_ready")
        w_used = m.sem("w_used")
        bank_ready = m.sem("bank_ready")
        bank_free = m.sem("bank_free")
        norm_done = m.sem("norm_done")
        src_hi_done = m.sem("src_hi_done")
        src_ready = m.sem("src_ready")
        bias_set = m.sem("bias_set")
        gelu_done = m.sem("gelu_done")
        centred = m.sem("centred")
        squared = m.sem("squared")
        summed = m.sem("summed")
        stored = m.sem("stored")
        zeroed = m.sem("zeroed")
        stats_mm = m.sem("stats_mm")
        stats_dve = m.sem("stats_dve")
        stats_std = m.sem("stats_std")
        stats_read = m.sem("stats_read")
        pool_set = m.sem("pool_set")
        ids_in = m.sem("ids_in")
        gathered = m.sem("gathered")

        block = ctx.enter_context(nc.Block())

        w_all = io["w_enc"]
        pre = scratch["pre"]
        used_before = lambda g, k: (w_used, 15 * g + k - 3) if k >= 4 else (
            (bank_ready, 8 * g) if k == 3 else (w_used, 15 * g + k - 2))

        @block.sync
        def _(sp):
            sp.dma_start(bias[:, :], io["b_enc"]).then_inc(consts_in, 16)
            sp.dma_start(ln_g[:, :], io["ln_g"]).then_inc(consts_in, 16)
            sp.dma_start(ln_b[:, :], io["ln_b"]).then_inc(consts_in, 16)

            def load(g, k):
                sp.dma_start(w_stage[:, k % RING, :], w_all[g, k]).then_inc(w_in[k % RING], 16)

            for k in range(RING):
                load(0, k)
            for k in range(RING, KT):
                sp.wait_ge(w_ready, k - RING + 1)
                load(0, k)
            with sp.Fori(1, GROUPS) as g:
                for k in range(KT):
                    sp.wait_ge(w_ready, 16 * g + k - RING + 1)
                    load(g, k)

        @block.gpsimd
        def _(pool):
            for k in range(2):
                pool.dma_start(src_stage[:, k, :], io["xT"][k]).then_inc(src_in[k], 16)
            nc.gpsimd.memset(mean_w[:, :], 1.0 / IN).then_inc(pool_set, 1)
            nc.gpsimd.memset(keep["ident"][:, :], 0.0).then_inc(pool_set, 1)
            pool.wait_ge(pool_set, 2)
            nc.gpsimd.affine_select(out=keep["ident"][:, :], in_=keep["ident"][:, :],
                                    compare_op=ALU.not_equal, fill=1.0, base=0,
                                    pattern=[[-1, P]], channel_multiplier=1).then_inc(pool_set, 1)
            for k in range(2, KT):
                pool.wait_ge(src_ready, k - 1)
                pool.dma_start(src_stage[:, k % 2, :], io["xT"][k]).then_inc(src_in[k % 2], 16)
            pool.dma_start(keep["ids"][:, :, :], io["ids"]).then_inc(ids_in, 16)
            pool.wait_ge(ids_in, 16)
            for i in range(NT):
                for c in range(CHUNKS):
                    pool.indirect_dma_start(
                        keep["strength"][:, (c * NT + i) * NT:(c * NT + i + 1) * NT], None, io[f"tbl_{i}"],
                        bass.IndirectOffsetOnAxis(ap=keep["ids"][:, c, i:i + 1], axis=0)).then_inc(gathered, 16)

            def store(g):
                for b in range(8):
                    pool.wait_ge(bank_free, 8 * g + 8 + b + 1)
                    pool.dma_start(pre[g, b // 2, :, (b % 2) * HALF:(b % 2 + 1) * HALF],
                                   out_stage[:, b, :]).then_inc(stored, 16)

            def load_h(e):
                for k in range(KT):
                    pool.wait_ge(src_ready, KT * (e + 1) + k - 1)
                    pool.dma_start(src_stage[:, k % 2, :], pre[4 * e + k // 4, k % 4]).then_inc(src_in[k % 2], 16)

            with pool.Fori(0, W1_GROUPS) as g:
                store(g)
            pool.wait_ge(stored, 16 * 8 * W1_GROUPS)
            pool.wait_ge(stats_dve, 10)
            load_h(0)
            with pool.Fori(TOP, TOP + 4) as g:
                store(g)
            load_h(1)
            with pool.Fori(TOP + 4, GROUPS) as g:
                store(g)
            pool.wait_ge(stored, 16 * 8 * GROUPS)
            pool.wait_ge(gathered, 16 * NT * CHUNKS)

        @block.scalar
        def _(act):
            act.sem_inc(bank_free, 8)
            act.wait_ge(consts_in, 48)

            def split_w(g, k):
                act.wait_ge(w_in[k % RING], 16 * (4 * g + k // RING + 1))
                act.activation(w_hi[:, k % RING, :], w_stage[:, k % RING, :],
                               ACT.Identity).then_inc(w_hi_done, 1)

            def split_w_later(g, k):
                act.wait_ge(*used_before(g, k))
                split_w(g, k)

            def split_src(s, k):
                act.activation(src_hi[:, k, :], src_stage[:, k % 2, :], ACT.Identity).then_inc(src_hi_done, 1)

            def evacuate(g, with_stats):
                act.activation(group_bias[:, :], bias[:, bass.ds(g * GROUP, GROUP)], ACT.Copy).then_inc(bias_set, 1)
                act.wait_ge(bias_set, g + 1)
                for b in range(8):
                    act.wait_ge(bank_ready, 8 * g + b + 1)
                    if with_stats:
                        if not isinstance(g, int) or b >= 2:
                            act.wait_ge(summed, 16 * g + 2 * b - 3)
                        act.activation(square[:, b % 2, :], acc[:, b, :], ACT.Square,
                                       bias=group_bias[:, b // 2:b // 2 + 1]).then_inc(squared, 1)
                    if not isinstance(g, int) or g > 0:
                        act.wait_ge(stored, 128 * g)
                    act.activation(out_stage[:, b, :], acc[:, b, :], ACT.Identity,
                                   bias=group_bias[:, b // 2:b // 2 + 1]).then_inc(bank_free, 1)

            def make_h(e, k):
                act.wait_ge(norm_done, KT * e + k + 1)
                if k < 15:
                    act.wait_ge(w_used, 15 * (8 + 4 * e) + k + 1)
                else:
                    act.wait_ge(bank_ready, 8 * (9 + 4 * e))
                act.activation(src_stage[:, k % 2, :], src_stage[:, k % 2, :], ACT.Gelu,
                               scale=ln_g[:, e * KT + k:e * KT + k + 1],
                               bias=ln_b[:, e * KT + k:e * KT + k + 1]).then_inc(gelu_done, 1)
                act.wait_ge(gelu_done, KT * e + k + 1)
                split_src(e + 1, k)

            for k in range(KT):
                act.wait_ge(src_in[k % 2], 16 * (k // 2 + 1))
                split_src(0, k)
                if k < RING:
                    split_w(0, k)
                else:
                    act.wait_ge(w_used, k - 3)
                    split_w(0, k)
            for k in range(RING):
                split_w_later(1, k)
            evacuate(0, True)
            with act.Fori(1, W1_GROUPS) as g:
                for k in range(RING, KT):
                    split_w_later(g, k)
                for k in range(RING):
                    split_w_later(g + 1, k)
                evacuate(g, True)
            act.wait_ge(summed, 16 * W1_GROUPS)
            for e in range(2):
                act.wait_ge(stats_dve, 4 * e + 4)
                act.activation(stats[:, e, 1, :], stats[:, e, 1, :], ACT.Sqrt).then_inc(stats_std, 1)
            for e in range(2):
                g = TOP + 4 * e
                for k in range(RING, KT):
                    split_w_later(g, k)
                    make_h(e, k - RING)
                for k in range(RING):
                    split_w_later(g + 1, k)
                    make_h(e, KT - RING + k)
                evacuate(g, False)
                with act.Fori(g + 1, g + 4) as g:
                    for k in range(RING, KT):
                        split_w_later(g, k)
                    for k in range(RING):
                        split_w_later(g + 1, k)
                    evacuate(g, False)
            for k in range(RING, KT):
                split_w_later(GROUPS - 1, k)
            evacuate(GROUPS - 1, False)

        @block.vector
        def _(dve):
            def split_w(g, k):
                dve.wait_ge(w_hi_done, 16 * g + k + 1)
                dve.tensor_tensor(w_lo[:, k % RING, :], w_stage[:, k % RING, :],
                                  w_hi[:, k % RING, :].bitcast(F32), ALU.subtract).then_inc(w_ready, 1)

            def split_src(s, k):
                dve.wait_ge(src_hi_done, KT * s + k + 1)
                dve.tensor_tensor(src_lo[:, k, :], src_stage[:, k % 2, :], src_hi[:, k, :].bitcast(F32),
                                  ALU.subtract).then_inc(src_ready, 1)

            def add_stats(g, e):
                for b in range(8):
                    half = slice((b % 2) * HALF, (b % 2 + 1) * HALF)
                    dve.wait_ge(squared, 8 * g + b + 1)
                    if not isinstance(g, int) or b >= 2:
                        dve.wait_ge(summed, 16 * g + 2 * b - 3)
                    dve.tensor_tensor(stats[:, e, 1, half], stats[:, e, 1, half], square[:, b % 2, :],
                                      ALU.add).then_inc(summed, 1)
                    dve.wait_ge(bank_free, 8 + 8 * g + b + 1)
                    if not isinstance(g, int) or b >= 2:
                        dve.wait_ge(summed, 16 * g + 2 * b - 2)
                    dve.tensor_tensor(stats[:, e, 0, half], stats[:, e, 0, half], out_stage[:, b, :],
                                      ALU.add).then_inc(summed, 1)

            def normalise(e, k):
                dve.wait_ge(src_in[k % 2], 16 * (8 * (e + 1) + k // 2 + 1))
                dve.tensor_tensor(src_stage[:, k % 2, :], src_stage[:, k % 2, :], stats[:, e, 0, :],
                                  ALU.subtract).then_inc(centred, 1)
                dve.wait_ge(centred, KT * e + k + 1)
                dve.tensor_tensor(src_stage[:, k % 2, :], src_stage[:, k % 2, :], stats[:, e, 1, :],
                                  ALU.mult).then_inc(norm_done, 1)

            dve.memset(stats[:, :, :, :], 0.0).then_inc(zeroed, 1)
            for k in range(KT):
                split_src(0, k)
                split_w(0, k)
            for k in range(RING):
                split_w(1, k)
            dve.wait_ge(zeroed, 1)
            add_stats(0, 0)
            for e in range(2):
                with dve.Fori(max(4 * e, 1), 4 * e + 4) as g:
                    for k in range(RING, KT):
                        split_w(g, k)
                    for k in range(RING):
                        split_w(g + 1, k)
                    add_stats(g, e)
            for e in range(2):
                both = lambda i: acc[:, 4 * e + 2 * i:4 * e + 2 * i + 2, :].rearrange("p h n -> p (h n)")
                dve.wait_ge(stats_mm, 4 * e + 4)
                dve.tensor_copy(stats[:, e, 0, :], both(0)).then_inc(stats_dve, 1)
                dve.wait_ge(stats_dve, 4 * e + 1)
                dve.tensor_tensor(src_stage[:, e, :], stats[:, e, 0, :], stats[:, e, 0, :],
                                  ALU.mult).then_inc(stats_dve, 1)
                dve.wait_ge(stats_dve, 4 * e + 2)
                dve.tensor_tensor(stats[:, e, 1, :], both(1), src_stage[:, e, :],
                                  ALU.subtract).then_inc(stats_dve, 1)
                dve.wait_ge(stats_dve, 4 * e + 3)
                dve.tensor_scalar(stats[:, e, 1, :], stats[:, e, 1, :], 0.0, LN_EPS, ALU.max,
                                  ALU.add).then_inc(stats_dve, 1)
            for e in range(2):
                dve.wait_ge(stats_std, e + 1)
                dve.reciprocal(stats[:, e, 1, :], stats[:, e, 1, :]).then_inc(stats_dve, 1)
            dve.wait_ge(stats_dve, 10)

            for e in range(2):
                g = TOP + 4 * e
                for k in range(RING, KT):
                    split_w(g, k)
                    normalise(e, k - RING)
                    split_src(e + 1, k - RING)
                for k in range(RING):
                    split_w(g + 1, k)
                    normalise(e, KT - RING + k)
                    split_src(e + 1, KT - RING + k)
                with dve.Fori(g + 1, g + 4) as g:
                    for k in range(RING, KT):
                        split_w(g, k)
                    for k in range(RING):
                        split_w(g + 1, k)
            for k in range(RING, KT):
                split_w(GROUPS - 1, k)

        @block.tensor
        def _(pe):
            def gemm(g, source):
                for k in range(KT):
                    if not isinstance(g, int):
                        pe.wait_ge(w_ready, KT * g + k + 1)
                    else:
                        pe.wait_ge(w_ready, KT * g + k + 1)
                    pe.wait_ge(src_ready, KT * source + k + 1)
                    for mt in range(GROUP):
                        hi = w_hi[:, k % RING, mt * P:(mt + 1) * P]
                        lo = w_lo[:, k % RING, mt * P:(mt + 1) * P]
                        for h in range(2):
                            if k == 0:
                                pe.wait_ge(bank_free, 8 * g + 2 * mt + h + 1)
                            cols = slice(h * HALF, (h + 1) * HALF)
                            pe.matmul(acc[:, 2 * mt + h, :], hi, src_hi[:, k, cols], start=k == 0, stop=False)
                            pe.matmul(acc[:, 2 * mt + h, :], hi, src_lo[:, k, cols], start=False, stop=False)
                        for h in range(2):
                            cols = slice(h * HALF, (h + 1) * HALF)
                            last = pe.matmul(acc[:, 2 * mt + h, :], lo, src_hi[:, k, cols],
                                             start=False, stop=k == KT - 1)
                            if k == KT - 1:
                                last.then_inc(bank_ready, 1)
                    if k < KT - 1:
                        last.then_inc(w_used, 1)

            with pe.Fori(0, W1_GROUPS) as g:
                gemm(g, 0)
            pe.wait_ge(summed, 16 * W1_GROUPS)
            pe.wait_ge(bank_free, 8 * W1_GROUPS + 8)
            pe.wait_ge(pool_set, 1)
            for e in range(2):
                for i in range(2):
                    for h in range(2):
                        pe.matmul(acc[:, 4 * e + 2 * i + h, :], mean_w[:, :],
                                  stats[:, e, i, h * HALF:(h + 1) * HALF], start=True, stop=True
                                  ).then_inc(stats_mm, 1)
            pe.wait_ge(stats_dve, 7)
            gemm(TOP, 0)
            with pe.Fori(TOP + 1, TOP + 5) as g:
                gemm(g, 1)
            with pe.Fori(TOP + 5, GROUPS) as g:
                gemm(g, 2)


def attention(nc, io, scratch, keep):
    QR, QI, KR, KI, VR, VI = range(6)
    BLK = TOK // P
    SB = P // NT
    W_TILES = 6 * DK
    with ExitStack() as ctx:
        m = Mem(nc, ctx, "att_")
        stage = m.sb("stage", [P, 4, D])
        w_hi = m.sb("w_hi", [P, 6, DK, D], F32R)
        w_lo = m.sb("w_lo", [P, 6, DK, D], F32R)
        s_hi = m.sb("s_hi", [P, 2, DK, TOK], F32R)
        s_lo = m.sb("s_lo", [P, 2, DK, TOK], F32R)
        q1 = m.sb("q1", [P, 2, 2, TOK])
        q2 = m.sb("q2", [P, 2, 2, TOK])
        kk = m.sb("kk", [P, 2, 2, TOK])
        val = m.sb("val", [P, BLK, H, 2, HD])
        sq_r = m.sb("sq_r", [P, 2 * BLK, P])
        sq_i = m.sb("sq_i", [P, 2 * BLK, P])
        mask = m.sb("mask", [P, SB, NT])
        prob = m.sb("prob", [P, H, BLK, NT])
        peak = m.sb("peak", [P, H * BLK])
        total = m.sb("total", [P, H * BLK])
        wide = m.sb("wide", [P, H, P])
        wide_t = m.sb("wide_t", [P, H, P])
        out_st = m.sb("out_st", [P, 2, H, P])
        qk_bias = m.sb("qk_bias", [P, 4, DK])
        v_bias = m.sb("v_bias", [P, H])
        ps = m.psum("ps", [P, 8, BANK])

        w_bias_in = m.sem("w_bias_in")
        tile_in = [m.sem(f"tile_in{i}") for i in range(4)]
        hi_done = m.sem("hi_done")
        split_done = m.sem("split_done")
        gemm_ready = m.sem("gemm_ready")
        even_free = m.sem("even_free")
        odd_free = m.sem("odd_free")
        scores_done = m.sem("scores_done")
        score_free = m.sem("score_free")
        extracted = m.sem("extracted")
        chain = m.sem("chain")
        root_done = m.sem("root_done")
        shifted = m.sem("shifted")
        exp_done = m.sem("exp_done")
        prob_ready = m.sem("prob_ready")
        wide_ready = m.sem("wide_ready")
        turned = m.sem("turned")
        turned_out = m.sem("turned_out")
        mixed = m.sem("mixed")
        mixed_out = m.sem("mixed_out")
        stored = [m.sem(f"stored{i}") for i in range(2)]
        mask_set = m.sem("mask_set")

        block = ctx.enter_context(nc.Block())
        s_src = scratch["pre"]
        out = scratch["mixed"]

        @block.sync
        def _(sp):
            sp.sem_inc(stored[0], 16)
            sp.sem_inc(stored[1], 16)
            sp.dma_start(qk_bias[:, :, :], io["b_qk"]).then_inc(w_bias_in, 16)
            sp.dma_start(v_bias[:, :], io["b_v"]).then_inc(w_bias_in, 16)
            for t in range(W_TILES):
                if t >= 4:
                    sp.wait_ge(split_done, t - 3)
                sp.dma_start(stage[:, t % 4, :], io["w_qkv"][t]).then_inc(tile_in[t % 4], 16)

            def load(c, tiles):
                for t in tiles:
                    e, kt = t // DK, t % DK
                    sp.wait_ge(split_done, W_TILES + 8 * c + t - 3)
                    src = s_src[9 + 4 * e:13 + 4 * e, kt, :, bass.ds(c * CB, CB)].rearrange("n p b -> p n b")
                    sp.dma_start(stage[:, t % 4, :].rearrange("p (n b) -> p n b", n=NT),
                                 src).then_inc(tile_in[t % 4], 16)

            def store(c, blk):
                sp.wait_ge(mixed_out, BLK * c + blk + 2)
                sp.dma_start(out[c, blk], out_st[:, blk % 2, :, :]).then_inc(stored[blk % 2], 16)

            load(0, range(8))
            with sp.Fori(0, CHUNKS - 1) as c:
                load(c + 1, range(0, 6))
                store(c, 0)
                load(c + 1, range(6, 8))
                for blk in range(1, BLK):
                    store(c, blk)
            for blk in range(BLK):
                store(CHUNKS - 1, blk)
            for i in range(2):
                sp.wait_ge(stored[i], 16 * (1 + CHUNKS * BLK // 2))

        @block.gpsimd
        def _(pool):
            pool.sem_inc(wide_ready, 1)
            nc.gpsimd.memset(mask[:, :, :], 1.0).then_inc(mask_set, 1)
            pool.wait_ge(mask_set, 1)
            nc.gpsimd.affine_select(out=mask[:, :, :], in_=mask[:, :, :], compare_op=ALU.is_ge, fill=0.0,
                                    base=0, pattern=[[-NT, SB], [0, NT]], channel_multiplier=1).then_inc(mask_set, 1)
            pool.wait_ge(mask_set, 2)
            nc.gpsimd.affine_select(out=mask[:, :, :], in_=mask[:, :, :], compare_op=ALU.is_ge, fill=0.0,
                                    base=NT - 1, pattern=[[NT, SB], [0, NT]], channel_multiplier=-1
                                    ).then_inc(mask_set, 1)
            pool.wait_ge(mask_set, 3)
            with pool.Fori(0, CHUNKS) as c:
                for blk in range(BLK):
                    pool.wait_ge(prob_ready, c + 1)
                    pool.wait_ge(turned, BLK * c + blk + 1)
                    nc.gpsimd.tensor_tensor(
                        wide[:, :, :].rearrange("p h (b n) -> p h b n", n=NT),
                        prob[:, :, blk, :].unsqueeze(2).broadcast_to([P, H, SB, NT]),
                        mask[:, :, :].unsqueeze(1).broadcast_to([P, H, SB, NT]), ALU.mult).then_inc(wide_ready, 1)

        @block.scalar
        def _(act):
            act.sem_inc(odd_free, 2)
            act.sem_inc(turned_out, 1)
            act.wait_ge(w_bias_in, 32)

            def split_s(c, t):
                act.wait_ge(tile_in[t % 4], 16 * (W_TILES // 4 + 2 * c + t // 4 + 1))
                act.activation(s_hi[:, t // DK, t % DK, :].rearrange("p (b n) -> p b n", n=NT),
                               stage[:, t % 4, :].rearrange("p (n b) -> p b n", n=NT),
                               ACT.Identity).then_inc(hi_done, 1)

            def evacuate(c, mt):
                act.wait_ge(gemm_ready, 24 * c + 4 * mt + 2)
                act.wait_ge(scores_done, 4 * c + mt + 1)
                slot = mt % 2
                for h in range(2):
                    rows = slice(h * HD, (h + 1) * HD)
                    b = qk_bias[rows, QI, mt:mt + 1]
                    act.activation(q1[HD:P, slot, h, :], ps[rows, QI, :], ACT.Identity, bias=b)
                for h in range(2):
                    rows = slice(h * HD, (h + 1) * HD)
                    b = qk_bias[rows, QI, mt:mt + 1]
                    last = act.activation(q2[0:HD, slot, h, :], ps[rows, QI, :], ACT.Identity, bias=b)
                last.then_inc(odd_free, 1)
                act.wait_ge(gemm_ready, 24 * c + 4 * mt + 4)
                for h in range(2):
                    rows = slice(h * HD, (h + 1) * HD)
                    last = act.activation(kk[HD:P, slot, h, :], ps[rows, KI, :], ACT.Identity,
                                          bias=qk_bias[rows, KI, mt:mt + 1])
                last.then_inc(odd_free, 1)

            def square(c, mt):
                act.wait_ge(scores_done, 4 * c + mt + 3)
                act.wait_ge(extracted, 4 * c + mt + 1)
                act.activation(sq_r[:, :, :], ps[:, 4:6, :].rearrange("p a (k n) -> p (a k) n", k=BLK), ACT.Square)
                act.activation(sq_i[:, :, :], ps[:, 6:8, :].rearrange("p a (k n) -> p (a k) n", k=BLK),
                               ACT.Square).then_inc(score_free, 1)

            def evacuate_v(c, blk):
                act.wait_ge(gemm_ready, 24 * c + 16 + 2 * blk + 2)
                act.activation(val[:, blk, :, 1, :],
                               ps[:, (2 * blk + 1) % 4, :].rearrange("p (h d) -> p h d", h=H),
                               ACT.Copy).then_inc(odd_free, 1)

            def chunk(c, last_chunk):
                evacuate(c, 0)
                for mt in range(1, 4):
                    evacuate(c, mt)
                    square(c, mt - 1)
                act.wait_ge(mixed, BLK * c + 1)
                evacuate_v(c, 0)
                square(c, 3)
                act.wait_ge(shifted, 2 * c + 1)
                act.activation(prob[:, :, :, :], prob[:, :, :, :], ACT.Sqrt).then_inc(root_done, 1)
                evacuate_v(c, 1)
                act.wait_ge(shifted, 2 * c + 2)
                act.activation(prob[:, :, :, :], prob[:, :, :, :], ACT.Exp, scale=HD ** -0.5).then_inc(exp_done, 1)
                evacuate_v(c, 2)
                evacuate_v(c, 3)
                for blk in range(BLK):
                    act.wait_ge(turned, BLK * c + blk + 2)
                    act.wait_ge(mixed, BLK * c + blk + 1)
                    act.activation(wide_t[:, :, :], ps[:, 4:6, :].rearrange("p a (h n) -> p (a h) n", n=P),
                                   ACT.Copy).then_inc(turned_out, 1)
                    if not last_chunk:
                        for t in range(2 * blk, 2 * blk + 2):
                            split_s(c + 1, t)

            for t in range(W_TILES):
                act.wait_ge(tile_in[t % 4], 16 * (t // 4 + 1))
                act.activation(w_hi[:, t // DK, t % DK, :], stage[:, t % 4, :], ACT.Identity).then_inc(hi_done, 1)
            for t in range(8):
                split_s(0, t)
            with act.Fori(0, CHUNKS - 1) as c:
                chunk(c, False)
            chunk(CHUNKS - 1, True)

        @block.vector
        def _(dve):
            dve.sem_inc(even_free, 2)
            dve.sem_inc(extracted, 1)
            dve.sem_inc(mixed_out, 1)
            dve.wait_ge(w_bias_in, 32)
            dve.wait_ge(mask_set, 3)

            def split_s(c, t):
                dve.wait_ge(hi_done, W_TILES + 8 * c + t + 1)
                dve.tensor_tensor(s_lo[:, t // DK, t % DK, :].rearrange("p (b n) -> p b n", n=NT),
                                  stage[:, t % 4, :].rearrange("p (n b) -> p b n", n=NT),
                                  s_hi[:, t // DK, t % DK, :].bitcast(F32).rearrange("p (b n) -> p b n", n=NT),
                                  ALU.subtract).then_inc(split_done, 1)

            def evacuate(c, mt):
                dve.wait_ge(gemm_ready, 24 * c + 4 * mt + 1)
                dve.wait_ge(scores_done, 4 * c + mt + 1)
                slot = mt % 2
                for h in range(2):
                    rows = slice(h * HD, (h + 1) * HD)
                    dve.tensor_scalar(q1[0:HD, slot, h, :], ps[rows, QR, :], qk_bias[rows, QR, mt:mt + 1],
                                      None, ALU.add)
                for h in range(2):
                    rows = slice(h * HD, (h + 1) * HD)
                    last = dve.tensor_scalar(q2[HD:P, slot, h, :], ps[rows, QR, :], qk_bias[rows, QR, mt:mt + 1],
                                             -1.0, ALU.add, ALU.mult)
                last.then_inc(even_free, 1)
                dve.wait_ge(gemm_ready, 24 * c + 4 * mt + 3)
                for h in range(2):
                    rows = slice(h * HD, (h + 1) * HD)
                    last = dve.tensor_scalar(kk[0:HD, slot, h, :], ps[rows, KR, :], qk_bias[rows, KR, mt:mt + 1],
                                             None, ALU.add)
                last.then_inc(even_free, 1)

            def extract(c, mt):
                dve.wait_ge(score_free, 4 * c + mt + 1)
                dve.tensor_tensor(sq_r[:, :, :], sq_r[:, :, :], sq_i[:, :, :], ALU.add).then_inc(chain, 1)
                dve.wait_ge(chain, 11 * c + 2 * mt + 1)
                dve.tensor_tensor(sq_r[:, :, :], sq_r[:, :, :],
                                  mask[:, :, :].rearrange("p b n -> p (b n)").unsqueeze(1).broadcast_to(
                                      [P, 2 * BLK, P]), ALU.mult).then_inc(chain, 1)
                dve.wait_ge(chain, 11 * c + 2 * mt + 2)
                if mt == 0:
                    dve.wait_ge(wide_ready, BLK * c + 1)
                dve.tensor_reduce(prob[:, 2 * mt:2 * mt + 2, :, :].rearrange("p h k n -> p (h k) n"),
                                  sq_r[:, :, :].rearrange("p x (b n) -> p x n b", n=NT),
                                  AX_X, ALU.add).then_inc(extracted, 1)

            def evacuate_v(c, blk):
                dve.wait_ge(gemm_ready, 24 * c + 16 + 2 * blk + 1)
                dve.tensor_copy(val[:, blk, :, 0, :],
                                ps[:, (2 * blk) % 4, :].rearrange("p (h d) -> p h d", h=H)).then_inc(even_free, 1)

            def chunk(c, last_chunk):
                flat = prob[:, :, :, :].rearrange("p h k n -> p (h k) n")
                wide_peak = peak[:, :].unsqueeze(2).broadcast_to([P, H * BLK, NT])
                wide_total = total[:, :].unsqueeze(2).broadcast_to([P, H * BLK, NT])
                evacuate(c, 0)
                for mt in range(1, 4):
                    evacuate(c, mt)
                    extract(c, mt - 1)
                dve.wait_ge(mixed, BLK * c + 1)
                evacuate_v(c, 0)
                extract(c, 3)
                dve.wait_ge(extracted, 4 * c + 5)
                dve.tensor_scalar(flat, flat, EPS, None, ALU.add).then_inc(shifted, 1)
                evacuate_v(c, 1)
                dve.wait_ge(root_done, c + 1)
                dve.tensor_reduce(peak[:, :], flat, AX_X, ALU.max).then_inc(chain, 1)
                dve.wait_ge(chain, 11 * c + 9)
                dve.tensor_tensor(flat, flat, wide_peak, ALU.subtract).then_inc(shifted, 1)
                evacuate_v(c, 2)
                dve.wait_ge(exp_done, c + 1)
                dve.tensor_reduce(total[:, :], flat, AX_X, ALU.add).then_inc(chain, 1)
                dve.wait_ge(chain, 11 * c + 10)
                dve.reciprocal(total[:, :], total[:, :]).then_inc(chain, 1)
                dve.wait_ge(chain, 11 * c + 11)
                dve.tensor_tensor(flat, flat, wide_total, ALU.mult).then_inc(prob_ready, 1)
                evacuate_v(c, 3)
                for blk in range(BLK):
                    if not last_chunk:
                        for t in range(2 * blk, 2 * blk + 2):
                            split_s(c + 1, t)
                    dve.wait_ge(mixed, BLK * c + blk + 2)
                    dve.wait_ge(stored[blk % 2], 16 * (2 * c + blk // 2 + 1))
                    dve.tensor_tensor(out_st[:, blk % 2, :, :], ps[:, 6:8, :].rearrange("p a (h n) -> p (a h) n", n=P),
                                      v_bias[:, :].unsqueeze(2).broadcast_to([P, H, P]),
                                      ALU.add).then_inc(mixed_out, 1)

            for t in range(W_TILES):
                dve.wait_ge(hi_done, t + 1)
                dve.tensor_tensor(w_lo[:, t // DK, t % DK, :], stage[:, t % 4, :],
                                  w_hi[:, t // DK, t % DK, :].bitcast(F32), ALU.subtract).then_inc(split_done, 1)
            for t in range(8):
                split_s(0, t)
            with dve.Fori(0, CHUNKS - 1) as c:
                chunk(c, False)
            chunk(CHUNKS - 1, True)

        @block.tensor
        def _(pe):
            pe.sem_inc(scores_done, 2)
            pe.sem_inc(turned, 1)
            pe.sem_inc(mixed, 1)

            def bank_wait(c, i):
                pe.wait_ge(odd_free if i % 2 else even_free, 12 * c + i // 2 + 1)

            def project(c, mt):
                for j in (QR, QI, KR, KI):
                    bank_wait(c, 4 * mt + j)
                    e = j % 2
                    for kt in range(DK):
                        if mt == 0:
                            pe.wait_ge(split_done, W_TILES + 8 * c + DK * e + kt + 1)
                        hi = w_hi[:, j, kt, mt * P:(mt + 1) * P]
                        lo = w_lo[:, j, kt, mt * P:(mt + 1) * P]
                        pe.matmul(ps[:, j, :], hi, s_hi[:, e, kt, :], start=kt == 0, stop=False)
                        pe.matmul(ps[:, j, :], hi, s_lo[:, e, kt, :], start=False, stop=False)
                        last = pe.matmul(ps[:, j, :], lo, s_hi[:, e, kt, :], start=False, stop=kt == DK - 1)
                    last.then_inc(gemm_ready, 1)

            def values(c, blk):
                for e in range(2):
                    i = 2 * blk + e
                    bank_wait(c, 16 + i)
                    cols = slice(blk * P, (blk + 1) * P)
                    for kt in range(DK):
                        hi, lo = s_hi[:, e, kt, cols], s_lo[:, e, kt, cols]
                        pe.matmul(ps[:, i % 4, :], hi, w_hi[:, VR + e, kt, :], start=kt == 0, stop=False)
                        pe.matmul(ps[:, i % 4, :], hi, w_lo[:, VR + e, kt, :], start=False, stop=False)
                        last = pe.matmul(ps[:, i % 4, :], lo, w_hi[:, VR + e, kt, :], start=False,
                                         stop=kt == DK - 1)
                    last.then_inc(gemm_ready, 1)

            def scores(c, mt):
                pe.wait_ge(even_free, 12 * c + 2 * mt + 4)
                pe.wait_ge(odd_free, 12 * c + 2 * mt + 4)
                if mt == 0:
                    pe.wait_ge(turned_out, BLK * c + 1)
                    pe.wait_ge(mixed_out, BLK * c + 1)
                else:
                    pe.wait_ge(score_free, 4 * c + mt)
                slot = mt % 2
                for h in range(2):
                    for blk in range(BLK):
                        cols = slice(blk * P, (blk + 1) * P)
                        pe.matmul(ps[:, 4 + h, cols], q1[:, slot, h, cols], kk[:, slot, h, cols],
                                  start=True, stop=True)
                        last = pe.matmul(ps[:, 6 + h, cols], q2[:, slot, h, cols], kk[:, slot, h, cols],
                                         start=True, stop=True)
                last.then_inc(scores_done, 1)

            def turn(c, blk):
                pe.wait_ge(wide_ready, BLK * c + blk + 2)
                if blk == 0:
                    pe.wait_ge(score_free, 4 * c + 4)
                else:
                    pe.wait_ge(turned_out, BLK * c + blk + 1)
                for h in range(H):
                    last = pe.transpose(ps[:, 4 + h // 4, (h % 4) * P:(h % 4 + 1) * P], wide[:, h, :],
                                        keep["ident"][:, :])
                last.then_inc(turned, 1)

            def mix(c, blk):
                pe.wait_ge(turned_out, BLK * c + blk + 2)
                if blk == 0:
                    pe.wait_ge(even_free, 12 * c + 14)
                    pe.wait_ge(odd_free, 12 * c + 14)
                else:
                    pe.wait_ge(mixed_out, BLK * c + blk + 1)
                for h in range(H):
                    last = pe.matmul(ps[:, 6 + h // 4, (h % 4) * P:(h % 4 + 1) * P],
                                     val[:, blk, h, :, :].rearrange("p r d -> p (r d)"), wide_t[:, h, :],
                                     start=True, stop=True)
                last.then_inc(mixed, 1)

            with pe.Fori(0, CHUNKS) as c:
                project(c, 0)
                for mt in range(1, 4):
                    project(c, mt)
                    scores(c, mt - 1)
                values(c, 0)
                scores(c, 3)
                for blk in range(1, BLK):
                    values(c, blk)
                turn(c, 0)
                for blk in range(1, BLK):
                    turn(c, blk)
                    mix(c, blk - 1)
                mix(c, BLK - 1)


def out_proj(nc, io, scratch, keep, int_w):
    AHEAD = 6
    with ExitStack() as ctx:
        m = Mem(nc, ctx, "out_")
        stage = m.sb("stage", [P, 2, DK, TOK])
        w_hi = m.sb("w_hi", [P, 2, DK, D], F32R)
        w_lo = m.sb("w_lo", [P, 2, DK, D], F32R)
        x_hi = m.sb("x_hi", [P, 2, DK, TOK], F32R)
        x_lo = m.sb("x_lo", [P, 2, DK, TOK], F32R)
        out_st = m.sb("out_st", [P, 2, NT, DK, CB])
        int_stage = m.sb("int_stage", [P, 2, 2, D])
        bias = m.sb("bias", [P, 2, DK])
        ps = m.psum("ps", [P, 8, BANK])
        bias_in = m.sem("bias_in")
        tile_in = [m.sem(f"tile_in{i}") for i in range(2)]
        hi_done = m.sem("hi_done")
        split_done = m.sem("split_done")
        ready = m.sem("ready")
        free = m.sem("free")
        stored = [m.sem(f"stored{i}") for i in range(2)]
        int_in = [m.sem(f"int_in{i}") for i in range(2)]
        int_hi = m.sem("int_hi")
        int_split = m.sem("int_split")
        block = ctx.enter_context(nc.Block())
        src, dst = scratch["mixed"], scratch["attn"]

        @block.sync
        def _(sp):
            sp.dma_start(bias[:, :, :], io["b_o"]).then_inc(bias_in, 16)
            for r in range(2):
                sp.dma_start(stage[:, r, :, :], io["w_o"][r]).then_inc(tile_in[r], 16)

            def load(c):
                for r in range(2):
                    sp.wait_ge(split_done, 2 * c + r + 1)
                    for odd in range(2):
                        for blk in range(NT):
                            sp.dma_start(stage[odd * HD:(odd + 1) * HD, r, :, blk * P:(blk + 1) * P],
                                         src[c, blk, r * HD:(r + 1) * HD, odd::2, :]).then_inc(tile_in[r], 16)

            def store(c):
                for r in range(2):
                    sp.wait_ge(free, 8 * c + 4 * r + 12)
                    sp.dma_start(dst[c, r].rearrange("n p x -> p n x"),
                                 out_st[:, r, :, :, :].rearrange("p n k b -> p n (k b)")).then_inc(stored[r], 16)

            sp.sem_inc(stored[0], 16)
            sp.sem_inc(stored[1], 16)
            load(0)
            with sp.Fori(0, AHEAD) as c:
                for i in range(2):
                    sp.wait_ge(int_split, 2 * c + i + 1)
                    sp.dma_start(int_stage[:, i, :, :], io["w_int"][2 * c + i]).then_inc(int_in[i], 16)
                load(c + 1)
                store(c)
            for c in range(AHEAD, CHUNKS - 1):
                load(c + 1)
                store(c)
            store(CHUNKS - 1)
            for r in range(2):
                sp.wait_ge(stored[r], 16 * (CHUNKS + 1))

        @block.scalar
        def _(act):
            act.sem_inc(free, 8)
            act.wait_ge(bias_in, 16)
            for r in range(2):
                act.wait_ge(tile_in[r], 16)
                act.activation(w_hi[:, r, :, :], stage[:, r, :, :], ACT.Identity).then_inc(hi_done, 1)

            def split_x(c, r):
                act.wait_ge(tile_in[r], 16 + 128 * (c + 1))
                act.activation(x_hi[:, r, :, :], stage[:, r, :, :], ACT.Identity).then_inc(hi_done, 1)

            def evacuate(c, r):
                act.wait_ge(stored[r], 16 * (c + 1))
                for mt in range(DK):
                    act.wait_ge(ready, 8 * c + 4 * r + mt + 1)
                    act.activation(out_st[:, r, :, mt, :],
                                   ps[:, 4 * r + mt, :].rearrange("p (b n) -> p n b", n=NT),
                                   ACT.Identity, bias=bias[:, r, mt:mt + 1]).then_inc(free, 1)

            for r in range(2):
                split_x(0, r)
            with act.Fori(0, CHUNKS - 1) as c:
                for r in range(2):
                    evacuate(c, r)
                    split_x(c + 1, r)
            for r in range(2):
                evacuate(CHUNKS - 1, r)

        @block.vector
        def _(dve):
            for r in range(2):
                dve.wait_ge(hi_done, r + 1)
                dve.tensor_tensor(w_lo[:, r, :, :], stage[:, r, :, :], w_hi[:, r, :, :].bitcast(F32),
                                  ALU.subtract).then_inc(split_done, 1)

            def split_x(c, r):
                dve.wait_ge(hi_done, 2 * c + r + 3)
                dve.tensor_tensor(x_lo[:, r, :, :], stage[:, r, :, :], x_hi[:, r, :, :].bitcast(F32),
                                  ALU.subtract).then_inc(split_done, 1)

            def split_int(c, i):
                tile = (slice(None), bass.ds(2 * c + i, 1), slice(None), slice(None))
                staged = int_stage[:, i:i + 1, :, :]
                dve.wait_ge(int_in[i], 16 * c + 16)
                dve.tensor_scalar(int_w["hi"][tile], staged, 1.0, None, ALU.mult).then_inc(int_hi, 1)
                dve.wait_ge(int_hi, 2 * c + i + 1)
                dve.tensor_tensor(int_w["lo"][tile], staged, int_w["hi"][tile].bitcast(F32),
                                  ALU.subtract).then_inc(int_split, 1)

            dve.sem_inc(int_split, 2)
            with dve.Fori(0, AHEAD) as c:
                for r in range(2):
                    split_x(c, r)
                    split_int(c, r)
            for c in range(AHEAD, CHUNKS):
                for r in range(2):
                    split_x(c, r)

        @block.tensor
        def _(pe):
            with pe.Fori(0, CHUNKS) as c:
                for r in range(2):
                    pe.wait_ge(split_done, 2 * c + r + 3)
                    for mt in range(DK):
                        pe.wait_ge(free, 8 * c + 4 * r + mt + 1)
                        for kt in range(DK):
                            hi = w_hi[:, r, kt, mt * P:(mt + 1) * P]
                            lo = w_lo[:, r, kt, mt * P:(mt + 1) * P]
                            pe.matmul(ps[:, 4 * r + mt, :], hi, x_hi[:, r, kt, :], start=kt == 0, stop=False)
                            pe.matmul(ps[:, 4 * r + mt, :], hi, x_lo[:, r, kt, :], start=False, stop=False)
                            last = pe.matmul(ps[:, 4 * r + mt, :], lo, x_hi[:, r, kt, :], start=False,
                                             stop=kt == DK - 1)
                        last.then_inc(ready, 1)


def interference(nc, io, scratch, keep, int_w):
    RE, IM, NEG = range(3)
    PAIRS = [(0, 1), (0, 2), (1, 2), (0, 3), (1, 3), (2, 3)]
    ON_POOL = 3
    N_PAIRS = len(PAIRS)
    W_LOADS = 4
    TINY = 1e-36
    ZERO_MAG = 1.01e-18
    with ExitStack() as ctx:
        m = Mem(nc, ctx, "int_")
        stage = m.sb("stage", [P, 2, 2, D])
        w3_hi = m.sb("w3_hi", [P, W_LOADS, 2, D], F32R)
        w3_lo = m.sb("w3_lo", [P, W_LOADS, 2, D], F32R)
        a_hi = m.sb("a_hi", [P, 2, 3, D], F32R)
        a_lo = m.sb("a_lo", [P, 2, 3, D], F32R)
        unit = m.sb("unit", [P, 2, NT, D])
        mag = m.sb("mag", [P, NT, D])
        inv = m.sb("inv", [P, NT, D])
        is_zero = m.sb("is_zero", [P, NT, D], BF16)
        s_now = m.sb("s_now", [P, NT, NT])
        prod = m.sb("prod", [P, 2, D])
        sup = m.sb("sup", [P, 2, D])
        norm = m.sb("norm", [P, 1])
        tiny = m.sb("tiny", [P, 1])
        ps = m.psum("ps", [P, 8, BANK])
        slot = lambda p: sup if p % 2 else prod

        tile_in = [m.sem(f"tile_in{i}") for i in range(2)]
        hi_done = m.sem("hi_done")
        w_split = m.sem("w_split")
        a_split = m.sem("a_split")
        neg_done = m.sem("neg_done")
        ready = m.sem("ready")
        free = m.sem("free")
        tiny_set = m.sem("tiny_set")
        squares = m.sem("squares")
        sq_sum = m.sem("sq_sum")
        rooted = m.sem("rooted")
        strength_set = m.sem("strength_set")
        inverted = m.sem("inverted")
        flagged = m.sem("flagged")
        units = m.sem("units")
        multiplied = m.sem("multiplied")
        dot_sum = m.sem("dot_sum")
        pool_step = m.sem("pool_step")
        cosine = m.sem("cosine")
        weighted = m.sem("weighted")
        w_scaled = m.sem("w_scaled")
        applied = m.sem("applied")
        sup_sum = m.sem("sup_sum")
        norm_sum = m.sem("norm_sum")
        norm_root = m.sem("norm_root")
        norm_inv = m.sem("norm_inv")
        sup_scaled = m.sem("sup_scaled")
        stored = m.sem("stored")
        block = ctx.enter_context(nc.Block())
        src, dst = scratch["attn"], scratch["sup"]
        strength = keep["strength"]
        ahead = lambda s: [(s + 1, 2), (s + 1, 3), (s + 2, 0), (s + 2, 1)]

        def staged(c, n):
            early = isinstance(c, int) and NT * c + n < 2
            return NT * c + n + 1 + (0 if early else W_LOADS)

        @block.sync
        def _(sp):
            sp.sem_inc(stored, 16)

            def load(c, n):
                sp.dma_start(stage[:, n % 2, :, :], src[c, :, n].rearrange("r p x -> p r x")
                             ).then_inc(tile_in[n % 2], 16)

            def store(c):
                sp.wait_ge(sup_scaled, c + 1)
                sp.dma_start(dst[c], sup[:, :, :]).then_inc(stored, 16)

            load(0, 0)
            load(0, 1)
            for t in range(W_LOADS):
                if t < 2:
                    sp.wait_ge(neg_done, t + 1)
                else:
                    sp.wait_ge(w_split, t - 1)
                sp.dma_start(stage[:, t % 2, :, :], io["w_int"][12 + t]).then_inc(tile_in[t % 2], 16)
            for n in range(2, NT + 2):
                if n < 4:
                    sp.wait_ge(w_split, n + 1)
                else:
                    sp.wait_ge(neg_done, n - 1)
                load(n // NT, n % NT)

            def chunk(s, loads):
                for c, n in loads:
                    sp.wait_ge(neg_done, NT * c + n - 1)
                    load(c, n)
                store(s)

            with sp.Fori(0, CHUNKS - 2) as s:
                chunk(s, ahead(s))
            chunk(CHUNKS - 2, ahead(CHUNKS - 2)[:2])
            chunk(CHUNKS - 1, [])
            sp.wait_ge(stored, 16 * (CHUNKS + 1))

        @block.gpsimd
        def _(pool):
            nc.gpsimd.memset(tiny[:, :], TINY).then_inc(tiny_set, 1)

            def split_attn(c, n):
                pool.wait_ge(hi_done, staged(c, n))
                nc.gpsimd.tensor_tensor(a_lo[:, n % 2, 0:2, :], stage[:, n % 2, :, :],
                                        a_hi[:, n % 2, 0:2, :].bitcast(F32), ALU.subtract).then_inc(a_split, 1)

            def add_squares(c, n):
                pool.wait_ge(squares, NT * c + n + 1)
                nc.gpsimd.tensor_tensor(mag[:, n, :], mag[:, n, :], prod[:, n % 2, :], ALU.add).then_inc(sq_sum, 1)

            def finish_pair(c, p):
                i, j = PAIRS[p]
                f = slot(p)[:, 0, :]
                steps = 2 * ON_POOL + N_PAIRS - ON_POOL
                done = 2 * p if p < ON_POOL else ON_POOL + p
                if p < ON_POOL:
                    pool.wait_ge(multiplied, N_PAIRS * c + p + 1)
                    nc.gpsimd.tensor_tensor(f, f, slot(p)[:, 1, :], ALU.add).then_inc(pool_step, 1)
                    done += 1
                    pool.wait_ge(pool_step, steps * c + done)
                else:
                    pool.wait_ge(dot_sum, (N_PAIRS - ON_POOL) * c + p - ON_POOL + 1)
                pool.wait_ge(flagged, NT * c + j + 1)
                nc.gpsimd.tensor_tensor(f, f, is_zero[:, i, :], ALU.add).then_inc(pool_step, 1)
                pool.wait_ge(pool_step, steps * c + done + 1)
                nc.gpsimd.tensor_tensor(f, f, is_zero[:, j, :], ALU.add).then_inc(cosine, 1)

            def chunk(s, splits, next_too):
                add_squares(s, 2)
                add_squares(s, 3)
                finish_pair(s, 0)
                for c, n in splits[:1]:
                    split_attn(c, n)
                finish_pair(s, 1)
                finish_pair(s, 2)
                for c, n in splits[1:2]:
                    split_attn(c, n)
                for p in range(3, N_PAIRS):
                    finish_pair(s, p)
                for c, n in splits[2:]:
                    split_attn(c, n)
                if next_too:
                    add_squares(s + 1, 0)
                    add_squares(s + 1, 1)

            for n in range(NT + 2):
                split_attn(n // NT, n % NT)
            add_squares(0, 0)
            add_squares(0, 1)
            with pool.Fori(0, CHUNKS - 2) as s:
                chunk(s, ahead(s), True)
            chunk(CHUNKS - 2, ahead(CHUNKS - 2)[:2], True)
            chunk(CHUNKS - 1, [], False)

        @block.scalar
        def _(act):
            act.sem_inc(free, NT)

            def split_attn(c, n):
                early = isinstance(c, int) and NT * c + n < 2
                act.wait_ge(tile_in[n % 2], 16 * (2 * c + n // 2 + 1 + (0 if early else W_LOADS // 2)))
                if not early:
                    act.wait_ge(ready, NT * c + n - 1)
                act.activation(a_hi[:, n % 2, 0:2, :], stage[:, n % 2, :, :], ACT.Identity).then_inc(hi_done, 1)
                act.activation(a_hi[:, n % 2, NEG, :], stage[:, n % 2, IM, :], ACT.Identity, scale=-1.0)
                act.wait_ge(a_split, NT * c + n + 1)
                act.activation(a_lo[:, n % 2, NEG, :], a_lo[:, n % 2, IM, :].bitcast(F32), ACT.Identity,
                               scale=-1.0).then_inc(neg_done, 1)

            def square(c, n):
                act.wait_ge(ready, NT * c + n + 1)
                act.wait_ge(w_scaled, 3 * c + (2 if n < 2 else 3))
                if not isinstance(c, int) or c > 0 or n >= 2:
                    act.wait_ge(sq_sum, NT * c + n - 1)
                act.activation(mag[:, n, :], ps[:, 2 * n, :], ACT.Square)
                act.activation(prod[:, n % 2, :], ps[:, 2 * n + 1, :], ACT.Square).then_inc(squares, 1)

            def root_and_copy(c, n):
                act.wait_ge(sq_sum, NT * c + n + 1)
                act.activation(mag[:, n, :], mag[:, n, :], ACT.Sqrt, bias=tiny[:, 0:1]).then_inc(rooted, 1)
                act.wait_ge(sup_sum, 3 * c + max(n, 1))
                act.activation(unit[:, :, n, :], ps[:, 2 * n:2 * n + 2, :], ACT.Copy).then_inc(free, 1)

            def chunk(s, splits, next_too):
                root_and_copy(s, 0)
                square(s, 2)
                root_and_copy(s, 1)
                square(s, 3)
                root_and_copy(s, 2)
                root_and_copy(s, 3)
                for c, n in splits:
                    split_attn(c, n)
                if next_too:
                    square(s + 1, 0)
                    square(s + 1, 1)
                act.wait_ge(norm_sum, s + 1)
                act.activation(norm[:, :], norm[:, :], ACT.Sqrt).then_inc(norm_root, 1)
                act.wait_ge(norm_inv, s + 1)
                act.activation(sup[:, :, :], sup[:, :, :], ACT.Identity, scale=norm[:, 0:1]).then_inc(sup_scaled, 1)

            split_attn(0, 0)
            split_attn(0, 1)
            for t in range(W_LOADS):
                act.wait_ge(tile_in[t % 2], 16 * (t // 2 + 2))
                act.activation(w3_hi[:, t, :, :], stage[:, t % 2, :, :], ACT.Identity).then_inc(hi_done, 1)
            act.wait_ge(tiny_set, 1)
            for n in range(2, NT + 2):
                split_attn(n // NT, n % NT)
            square(0, 0)
            square(0, 1)
            with act.Fori(0, CHUNKS - 2) as s:
                chunk(s, ahead(s), True)
            chunk(CHUNKS - 2, ahead(CHUNKS - 2)[:2], True)
            chunk(CHUNKS - 1, [], False)

        @block.vector
        def _(dve):
            dve.sem_inc(w_scaled, 3)
            dve.sem_inc(sup_sum, 3)
            for t in range(W_LOADS):
                dve.wait_ge(hi_done, t + 3)
                dve.tensor_tensor(w3_lo[:, t, :, :], stage[:, t % 2, :, :], w3_hi[:, t, :, :].bitcast(F32),
                                  ALU.subtract).then_inc(w_split, 1)

            def unit_vector(c, n):
                dve.wait_ge(rooted, NT * c + n + 1)
                dve.tensor_scalar(is_zero[:, n, :], mag[:, n, :], ZERO_MAG, None, ALU.is_le).then_inc(flagged, 1)
                dve.reciprocal(inv[:, n, :], mag[:, n, :]).then_inc(inverted, 1)
                dve.wait_ge(inverted, NT * c + n + 1)
                dve.wait_ge(free, NT * c + n + NT + 1)
                dve.tensor_tensor(unit[:, :, n, :], unit[:, :, n, :],
                                  inv[:, n, :].unsqueeze(1).broadcast_to([P, 2, D]), ALU.mult).then_inc(units, 1)

            def multiply_pair(c, p):
                i, j = PAIRS[p]
                dve.wait_ge(units, NT * c + j + 1)
                if p == 0:
                    dve.wait_ge(sq_sum, NT * c + NT)
                elif p == 1:
                    dve.wait_ge(stored, 16 * c + 16)
                else:
                    dve.wait_ge(weighted, 2 * (N_PAIRS * c + p - 1))
                dve.tensor_tensor(slot(p)[:, :, :], unit[:, :, i, :], unit[:, :, j, :],
                                  ALU.mult).then_inc(multiplied, 1)
                if p >= ON_POOL:
                    dve.wait_ge(multiplied, N_PAIRS * c + p + 1)
                    dve.tensor_tensor(slot(p)[:, 0, :], slot(p)[:, 0, :], slot(p)[:, 1, :],
                                      ALU.add).then_inc(dot_sum, 1)

            def weigh_pair(c, p):
                dve.wait_ge(cosine, N_PAIRS * c + p + 1)
                f = slot(p)[:, 0, :]
                for k, (a, b) in enumerate((PAIRS[p], PAIRS[p][::-1])):
                    earlier = [2 * q + PAIRS[q].index(b) for q in range(p) if b in PAIRS[q]]
                    weight = s_now[:, a, b:b + 1]
                    if not earlier:
                        dve.tensor_scalar(inv[:, b, :], f, weight, s_now[:, b, b:b + 1],
                                          ALU.mult, ALU.add).then_inc(weighted, 1)
                    else:
                        dve.wait_ge(weighted, 2 * N_PAIRS * c + 2 * p + k - (1 if k else 0))
                        dve.scalar_tensor_tensor(out=inv[:, b, :], in0=f, scalar=weight, in1=inv[:, b, :],
                                                 op0=ALU.mult, op1=ALU.add).then_inc(weighted, 1)

            def apply(c, first, tokens, k):
                some = slice(first, first + tokens)
                dve.tensor_tensor(inv[:, some, :], inv[:, some, :], mag[:, some, :],
                                  ALU.mult).then_inc(w_scaled, 1)
                dve.wait_ge(w_scaled, 3 * c + 3 + k)
                for n in range(first, first + tokens):
                    dve.tensor_tensor(unit[:, :, n, :], unit[:, :, n, :],
                                      inv[:, n, :].unsqueeze(1).broadcast_to([P, 2, D]),
                                      ALU.mult).then_inc(applied, 1)

            with dve.Fori(0, CHUNKS) as c:
                dve.tensor_scalar(s_now[:, :, :].rearrange("p i j -> p (i j)"),
                                  strength[:, bass.ds(c * NT * NT, NT * NT)], 1.0, None, ALU.mult
                                  ).then_inc(strength_set, 1)
                unit_vector(c, 0)
                unit_vector(c, 1)
                multiply_pair(c, 0)
                unit_vector(c, 2)
                dve.wait_ge(strength_set, c + 1)
                weigh_pair(c, 0)
                multiply_pair(c, 1)
                multiply_pair(c, 2)
                unit_vector(c, 3)
                weigh_pair(c, 1)
                multiply_pair(c, 3)
                weigh_pair(c, 2)
                multiply_pair(c, 4)
                weigh_pair(c, 3)
                multiply_pair(c, 5)
                dve.wait_ge(weighted, 2 * N_PAIRS * c + 8)
                apply(c, 0, 1, 1)
                weigh_pair(c, 4)
                dve.wait_ge(weighted, 2 * N_PAIRS * c + 10)
                apply(c, 1, 1, 2)
                weigh_pair(c, 5)
                dve.wait_ge(weighted, 2 * N_PAIRS * c + 12)
                dve.wait_ge(applied, NT * c + 2)
                dve.tensor_tensor(sup[:, :, :], unit[:, :, 0, :], unit[:, :, 1, :], ALU.add).then_inc(sup_sum, 1)
                apply(c, 2, 2, 3)
                for n in (2, 3):
                    dve.wait_ge(applied, NT * c + n + 1)
                    dve.wait_ge(sup_sum, 3 * c + n + 2)
                    dve.tensor_tensor(sup[:, :, :], sup[:, :, :], unit[:, :, n, :], ALU.add).then_inc(sup_sum, 1)
                dve.wait_ge(applied, NT * c + NT)
                dve.wait_ge(sup_sum, 3 * c + 6)
                dve.tensor_tensor_reduce(out=inv[:, 0:2, :], in0=sup[:, :, :], in1=sup[:, :, :], scale=1.0,
                                         scalar=EPS, op0=ALU.mult, op1=ALU.add,
                                         accum_out=norm[:, :]).then_inc(norm_sum, 1)
                dve.wait_ge(norm_root, c + 1)
                dve.reciprocal(norm[:, :], norm[:, :]).then_inc(norm_inv, 1)

        @block.tensor
        def _(pe):
            def weights(n, w, kt):
                if n < 3:
                    t = n * 4 + w * 2 + kt // 2
                    return int_w["hi"][:, t, kt % 2, :], int_w["lo"][:, t, kt % 2, :]
                return w3_hi[:, w * 2 + kt // 2, kt % 2, :], w3_lo[:, w * 2 + kt // 2, kt % 2, :]

            with pe.Fori(0, CHUNKS) as c:
                for n in range(NT):
                    pe.wait_ge(neg_done, NT * c + n + 1)
                    pe.wait_ge(free, NT * c + n + 1)
                    if n == 3:
                        pe.wait_ge(w_split, W_LOADS)
                    R, I = ps[:, 2 * n, :], ps[:, 2 * n + 1, :]
                    for kt in range(DK):
                        cols = slice(kt * CB, (kt + 1) * CB)
                        for out, comp, w in ((R, RE, 0), (I, RE, 1), (I, IM, 0), (R, NEG, 1)):
                            first = kt == 0 and comp == RE
                            end = kt == DK - 1 and comp in (IM, NEG)
                            hi, lo = a_hi[:, n % 2, comp, cols], a_lo[:, n % 2, comp, cols]
                            wh, wl = weights(n, w, kt)
                            pe.matmul(out, hi, wh, start=first, stop=False)
                            pe.matmul(out, hi, wl, start=False, stop=False)
                            last = pe.matmul(out, lo, wh, start=False, stop=end)
                    last.then_inc(ready, 1)


def head(nc, io, scratch, keep):
    HALF = B // 2
    HC = HALF // CB
    RE, IM, NEG = range(3)
    MEAS, POST, TOP1, TOP2, W_TILES = 0, 8, 12, 16, 18
    with ExitStack() as ctx:
        m = Mem(nc, ctx, "head_")
        w_stage = m.sb("w_stage", [P, 6, D])
        w_hi = m.sb("w_hi", [P, W_TILES, D], F32R)
        w_lo = m.sb("w_lo", [P, W_TILES, D], F32R)
        sup = m.sb("sup", [P, HC, 2, D])
        top_x = m.sb("top_x", [P, DK, HALF])
        x_hi = m.sb("x_hi", [P, 3, DK, HALF], F32R)
        x_lo = m.sb("x_lo", [P, 3, DK, HALF], F32R)
        act_a = m.sb("act_a", [P, DK, HALF])
        act_b = m.sb("act_b", [P, DK, HALF])
        stat = m.sb("stat", [P, 4, HALF])
        h2 = m.sb("h2", [P, 2, HALF])
        y, y2 = m.sb("y", [1, HALF]), m.sb("y2", [1, HALF])
        bias = m.sb("bias", [P, 5, DK])
        mean_w = m.sb("mean_w", [P, P])
        ps = m.psum("ps", [P, 8, BANK])

        bias_in = m.sem("bias_in")
        w_in = [m.sem(f"w_in{i}") for i in range(3)]
        w_hi_done = m.sem("w_hi_done")
        w_split = m.sem("w_split")
        sup_in = m.sem("sup_in")
        top_x_in = m.sem("top_x_in")
        mean_set = m.sem("mean_set")
        supT = m.sem("supT")
        x_hi_done = m.sem("x_hi_done")
        x_split = m.sem("x_split")
        x_neg = m.sem("x_neg")
        measured = m.sem("measured")
        meas_sq = m.sem("meas_sq")
        amp_sq = m.sem("amp_sq")
        amp = m.sem("amp")
        posted = m.sem("posted")
        post_out = m.sem("post_out")
        col_sum = m.sem("col_sum")
        col_mean = m.sem("col_mean")
        var = m.sem("var")
        std = m.sem("std")
        normed = m.sem("normed")
        gelu = m.sem("gelu")
        top1 = m.sem("top1")
        top1_sum = m.sem("top1_sum")
        top1_out = m.sem("top1_out")
        top2 = m.sem("top2")
        top2_out = m.sem("top2_out")
        top3 = m.sem("top3")
        top3_out = m.sem("top3_out")
        stored = m.sem("stored")
        block = ctx.enter_context(nc.Block())
        src, top_part, out = scratch["sup"], scratch["pre"], io["out"]

        @block.sync
        def _(sp):
            sp.dma_start(bias[:, :, :], io["b_head"]).then_inc(bias_in, 16)
            for hb in range(2):
                if hb:
                    sp.wait_ge(supT, 2)
                for c in range(HC):
                    sp.dma_start(sup[:, c, :, :], src[hb * HC + c]).then_inc(sup_in, 16)
                if hb == 0:
                    for t in range(W_TILES // 2):
                        if t >= 3:
                            sp.wait_ge(w_split, t - 2)
                        s = 2 * (t % 3)
                        sp.dma_start(w_stage[:, s:s + 2, :], io["w_head"][t]).then_inc(w_in[t % 3], 16)
                if hb:
                    sp.wait_ge(top1_sum, 1)
                sp.dma_start(top_x[:, :, :], top_part[8, :, :, hb * HALF:(hb + 1) * HALF].rearrange("k p b -> p k b")
                             ).then_inc(top_x_in, 16)
            for hb in range(2):
                sp.wait_ge(top3_out, hb + 1)
                sp.dma_start(out[hb], y[0:1, :] if hb == 0 else y2[0:1, :]).then_inc(stored, 16)
            sp.wait_ge(stored, 32)

        @block.gpsimd
        def _(pool):
            nc.gpsimd.memset(mean_w[:, :], 1.0 / D).then_inc(mean_set, 1)

        flat = lambda t: t.rearrange("p k n -> p (k n)")

        @block.scalar
        def _(act):
            def split_w(t):
                act.wait_ge(w_in[t % 3], 16 * (t // 3 + 1))
                s = 2 * (t % 3)
                act.activation(w_hi[:, 2 * t:2 * t + 2, :], w_stage[:, s:s + 2, :], ACT.Identity).then_inc(w_hi_done, 1)

            for t in range(4):
                split_w(t)
            act.wait_ge(bias_in, 16)
            for hb in range(2):
                if hb:
                    act.wait_ge(top2, 2)
                for part in range(2):
                    act.wait_ge(supT, 2 * hb + part + 1)
                    act.activation(x_hi[:, part, :, :], ps[:, 4 * part:4 * part + 4, :],
                                   ACT.Identity).then_inc(x_hi_done, 1)
                act.wait_ge(x_hi_done, 6 * hb + 2)
                act.activation(x_hi[:, NEG, :, :], x_hi[:, IM, :, :].bitcast(F32), ACT.Identity,
                               scale=-1.0).then_inc(x_hi_done, 1)
                act.wait_ge(x_split, 5 * hb + 2)
                act.activation(x_lo[:, NEG, :, :], x_lo[:, IM, :, :].bitcast(F32), ACT.Identity,
                               scale=-1.0).then_inc(x_neg, 1)
                if hb == 0:
                    for t in range(4, W_TILES // 2):
                        split_w(t)
                act.wait_ge(measured, 8 * hb + 4)
                act.activation(act_a[:, :, :], ps[:, 0:4, :], ACT.Square).then_inc(meas_sq, 1)
                act.wait_ge(measured, 8 * hb + 8)
                act.activation(act_b[:, :, :], ps[:, 4:8, :], ACT.Square).then_inc(meas_sq, 1)
                act.wait_ge(amp_sq, hb + 1)
                act.activation(act_a[:, :, :], act_a[:, :, :], ACT.Sqrt).then_inc(amp, 1)
                act.wait_ge(amp, hb + 1)
                act.activation(x_hi[:, 0, :, :], act_a[:, :, :], ACT.Identity).then_inc(x_hi_done, 1)
                act.wait_ge(x_split, 5 * hb + 3)
                for mt in range(DK):
                    act.wait_ge(posted, 4 * hb + mt + 1)
                    last = act.activation(act_a[:, mt, :], ps[:, mt, :], ACT.Identity, bias=bias[:, 0, mt:mt + 1])
                last.then_inc(post_out, 1)
                act.wait_ge(post_out, 2 * hb + 1)
                act.activation(act_b[:, :, :], act_a[:, :, :], ACT.Square).then_inc(post_out, 1)
                act.wait_ge(var, 4 * hb + 4)
                act.activation(stat[:, 1, :], stat[:, 1, :], ACT.Sqrt).then_inc(std, 1)
                act.wait_ge(normed, 3 * hb + 3)
                for mt in range(DK):
                    last = act.activation(act_a[:, mt, :], act_a[:, mt, :], ACT.Gelu, scale=bias[:, 1, mt:mt + 1],
                                          bias=bias[:, 2, mt:mt + 1])
                last.then_inc(gelu, 1)
                act.wait_ge(gelu, hb + 1)
                act.activation(x_hi[:, 1, :, :], act_a[:, :, :], ACT.Identity).then_inc(x_hi_done, 1)
                act.wait_ge(top1_sum, hb + 1)
                act.activation(act_b[:, :, :], act_b[:, :, :], ACT.Relu).then_inc(top1_out, 1)
                act.wait_ge(top1_out, hb + 1)
                act.activation(x_hi[:, 2, :, :], act_b[:, :, :], ACT.Identity).then_inc(x_hi_done, 1)
                for mt in range(2):
                    act.wait_ge(top2, 2 * hb + mt + 1)
                    last = act.activation(h2[:, mt, :], ps[:, 4 + mt, :], ACT.Relu, bias=bias[:, 3, mt:mt + 1])
                last.then_inc(top2_out, 1)
                act.wait_ge(top3, hb + 1)
                act.activation((y if hb == 0 else y2)[0:1, :], ps[0:1, 6, :], ACT.Copy).then_inc(top3_out, 1)

        @block.vector
        def _(dve):
            def split_w(t):
                dve.wait_ge(w_hi_done, t + 1)
                s = 2 * (t % 3)
                dve.tensor_tensor(w_lo[:, 2 * t:2 * t + 2, :], w_stage[:, s:s + 2, :],
                                  w_hi[:, 2 * t:2 * t + 2, :].bitcast(F32), ALU.subtract).then_inc(w_split, 1)

            for t in range(4):
                split_w(t)
            for hb in range(2):
                for part in range(2):
                    dve.wait_ge(x_hi_done, 6 * hb + part + 1)
                    dve.tensor_tensor(x_lo[:, part, :, :], ps[:, 4 * part:4 * part + 4, :],
                                      x_hi[:, part, :, :].bitcast(F32), ALU.subtract).then_inc(x_split, 1)
                if hb == 0:
                    for t in range(4, W_TILES // 2):
                        split_w(t)
                dve.wait_ge(meas_sq, 2 * hb + 2)
                dve.tensor_tensor(act_a[:, :, :], act_a[:, :, :], act_b[:, :, :], ALU.add).then_inc(amp_sq, 1)
                dve.wait_ge(x_hi_done, 6 * hb + 4)
                dve.tensor_tensor(x_lo[:, 0, :, :], act_a[:, :, :], x_hi[:, 0, :, :].bitcast(F32),
                                  ALU.subtract).then_inc(x_split, 1)
                for i, t in enumerate((act_a, act_b)):
                    dve.wait_ge(post_out, 2 * hb + i + 1)
                    dve.tensor_reduce(stat[:, i, :], t[:, :, :].rearrange("p k n -> p n k"), AX_X,
                                      ALU.add).then_inc(col_sum, 1)
                dve.wait_ge(col_mean, 2 * hb + 2)
                dve.tensor_copy(stat[:, 0, :], ps[:, 4, :]).then_inc(var, 1)
                dve.wait_ge(var, 4 * hb + 1)
                dve.tensor_tensor(stat[:, 2, :], stat[:, 0, :], stat[:, 0, :], ALU.mult).then_inc(var, 1)
                dve.wait_ge(var, 4 * hb + 2)
                dve.tensor_tensor(stat[:, 1, :], ps[:, 5, :], stat[:, 2, :], ALU.subtract).then_inc(var, 1)
                dve.wait_ge(var, 4 * hb + 3)
                dve.tensor_scalar(stat[:, 1, :], stat[:, 1, :], 0.0, LN_EPS, ALU.max, ALU.add).then_inc(var, 1)
                wide = lambda i: stat[:, i, :].unsqueeze(1).broadcast_to([P, DK, HALF])
                dve.tensor_tensor(act_a[:, :, :], act_a[:, :, :], wide(0), ALU.subtract).then_inc(normed, 1)
                dve.wait_ge(std, hb + 1)
                dve.reciprocal(stat[:, 3, :], stat[:, 1, :]).then_inc(normed, 1)
                dve.wait_ge(normed, 3 * hb + 2)
                dve.tensor_tensor(act_a[:, :, :], act_a[:, :, :], wide(3), ALU.mult).then_inc(normed, 1)
                dve.wait_ge(x_hi_done, 6 * hb + 5)
                dve.tensor_tensor(x_lo[:, 1, :, :], act_a[:, :, :], x_hi[:, 1, :, :].bitcast(F32),
                                  ALU.subtract).then_inc(x_split, 1)
                dve.wait_ge(top1, 4 * hb + 4)
                dve.wait_ge(top_x_in, 16 * (hb + 1))
                dve.tensor_tensor(act_b[:, :, :], ps[:, 0:4, :], top_x[:, :, :], ALU.add).then_inc(top1_sum, 1)
                dve.wait_ge(x_hi_done, 6 * hb + 6)
                dve.tensor_tensor(x_lo[:, 2, :, :], act_b[:, :, :], x_hi[:, 2, :, :].bitcast(F32),
                                  ALU.subtract).then_inc(x_split, 1)

        @block.tensor
        def _(pe):
            def product(bank, w, wcols, comp, first, end):
                for kt in range(DK):
                    hi, lo = w_hi[:, w[kt], wcols[kt]], w_lo[:, w[kt], wcols[kt]]
                    pe.matmul(ps[:, bank, :], hi, x_hi[:, comp, kt, :], start=first and kt == 0, stop=False)
                    pe.matmul(ps[:, bank, :], hi, x_lo[:, comp, kt, :], start=False, stop=False)
                    last = pe.matmul(ps[:, bank, :], lo, x_hi[:, comp, kt, :], start=False,
                                     stop=end and kt == DK - 1)
                return last

            def tiles(base, mt):
                return [base + kt for kt in range(DK)], [slice(mt * P, (mt + 1) * P)] * DK

            for hb in range(2):
                pe.wait_ge(sup_in, 16 * HC * (hb + 1))
                if hb:
                    pe.wait_ge(top3_out, 1)
                for part in range(2):
                    for kt in range(DK):
                        for c in range(HC):
                            last = pe.transpose(ps[:, 4 * part + kt, c * P:(c + 1) * P],
                                                sup[:, c, part, kt * P:(kt + 1) * P], keep["ident"][:, :])
                    last.then_inc(supT, 1)
                pe.wait_ge(w_split, 4)
                pe.wait_ge(x_split, 5 * hb + 2)
                pe.wait_ge(x_neg, hb + 1)
                for mt in range(DK):
                    product(mt, *tiles(MEAS, mt), RE, True, False)
                    product(mt, *tiles(MEAS + 4, mt), NEG, False, True).then_inc(measured, 1)
                for mt in range(DK):
                    product(4 + mt, *tiles(MEAS + 4, mt), RE, True, False)
                    product(4 + mt, *tiles(MEAS, mt), IM, False, True).then_inc(measured, 1)
                pe.wait_ge(w_split, W_TILES // 2)
                pe.wait_ge(x_split, 5 * hb + 3)
                for mt in range(DK):
                    product(mt, *tiles(POST, mt), 0, True, True).then_inc(posted, 1)
                pe.wait_ge(mean_set, 1)
                for i in range(2):
                    pe.wait_ge(col_sum, 2 * hb + i + 1)
                    pe.matmul(ps[:, 4 + i, :], mean_w[:, :], stat[:, i, :], start=True, stop=True).then_inc(col_mean, 1)
                pe.wait_ge(x_split, 5 * hb + 4)
                for mt in range(DK):
                    product(mt, *tiles(TOP1, mt), 1, True, True).then_inc(top1, 1)
                pe.wait_ge(x_split, 5 * hb + 5)
                pe.wait_ge(var, 4 * hb + 3)
                for mt in range(2):
                    w = [TOP2 + kt // 2 for kt in range(DK)]
                    cols = [slice((kt % 2) * 256 + mt * P, (kt % 2) * 256 + (mt + 1) * P) for kt in range(DK)]
                    product(4 + mt, w, cols, 2, True, True).then_inc(top2, 1)
                pe.wait_ge(top2_out, hb + 1)
                for mt in range(2):
                    last = pe.matmul(ps[0:1, 6, :], bias[:, 4, mt:mt + 1], h2[:, mt, :], start=mt == 0, stop=mt == 1)
                last.then_inc(top3, 1)


def build(nc, io):
    scratch = {
        "pre": nc.dram_tensor("pre", (17, GROUP, P, B), F32).ap(),
        "mixed": nc.dram_tensor("mixed", (CHUNKS, NT, P, H, P), F32).ap(),
        "attn": nc.dram_tensor("attn", (CHUNKS, 2, NT, P, DK * CB), F32).ap(),
        "sup": nc.dram_tensor("sup", (CHUNKS, P, 2, D), F32).ap(),
    }
    with ExitStack() as ctx:
        m = Mem(nc, ctx, "keep_")
        keep = {
            "ident": m.sb("ident", [P, P]),
            "ids": m.sb("ids", [P, CHUNKS, NT], I32),
            "strength": m.sb("strength", [P, CHUNKS * NT * NT]),
        }
        encoders(nc, io, scratch, keep)
        attention(nc, io, scratch, keep)
        with ExitStack() as later:
            w = Mem(nc, later, "int_")
            int_w = {part: w.sb("w_" + part, [P, 12, 2, D], F32R) for part in ("hi", "lo")}
            out_proj(nc, io, scratch, keep, int_w)
            interference(nc, io, scratch, keep, int_w)
        head(nc, io, scratch, keep)


def kernel(**inputs):
    import numpy as np
    import concourse.bacc as bacc
    from concourse.bass_utils import run_bass_kernel_spmd as run

    v = {k.replace("L0_rec_", ""): np.asarray(a) for k, a in inputs.items()}

    def rows(w):
        return w.reshape(-1, P, w.shape[1])

    def cols(*vectors):
        return np.concatenate([x.reshape(-1, P) for x in vectors]).T

    w_enc = np.concatenate([v["er_W1"].T, v["ei_W1"].T, v["W_top1"][D:], v["er_W2"].T, v["ei_W2"].T], axis=1)
    head_w = np.concatenate([
        rows(v["meas_Mr"].T), rows(v["meas_Mi"].T), rows(v["post_W"].T), rows(v["W_top1"][:D]),
        rows(v["W_top2"]).reshape(2, 2, P, 256).transpose(0, 2, 1, 3).reshape(2, P, D)])
    int_w = np.stack([v["int_Wr"], v["int_Wi"]], axis=1).transpose(0, 1, 3, 2)
    zero = np.zeros(256, np.float32)
    arrays = {
        "xT": v["r_x"].T.reshape(KT, P, B),
        "w_enc": w_enc.reshape(KT, P, 17, D).transpose(2, 0, 1, 3),
        "b_enc": cols(v["er_b1"], v["ei_b1"], v["b_top1"], v["er_b2"], v["ei_b2"]),
        "ln_g": cols(v["er_g1"], v["ei_g1"]),
        "ln_b": cols(v["er_be1"], v["ei_be1"]),
        "ids": v["ids"].reshape(CHUNKS, P, NT).transpose(1, 0, 2),
        "tbl_0": v["tbl_0"], "tbl_1": v["tbl_1"], "tbl_2": v["tbl_2"], "tbl_3": v["tbl_3"],
        "w_qkv": np.concatenate([rows(v[w].T) for w in ("Wq_r", "Wq_i", "Wk_r", "Wk_i", "Wv_r", "Wv_i")]),
        "b_qk": cols(v["bq_r"], v["bq_i"], v["bk_r"], v["bk_i"]).reshape(P, 4, DK),
        "b_v": np.stack([v["bv_r"].reshape(H, HD), v["bv_i"].reshape(H, HD)]).transpose(0, 2, 1).reshape(P, H),
        "w_o": np.stack([v["Wo_r"].T, v["Wo_i"].T]).reshape(2, DK, P, D).transpose(0, 2, 1, 3),
        "b_o": cols(v["bo_r"], v["bo_i"]).reshape(P, 2, DK),
        "w_int": int_w.reshape(16, 2, P, D).transpose(0, 2, 1, 3),
        "w_head": head_w.reshape(9, 2, P, D).transpose(0, 2, 1, 3),
        "b_head": cols(v["post_b"], v["post_g"], v["post_be"], v["b_top2"], zero, v["W_top3"][:, 0], zero
                       ).reshape(P, 5, DK),
    }
    arrays = {name: np.ascontiguousarray(a) for name, a in arrays.items()}
    nc = bacc.Bacc("TRN2", target_bir_lowering=False, num_devices=1)
    io = {name: nc.dram_tensor(name, a.shape, mybir.dt.from_np(a.dtype), kind="ExternalInput").ap()
          for name, a in arrays.items()}
    y = nc.dram_tensor("y", (2, 1, B // 2), F32, kind="ExternalOutput").ap()
    io["out"] = y
    build(nc, io)
    result = run(nc, [arrays], core_ids=[0])
    return result.results[0]["y"].reshape(B, 1)
```

```python
from contextlib import ExitStack

import concourse.bass as bass
from concourse import mybir

F32 = mybir.dt.float32
F32R = mybir.dt.float32r
BF16 = mybir.dt.bfloat16
I32 = mybir.dt.int32
U32 = mybir.dt.uint32
ACT = mybir.ActivationFunctionType
ALU = mybir.AluOpType
AX_X = mybir.AxisListType.X

P = 128
B = 1024
IN = 2048
D = 512
NT = 4
H = 8
HD = D // H
BANK = 512
KT = IN // P
DK = D // P
GROUP = 4
CB = 128
CHUNKS = B // CB
TOK = CB * NT
LN_EPS = 1e-5
EPS = 1e-8


class Mem:

    def __init__(self, nc, ctx, prefix):
        self.nc, self.ctx, self.prefix = nc, ctx, prefix

    def sb(self, name, shape, dt=F32):
        return self.ctx.enter_context(self.nc.sbuf_tensor(self.prefix + name, shape, dt))

    def psum(self, name, shape):
        return self.ctx.enter_context(self.nc.psum_tensor(self.prefix + name, shape, F32))

    def sem(self, name):
        return self.ctx.enter_context(self.nc.semaphore(self.prefix + name))


def encoders(nc, io, scratch, keep):
    W1_GROUPS, TOP, GROUPS = 8, 8, 17
    RING = 4
    SLOTS = 4
    EARLY = RING - 1
    HALF = B // 2
    with ExitStack() as ctx:
        m = Mem(nc, ctx, "enc_")
        src_hi = m.sb("src_hi", [P, KT, B], F32R)
        src_lo = m.sb("src_lo", [P, KT, B], F32R)
        src_stage = m.sb("src_stage", [P, SLOTS, B])
        w_stage = m.sb("w_stage", [P, RING, D])
        w_hi = m.sb("w_hi", [P, RING, D], F32R)
        w_lo = m.sb("w_lo", [P, RING, D], F32R)
        out_stage = m.sb("out_stage", [P, 8, BANK])
        square = m.sb("square", [P, 2, BANK])
        stats = m.sb("stats", [P, 2, 2, B])
        bias = m.sb("bias", [P, GROUPS * GROUP])
        group_bias = m.sb("group_bias", [P, GROUP])
        ln_g = m.sb("ln_g", [P, 2 * KT])
        ln_b = m.sb("ln_b", [P, 2 * KT])
        mean_w = m.sb("mean_w", [P, P])
        acc = m.psum("acc", [P, 8, BANK])

        consts_in = m.sem("consts_in")
        w_in = [m.sem(f"w_in{i}") for i in range(RING)]
        src_in = [m.sem(f"src_in{i}") for i in range(SLOTS)]
        w_hi_done = m.sem("w_hi_done")
        w_ready = m.sem("w_ready")
        w_used = m.sem("w_used")
        bank_ready = m.sem("bank_ready")
        bank_free = m.sem("bank_free")
        norm_done = m.sem("norm_done")
        src_hi_done = m.sem("src_hi_done")
        src_ready = m.sem("src_ready")
        bias_set = m.sem("bias_set")
        gelu_done = m.sem("gelu_done")
        centred = m.sem("centred")
        squared = m.sem("squared")
        summed = m.sem("summed")
        stored = m.sem("stored")
        zeroed = m.sem("zeroed")
        stats_mm = m.sem("stats_mm")
        stats_dve = m.sem("stats_dve")
        stats_std = m.sem("stats_std")
        stats_read = m.sem("stats_read")
        pool_set = m.sem("pool_set")
        ids_in = m.sem("ids_in")
        gathered = m.sem("gathered")

        block = ctx.enter_context(nc.Block())

        w_all = io["w_enc"]
        pre = scratch["pre"]
        used_before = lambda g, k: (w_used, 15 * g + k - 3) if k >= 4 else (
            (bank_ready, 8 * g) if k == 3 else (w_used, 15 * g + k - 2))

        @block.sync
        def _(sp):
            sp.dma_start(bias[:, :], io["b_enc"]).then_inc(consts_in, 16)
            sp.dma_start(ln_g[:, :], io["ln_g"]).then_inc(consts_in, 16)
            sp.dma_start(ln_b[:, :], io["ln_b"]).then_inc(consts_in, 16)

            def load(g, k):
                sp.dma_start(w_stage[:, k % RING, :], w_all[g, k]).then_inc(w_in[k % RING], 16)

            for k in range(RING):
                load(0, k)
            for k in range(RING, KT):
                sp.wait_ge(w_ready, k - RING + 1)
                load(0, k)
            with sp.Fori(1, GROUPS) as g:
                for k in range(KT):
                    sp.wait_ge(w_ready, 16 * g + k - RING + 1)
                    load(g, k)

        @block.gpsimd
        def _(pool):
            for k in range(SLOTS):
                pool.dma_start(src_stage[:, k, :], io["xT"][k]).then_inc(src_in[k], 16)
            nc.gpsimd.memset(mean_w[:, :], 1.0 / IN).then_inc(pool_set, 1)
            nc.gpsimd.memset(keep["ident"][:, :], 0.0).then_inc(pool_set, 1)
            pool.wait_ge(pool_set, 2)
            nc.gpsimd.affine_select(out=keep["ident"][:, :], in_=keep["ident"][:, :],
                                    compare_op=ALU.not_equal, fill=1.0, base=0,
                                    pattern=[[-1, P]], channel_multiplier=1).then_inc(pool_set, 1)
            for k in range(SLOTS, KT):
                pool.wait_ge(src_ready, k - SLOTS + 1)
                pool.dma_start(src_stage[:, k % SLOTS, :], io["xT"][k]).then_inc(src_in[k % SLOTS], 16)
            pool.dma_start(keep["ids"][:, :, :], io["ids"]).then_inc(ids_in, 16)
            pool.wait_ge(ids_in, 16)
            for i in range(NT):
                for c in range(CHUNKS):
                    pool.indirect_dma_start(
                        keep["strength"][:, (c * NT + i) * NT:(c * NT + i + 1) * NT], None, io[f"tbl_{i}"],
                        bass.IndirectOffsetOnAxis(ap=keep["ids"][:, c, i:i + 1], axis=0)).then_inc(gathered, 16)

            def store(g):
                for b in range(8):
                    pool.wait_ge(bank_free, 8 * g + 8 + b + 1)
                    pool.dma_start(pre[g, b // 2, :, (b % 2) * HALF:(b % 2 + 1) * HALF],
                                   out_stage[:, b, :]).then_inc(stored, 16)

            def load_h(e):
                for k in range(KT):
                    pool.wait_ge(src_ready, KT * (e + 1) + k - SLOTS + 1)
                    pool.dma_start(src_stage[:, k % SLOTS, :],
                                   pre[4 * e + k // 4, k % 4]).then_inc(src_in[k % SLOTS], 16)

            with pool.Fori(0, W1_GROUPS) as g:
                store(g)
            pool.wait_ge(stored, 16 * 8 * W1_GROUPS)
            pool.wait_ge(stats_dve, 10)
            load_h(0)
            with pool.Fori(TOP, TOP + 4) as g:
                store(g)
            load_h(1)
            with pool.Fori(TOP + 4, GROUPS) as g:
                store(g)
            pool.wait_ge(stored, 16 * 8 * GROUPS)
            pool.wait_ge(gathered, 16 * NT * CHUNKS)

        @block.scalar
        def _(act):
            act.sem_inc(bank_free, 8)
            act.wait_ge(consts_in, 48)

            def split_w(g, k):
                act.wait_ge(w_in[k % RING], 16 * (4 * g + k // RING + 1))
                act.activation(w_hi[:, k % RING, :], w_stage[:, k % RING, :],
                               ACT.Identity).then_inc(w_hi_done, 1)

            def split_w_later(g, k):
                act.wait_ge(*used_before(g, k))
                split_w(g, k)

            def split_src(s, k):
                act.activation(src_hi[:, k, :], src_stage[:, k % SLOTS, :], ACT.Identity).then_inc(src_hi_done, 1)

            def evacuate(g, with_stats):
                act.activation(group_bias[:, :], bias[:, bass.ds(g * GROUP, GROUP)], ACT.Copy).then_inc(bias_set, 1)
                act.wait_ge(bias_set, g + 1)
                for b in range(8):
                    act.wait_ge(bank_ready, 8 * g + b + 1)
                    if with_stats:
                        if not isinstance(g, int) or b >= 2:
                            act.wait_ge(summed, 16 * g + 2 * b - 3)
                        act.activation(square[:, b % 2, :], acc[:, b, :], ACT.Square,
                                       bias=group_bias[:, b // 2:b // 2 + 1]).then_inc(squared, 1)
                    if not isinstance(g, int) or g > 0:
                        act.wait_ge(stored, 128 * g)
                    act.activation(out_stage[:, b, :], acc[:, b, :], ACT.Identity,
                                   bias=group_bias[:, b // 2:b // 2 + 1]).then_inc(bank_free, 1)

            def make_h(e, k):
                act.wait_ge(norm_done, KT * e + k + 1)
                act.activation(src_stage[:, k % SLOTS, :], src_stage[:, k % SLOTS, :], ACT.Gelu,
                               scale=ln_g[:, e * KT + k:e * KT + k + 1],
                               bias=ln_b[:, e * KT + k:e * KT + k + 1]).then_inc(gelu_done, 1)
                act.wait_ge(gelu_done, KT * e + k + 1)
                if k < 15:
                    act.wait_ge(w_used, 15 * (8 + 4 * e) + k + 1)
                else:
                    act.wait_ge(bank_ready, 8 * (9 + 4 * e))
                split_src(e + 1, k)

            for k in range(KT):
                act.wait_ge(src_in[k % SLOTS], 16 * (k // SLOTS + 1))
                split_src(0, k)
                if k < RING:
                    split_w(0, k)
                else:
                    act.wait_ge(w_used, k - 3)
                    split_w(0, k)
            for k in range(EARLY):
                split_w_later(1, k)
            evacuate(0, True)
            with act.Fori(1, W1_GROUPS) as g:
                for k in range(EARLY, KT):
                    split_w_later(g, k)
                for k in range(EARLY):
                    split_w_later(g + 1, k)
                evacuate(g, True)
            act.wait_ge(summed, 16 * W1_GROUPS)
            for e in range(2):
                act.wait_ge(stats_dve, 4 * e + 4)
                act.activation(stats[:, e, 1, :], stats[:, e, 1, :], ACT.Sqrt).then_inc(stats_std, 1)
            for e in range(2):
                g = TOP + 4 * e
                for k in range(EARLY, KT):
                    split_w_later(g, k)
                    if k >= RING:
                        make_h(e, k - RING)
                for k in range(EARLY):
                    split_w_later(g + 1, k)
                    if k < 2:
                        make_h(e, KT - RING + k)
                evacuate(g, False)
                make_h(e, KT - 2)
                make_h(e, KT - 1)
                with act.Fori(g + 1, g + 4) as g:
                    for k in range(EARLY, KT):
                        split_w_later(g, k)
                    for k in range(EARLY):
                        split_w_later(g + 1, k)
                    evacuate(g, False)
            for k in range(EARLY, KT):
                split_w_later(GROUPS - 1, k)
            evacuate(GROUPS - 1, False)

        @block.vector
        def _(dve):
            def split_w(g, k):
                dve.wait_ge(w_hi_done, 16 * g + k + 1)
                dve.tensor_tensor(w_lo[:, k % RING, :], w_stage[:, k % RING, :],
                                  w_hi[:, k % RING, :].bitcast(F32), ALU.subtract).then_inc(w_ready, 1)

            def split_src(s, k):
                dve.wait_ge(src_hi_done, KT * s + k + 1)
                dve.tensor_tensor(src_lo[:, k, :], src_stage[:, k % SLOTS, :], src_hi[:, k, :].bitcast(F32),
                                  ALU.subtract).then_inc(src_ready, 1)

            def add_stats(g, e):
                for b in range(8):
                    half = slice((b % 2) * HALF, (b % 2 + 1) * HALF)
                    dve.wait_ge(squared, 8 * g + b + 1)
                    if not isinstance(g, int) or b >= 2:
                        dve.wait_ge(summed, 16 * g + 2 * b - 3)
                    dve.tensor_tensor(stats[:, e, 1, half], stats[:, e, 1, half], square[:, b % 2, :],
                                      ALU.add).then_inc(summed, 1)
                    dve.wait_ge(bank_free, 8 + 8 * g + b + 1)
                    if not isinstance(g, int) or b >= 2:
                        dve.wait_ge(summed, 16 * g + 2 * b - 2)
                    dve.tensor_tensor(stats[:, e, 0, half], stats[:, e, 0, half], out_stage[:, b, :],
                                      ALU.add).then_inc(summed, 1)

            def normalise(e, k):
                dve.wait_ge(src_in[k % SLOTS], 16 * (KT // SLOTS * (e + 1) + k // SLOTS + 1))
                dve.tensor_tensor(src_stage[:, k % SLOTS, :], src_stage[:, k % SLOTS, :], stats[:, e, 0, :],
                                  ALU.subtract).then_inc(centred, 1)
                dve.wait_ge(centred, KT * e + k + 1)
                dve.tensor_tensor(src_stage[:, k % SLOTS, :], src_stage[:, k % SLOTS, :], stats[:, e, 1, :],
                                  ALU.mult).then_inc(norm_done, 1)

            dve.memset(stats[:, :, :, :], 0.0).then_inc(zeroed, 1)
            for k in range(KT):
                split_src(0, k)
                split_w(0, k)
            for k in range(EARLY):
                split_w(1, k)
            dve.wait_ge(zeroed, 1)
            add_stats(0, 0)
            for e in range(2):
                with dve.Fori(max(4 * e, 1), 4 * e + 4) as g:
                    for k in range(EARLY, KT):
                        split_w(g, k)
                    for k in range(EARLY):
                        split_w(g + 1, k)
                    add_stats(g, e)
            for e in range(2):
                both = lambda i: acc[:, 4 * e + 2 * i:4 * e + 2 * i + 2, :].rearrange("p h n -> p (h n)")
                dve.wait_ge(stats_mm, 4 * e + 4)
                dve.tensor_copy(stats[:, e, 0, :], both(0)).then_inc(stats_dve, 1)
                dve.wait_ge(stats_dve, 4 * e + 1)
                dve.tensor_tensor(src_stage[:, e, :], stats[:, e, 0, :], stats[:, e, 0, :],
                                  ALU.mult).then_inc(stats_dve, 1)
                dve.wait_ge(stats_dve, 4 * e + 2)
                dve.tensor_tensor(stats[:, e, 1, :], both(1), src_stage[:, e, :],
                                  ALU.subtract).then_inc(stats_dve, 1)
                dve.wait_ge(stats_dve, 4 * e + 3)
                dve.tensor_scalar(stats[:, e, 1, :], stats[:, e, 1, :], 0.0, LN_EPS, ALU.max,
                                  ALU.add).then_inc(stats_dve, 1)
            for e in range(2):
                dve.wait_ge(stats_std, e + 1)
                dve.reciprocal(stats[:, e, 1, :], stats[:, e, 1, :]).then_inc(stats_dve, 1)
            dve.wait_ge(stats_dve, 10)

            for e in range(2):
                g = TOP + 4 * e
                def next_h(k):
                    if k < KT - 1:
                        normalise(e, k + 1)
                    split_src(e + 1, k)

                normalise(e, 0)
                for k in range(EARLY, KT):
                    split_w(g, k)
                    if k >= RING:
                        next_h(k - RING)
                for k in range(EARLY):
                    split_w(g + 1, k)
                    if k < 2:
                        next_h(KT - RING + k)
                next_h(KT - 2)
                next_h(KT - 1)
                with dve.Fori(g + 1, g + 4) as g:
                    for k in range(EARLY, KT):
                        split_w(g, k)
                    for k in range(EARLY):
                        split_w(g + 1, k)
            for k in range(EARLY, KT):
                split_w(GROUPS - 1, k)

        @block.tensor
        def _(pe):
            def gemm(g, source):
                for k in range(KT):
                    pe.wait_ge(w_ready, KT * g + k + 1)
                    pe.wait_ge(src_ready, KT * source + k + 1)
                    for mt in range(GROUP):
                        hi = w_hi[:, k % RING, mt * P:(mt + 1) * P]
                        lo = w_lo[:, k % RING, mt * P:(mt + 1) * P]
                        for h in range(2):
                            if k == 0:
                                pe.wait_ge(bank_free, 8 * g + 2 * mt + h + 1)
                            cols = slice(h * HALF, (h + 1) * HALF)
                            pe.matmul(acc[:, 2 * mt + h, :], hi, src_hi[:, k, cols], start=k == 0, stop=False)
                            pe.matmul(acc[:, 2 * mt + h, :], hi, src_lo[:, k, cols], start=False, stop=False)
                        for h in range(2):
                            cols = slice(h * HALF, (h + 1) * HALF)
                            last = pe.matmul(acc[:, 2 * mt + h, :], lo, src_hi[:, k, cols],
                                             start=False, stop=k == KT - 1)
                            if k == KT - 1:
                                last.then_inc(bank_ready, 1)
                    if k < KT - 1:
                        last.then_inc(w_used, 1)

            with pe.Fori(0, W1_GROUPS) as g:
                gemm(g, 0)
            pe.wait_ge(summed, 16 * W1_GROUPS)
            pe.wait_ge(bank_free, 8 * W1_GROUPS + 8)
            pe.wait_ge(pool_set, 1)
            for e in range(2):
                for i in range(2):
                    for h in range(2):
                        pe.matmul(acc[:, 4 * e + 2 * i + h, :], mean_w[:, :],
                                  stats[:, e, i, h * HALF:(h + 1) * HALF], start=True, stop=True
                                  ).then_inc(stats_mm, 1)
            pe.wait_ge(stats_dve, 7)
            gemm(TOP, 0)
            with pe.Fori(TOP + 1, TOP + 5) as g:
                gemm(g, 1)
            with pe.Fori(TOP + 5, GROUPS) as g:
                gemm(g, 2)


def attention(nc, io, scratch, keep):
    QR, QI, KR, KI, VR, VI = range(6)
    BLK = TOK // P
    SB = P // NT
    W_TILES = 6 * DK
    with ExitStack() as ctx:
        m = Mem(nc, ctx, "att_")
        stage = m.sb("stage", [P, 4, D])
        w_hi = m.sb("w_hi", [P, 6, DK, D], F32R)
        w_lo = m.sb("w_lo", [P, 6, DK, D], F32R)
        s_hi = m.sb("s_hi", [P, 2, DK, TOK], F32R)
        s_lo = m.sb("s_lo", [P, 2, DK, TOK], F32R)
        q1 = m.sb("q1", [P, 2, 2, TOK])
        q2 = m.sb("q2", [P, 2, 2, TOK])
        kk = m.sb("kk", [P, 2, 2, TOK])
        val = m.sb("val", [P, BLK, H, 2, HD])
        sq_r = m.sb("sq_r", [P, 2 * BLK, P])
        sq_i = m.sb("sq_i", [P, 2 * BLK, P])
        mask = m.sb("mask", [P, SB, NT])
        prob = m.sb("prob", [P, H, BLK, NT])
        peak = m.sb("peak", [P, H * BLK])
        total = m.sb("total", [P, H * BLK])
        wide = m.sb("wide", [P, H, P])
        wide_t = m.sb("wide_t", [P, H, P])
        out_st = m.sb("out_st", [P, 2, H, P])
        qk_bias = m.sb("qk_bias", [P, 4, DK])
        v_bias = m.sb("v_bias", [P, H])
        ps = m.psum("ps", [P, 8, BANK])

        w_bias_in = m.sem("w_bias_in")
        tile_in = [m.sem(f"tile_in{i}") for i in range(4)]
        hi_done = m.sem("hi_done")
        split_done = m.sem("split_done")
        gemm_ready = m.sem("gemm_ready")
        even_free = m.sem("even_free")
        odd_free = m.sem("odd_free")
        scores_done = m.sem("scores_done")
        score_free = m.sem("score_free")
        extracted = m.sem("extracted")
        chain = m.sem("chain")
        root_done = m.sem("root_done")
        shifted = m.sem("shifted")
        exp_done = m.sem("exp_done")
        prob_ready = m.sem("prob_ready")
        wide_ready = m.sem("wide_ready")
        turned = m.sem("turned")
        turned_out = m.sem("turned_out")
        mixed = m.sem("mixed")
        mixed_out = m.sem("mixed_out")
        stored = [m.sem(f"stored{i}") for i in range(2)]
        mask_set = m.sem("mask_set")

        block = ctx.enter_context(nc.Block())
        s_src = scratch["pre"]
        out = scratch["mixed"]

        def w_place(t):
            return t + DK if t < DK else t + 2 * DK

        def s_place(c, t):
            if isinstance(c, int) and c == 0:
                return t if t < DK else t + DK
            return None

        @block.sync
        def _(sp):
            sp.sem_inc(stored[0], 16)
            sp.sem_inc(stored[1], 16)
            sp.dma_start(qk_bias[:, :, :], io["b_qk"]).then_inc(w_bias_in, 16)
            sp.dma_start(v_bias[:, :], io["b_v"]).then_inc(w_bias_in, 16)

            def load_w(t):
                sp.wait_ge(split_done, w_place(t) - 3)
                sp.dma_start(stage[:, t % 4, :], io["w_qkv"][t]).then_inc(tile_in[t % 4], 16)

            def load(c, tiles):
                for t in tiles:
                    e, kt = t // DK, t % DK
                    if s_place(c, t) is None:
                        sp.wait_ge(split_done, W_TILES + 8 * c + t - 3)
                    elif s_place(c, t) >= 4:
                        sp.wait_ge(split_done, s_place(c, t) - 3)
                    src = s_src[9 + 4 * e:13 + 4 * e, kt, :, bass.ds(c * CB, CB)].rearrange("n p b -> p n b")
                    sp.dma_start(stage[:, t % 4, :].rearrange("p (n b) -> p n b", n=NT),
                                 src).then_inc(tile_in[t % 4], 16)

            def store(c, blk):
                sp.wait_ge(mixed_out, BLK * c + blk + 2)
                sp.dma_start(out[c, blk], out_st[:, blk % 2, :, :]).then_inc(stored[blk % 2], 16)

            load(0, range(DK))
            for t in range(DK):
                load_w(t)
            load(0, range(DK, 2 * DK))
            for t in range(DK, W_TILES):
                load_w(t)
            with sp.Fori(0, CHUNKS - 1) as c:
                load(c + 1, range(0, 6))
                store(c, 0)
                load(c + 1, range(6, 8))
                for blk in range(1, BLK):
                    store(c, blk)
            for blk in range(BLK):
                store(CHUNKS - 1, blk)
            for i in range(2):
                sp.wait_ge(stored[i], 16 * (1 + CHUNKS * BLK // 2))

        @block.gpsimd
        def _(pool):
            pool.sem_inc(wide_ready, 1)
            nc.gpsimd.memset(mask[:, :, :], 1.0).then_inc(mask_set, 1)
            pool.wait_ge(mask_set, 1)
            nc.gpsimd.affine_select(out=mask[:, :, :], in_=mask[:, :, :], compare_op=ALU.is_ge, fill=0.0,
                                    base=0, pattern=[[-NT, SB], [0, NT]], channel_multiplier=1).then_inc(mask_set, 1)
            pool.wait_ge(mask_set, 2)
            nc.gpsimd.affine_select(out=mask[:, :, :], in_=mask[:, :, :], compare_op=ALU.is_ge, fill=0.0,
                                    base=NT - 1, pattern=[[NT, SB], [0, NT]], channel_multiplier=-1
                                    ).then_inc(mask_set, 1)
            pool.wait_ge(mask_set, 3)
            with pool.Fori(0, CHUNKS) as c:
                for blk in range(BLK):
                    pool.wait_ge(prob_ready, c + 1)
                    pool.wait_ge(turned, BLK * c + blk + 1)
                    nc.gpsimd.tensor_tensor(
                        wide[:, :, :].rearrange("p h (b n) -> p h b n", n=NT),
                        prob[:, :, blk, :].unsqueeze(2).broadcast_to([P, H, SB, NT]),
                        mask[:, :, :].unsqueeze(1).broadcast_to([P, H, SB, NT]), ALU.mult).then_inc(wide_ready, 1)

        @block.scalar
        def _(act):
            act.sem_inc(odd_free, 2)
            act.sem_inc(turned_out, 1)
            act.wait_ge(w_bias_in, 32)

            def split_w(t):
                act.wait_ge(tile_in[t % 4], 16 * (w_place(t) // 4 + 1))
                act.activation(w_hi[:, t // DK, t % DK, :], stage[:, t % 4, :], ACT.Identity).then_inc(hi_done, 1)

            def split_s(c, t):
                if s_place(c, t) is None:
                    act.wait_ge(tile_in[t % 4], 16 * (W_TILES // 4 + 2 * c + t // 4 + 1))
                else:
                    act.wait_ge(tile_in[t % 4], 16 * (s_place(c, t) // 4 + 1))
                act.activation(s_hi[:, t // DK, t % DK, :].rearrange("p (b n) -> p b n", n=NT),
                               stage[:, t % 4, :].rearrange("p (n b) -> p b n", n=NT),
                               ACT.Identity).then_inc(hi_done, 1)

            def evacuate(c, mt):
                act.wait_ge(gemm_ready, 24 * c + 4 * mt + 2)
                act.wait_ge(scores_done, 4 * c + mt + 1)
                slot = mt % 2
                for h in range(2):
                    rows = slice(h * HD, (h + 1) * HD)
                    b = qk_bias[rows, QI, mt:mt + 1]
                    act.activation(q1[HD:P, slot, h, :], ps[rows, QI, :], ACT.Identity, bias=b)
                for h in range(2):
                    rows = slice(h * HD, (h + 1) * HD)
                    b = qk_bias[rows, QI, mt:mt + 1]
                    last = act.activation(q2[0:HD, slot, h, :], ps[rows, QI, :], ACT.Identity, bias=b)
                last.then_inc(odd_free, 1)
                act.wait_ge(gemm_ready, 24 * c + 4 * mt + 4)
                for h in range(2):
                    rows = slice(h * HD, (h + 1) * HD)
                    last = act.activation(kk[HD:P, slot, h, :], ps[rows, KI, :], ACT.Identity,
                                          bias=qk_bias[rows, KI, mt:mt + 1])
                last.then_inc(odd_free, 1)

            def square(c, mt):
                act.wait_ge(scores_done, 4 * c + mt + 3)
                act.wait_ge(extracted, 4 * c + mt + 1)
                act.activation(sq_r[:, :, :], ps[:, 4:6, :].rearrange("p a (k n) -> p (a k) n", k=BLK), ACT.Square)
                act.activation(sq_i[:, :, :], ps[:, 6:8, :].rearrange("p a (k n) -> p (a k) n", k=BLK),
                               ACT.Square).then_inc(score_free, 1)

            def evacuate_v(c, blk):
                act.wait_ge(gemm_ready, 24 * c + 16 + 2 * blk + 2)
                act.activation(val[:, blk, :, 1, :],
                               ps[:, (2 * blk + 1) % 4, :].rearrange("p (h d) -> p h d", h=H),
                               ACT.Copy).then_inc(odd_free, 1)

            def chunk(c, last_chunk):
                evacuate(c, 0)
                if s_place(c, 0) is not None:
                    for t in range(4 * DK, W_TILES):
                        split_w(t)
                for mt in range(1, 4):
                    evacuate(c, mt)
                    square(c, mt - 1)
                act.wait_ge(mixed, BLK * c + 1)
                evacuate_v(c, 0)
                square(c, 3)
                act.wait_ge(shifted, 2 * c + 1)
                act.activation(prob[:, :, :, :], prob[:, :, :, :], ACT.Sqrt).then_inc(root_done, 1)
                evacuate_v(c, 1)
                act.wait_ge(shifted, 2 * c + 2)
                act.activation(prob[:, :, :, :], prob[:, :, :, :], ACT.Exp, scale=HD ** -0.5).then_inc(exp_done, 1)
                evacuate_v(c, 2)
                evacuate_v(c, 3)
                for blk in range(BLK):
                    act.wait_ge(turned, BLK * c + blk + 2)
                    act.wait_ge(mixed, BLK * c + blk + 1)
                    act.activation(wide_t[:, :, :], ps[:, 4:6, :].rearrange("p a (h n) -> p (a h) n", n=P),
                                   ACT.Copy).then_inc(turned_out, 1)
                    if not last_chunk:
                        for t in range(2 * blk, 2 * blk + 2):
                            split_s(c + 1, t)

            for t in range(DK):
                split_s(0, t)
            for t in range(DK):
                split_w(t)
            for t in range(DK, 2 * DK):
                split_s(0, t)
            for t in range(DK, 4 * DK):
                split_w(t)
            chunk(0, False)
            with act.Fori(1, CHUNKS - 1) as c:
                chunk(c, False)
            chunk(CHUNKS - 1, True)

        @block.vector
        def _(dve):
            dve.sem_inc(even_free, 2)
            dve.sem_inc(extracted, 1)
            dve.sem_inc(mixed_out, 1)
            dve.wait_ge(w_bias_in, 32)
            dve.wait_ge(mask_set, 3)

            def split_w(t):
                dve.wait_ge(hi_done, w_place(t) + 1)
                dve.tensor_tensor(w_lo[:, t // DK, t % DK, :], stage[:, t % 4, :],
                                  w_hi[:, t // DK, t % DK, :].bitcast(F32), ALU.subtract).then_inc(split_done, 1)

            def split_s(c, t):
                if s_place(c, t) is None:
                    dve.wait_ge(hi_done, W_TILES + 8 * c + t + 1)
                else:
                    dve.wait_ge(hi_done, s_place(c, t) + 1)
                dve.tensor_tensor(s_lo[:, t // DK, t % DK, :].rearrange("p (b n) -> p b n", n=NT),
                                  stage[:, t % 4, :].rearrange("p (n b) -> p b n", n=NT),
                                  s_hi[:, t // DK, t % DK, :].bitcast(F32).rearrange("p (b n) -> p b n", n=NT),
                                  ALU.subtract).then_inc(split_done, 1)

            def evacuate(c, mt):
                dve.wait_ge(gemm_ready, 24 * c + 4 * mt + 1)
                dve.wait_ge(scores_done, 4 * c + mt + 1)
                slot = mt % 2
                for h in range(2):
                    rows = slice(h * HD, (h + 1) * HD)
                    dve.tensor_scalar(q1[0:HD, slot, h, :], ps[rows, QR, :], qk_bias[rows, QR, mt:mt + 1],
                                      None, ALU.add)
                for h in range(2):
                    rows = slice(h * HD, (h + 1) * HD)
                    last = dve.tensor_scalar(q2[HD:P, slot, h, :], ps[rows, QR, :], qk_bias[rows, QR, mt:mt + 1],
                                             -1.0, ALU.add, ALU.mult)
                last.then_inc(even_free, 1)
                dve.wait_ge(gemm_ready, 24 * c + 4 * mt + 3)
                for h in range(2):
                    rows = slice(h * HD, (h + 1) * HD)
                    last = dve.tensor_scalar(kk[0:HD, slot, h, :], ps[rows, KR, :], qk_bias[rows, KR, mt:mt + 1],
                                             None, ALU.add)
                last.then_inc(even_free, 1)

            def extract(c, mt):
                dve.wait_ge(score_free, 4 * c + mt + 1)
                dve.tensor_tensor(sq_r[:, :, :], sq_r[:, :, :], sq_i[:, :, :], ALU.add).then_inc(chain, 1)
                dve.wait_ge(chain, 11 * c + 2 * mt + 1)
                dve.tensor_tensor(sq_r[:, :, :], sq_r[:, :, :],
                                  mask[:, :, :].rearrange("p b n -> p (b n)").unsqueeze(1).broadcast_to(
                                      [P, 2 * BLK, P]), ALU.mult).then_inc(chain, 1)
                dve.wait_ge(chain, 11 * c + 2 * mt + 2)
                if mt == 0:
                    dve.wait_ge(wide_ready, BLK * c + 1)
                dve.tensor_reduce(prob[:, 2 * mt:2 * mt + 2, :, :].rearrange("p h k n -> p (h k) n"),
                                  sq_r[:, :, :].rearrange("p x (b n) -> p x n b", n=NT),
                                  AX_X, ALU.add).then_inc(extracted, 1)

            def evacuate_v(c, blk):
                dve.wait_ge(gemm_ready, 24 * c + 16 + 2 * blk + 1)
                dve.tensor_copy(val[:, blk, :, 0, :],
                                ps[:, (2 * blk) % 4, :].rearrange("p (h d) -> p h d", h=H)).then_inc(even_free, 1)

            def chunk(c, last_chunk):
                flat = prob[:, :, :, :].rearrange("p h k n -> p (h k) n")
                wide_peak = peak[:, :].unsqueeze(2).broadcast_to([P, H * BLK, NT])
                wide_total = total[:, :].unsqueeze(2).broadcast_to([P, H * BLK, NT])
                evacuate(c, 0)
                if s_place(c, 0) is not None:
                    for t in range(4 * DK, W_TILES):
                        split_w(t)
                for mt in range(1, 4):
                    evacuate(c, mt)
                    extract(c, mt - 1)
                dve.wait_ge(mixed, BLK * c + 1)
                evacuate_v(c, 0)
                extract(c, 3)
                dve.wait_ge(extracted, 4 * c + 5)
                dve.tensor_scalar(flat, flat, EPS, None, ALU.add).then_inc(shifted, 1)
                evacuate_v(c, 1)
                dve.wait_ge(root_done, c + 1)
                dve.tensor_reduce(peak[:, :], flat, AX_X, ALU.max).then_inc(chain, 1)
                dve.wait_ge(chain, 11 * c + 9)
                dve.tensor_tensor(flat, flat, wide_peak, ALU.subtract).then_inc(shifted, 1)
                evacuate_v(c, 2)
                dve.wait_ge(exp_done, c + 1)
                dve.tensor_reduce(total[:, :], flat, AX_X, ALU.add).then_inc(chain, 1)
                dve.wait_ge(chain, 11 * c + 10)
                dve.reciprocal(total[:, :], total[:, :]).then_inc(chain, 1)
                dve.wait_ge(chain, 11 * c + 11)
                dve.tensor_tensor(flat, flat, wide_total, ALU.mult).then_inc(prob_ready, 1)
                evacuate_v(c, 3)
                for blk in range(BLK):
                    if not last_chunk:
                        for t in range(2 * blk, 2 * blk + 2):
                            split_s(c + 1, t)
                    dve.wait_ge(mixed, BLK * c + blk + 2)
                    dve.wait_ge(stored[blk % 2], 16 * (2 * c + blk // 2 + 1))
                    dve.tensor_tensor(out_st[:, blk % 2, :, :], ps[:, 6:8, :].rearrange("p a (h n) -> p (a h) n", n=P),
                                      v_bias[:, :].unsqueeze(2).broadcast_to([P, H, P]),
                                      ALU.add).then_inc(mixed_out, 1)

            for t in range(DK):
                split_s(0, t)
            for t in range(DK):
                split_w(t)
            for t in range(DK, 2 * DK):
                split_s(0, t)
            for t in range(DK, 4 * DK):
                split_w(t)
            chunk(0, False)
            with dve.Fori(1, CHUNKS - 1) as c:
                chunk(c, False)
            chunk(CHUNKS - 1, True)

        @block.tensor
        def _(pe):
            pe.sem_inc(scores_done, 2)
            pe.sem_inc(turned, 1)
            pe.sem_inc(mixed, 1)

            def bank_wait(c, i):
                pe.wait_ge(odd_free if i % 2 else even_free, 12 * c + i // 2 + 1)

            def project(c, mt):
                for j in (QR, QI, KR, KI):
                    bank_wait(c, 4 * mt + j)
                    e = j % 2
                    for kt in range(DK):
                        if mt == 0 and s_place(c, 0) is None:
                            pe.wait_ge(split_done, W_TILES + 8 * c + DK * e + kt + 1)
                        elif mt == 0:
                            pe.wait_ge(split_done, w_place(DK * j + kt) + 1)
                        hi = w_hi[:, j, kt, mt * P:(mt + 1) * P]
                        lo = w_lo[:, j, kt, mt * P:(mt + 1) * P]
                        pe.matmul(ps[:, j, :], hi, s_hi[:, e, kt, :], start=kt == 0, stop=False)
                        pe.matmul(ps[:, j, :], hi, s_lo[:, e, kt, :], start=False, stop=False)
                        last = pe.matmul(ps[:, j, :], lo, s_hi[:, e, kt, :], start=False, stop=kt == DK - 1)
                    last.then_inc(gemm_ready, 1)

            def values(c, blk):
                for e in range(2):
                    i = 2 * blk + e
                    bank_wait(c, 16 + i)
                    cols = slice(blk * P, (blk + 1) * P)
                    for kt in range(DK):
                        if blk == 0 and s_place(c, 0) is not None:
                            pe.wait_ge(split_done, w_place(DK * (VR + e) + kt) + 1)
                        hi, lo = s_hi[:, e, kt, cols], s_lo[:, e, kt, cols]
                        pe.matmul(ps[:, i % 4, :], hi, w_hi[:, VR + e, kt, :], start=kt == 0, stop=False)
                        pe.matmul(ps[:, i % 4, :], hi, w_lo[:, VR + e, kt, :], start=False, stop=False)
                        last = pe.matmul(ps[:, i % 4, :], lo, w_hi[:, VR + e, kt, :], start=False,
                                         stop=kt == DK - 1)
                    last.then_inc(gemm_ready, 1)

            def scores(c, mt):
                pe.wait_ge(even_free, 12 * c + 2 * mt + 4)
                pe.wait_ge(odd_free, 12 * c + 2 * mt + 4)
                if mt == 0:
                    pe.wait_ge(turned_out, BLK * c + 1)
                    pe.wait_ge(mixed_out, BLK * c + 1)
                else:
                    pe.wait_ge(score_free, 4 * c + mt)
                slot = mt % 2
                for h in range(2):
                    for blk in range(BLK):
                        cols = slice(blk * P, (blk + 1) * P)
                        pe.matmul(ps[:, 4 + h, cols], q1[:, slot, h, cols], kk[:, slot, h, cols],
                                  start=True, stop=True)
                        last = pe.matmul(ps[:, 6 + h, cols], q2[:, slot, h, cols], kk[:, slot, h, cols],
                                         start=True, stop=True)
                last.then_inc(scores_done, 1)

            def turn(c, blk):
                pe.wait_ge(wide_ready, BLK * c + blk + 2)
                if blk == 0:
                    pe.wait_ge(score_free, 4 * c + 4)
                else:
                    pe.wait_ge(turned_out, BLK * c + blk + 1)
                for h in range(H):
                    last = pe.transpose(ps[:, 4 + h // 4, (h % 4) * P:(h % 4 + 1) * P], wide[:, h, :],
                                        keep["ident"][:, :])
                last.then_inc(turned, 1)

            def mix(c, blk):
                pe.wait_ge(turned_out, BLK * c + blk + 2)
                if blk == 0:
                    pe.wait_ge(even_free, 12 * c + 14)
                    pe.wait_ge(odd_free, 12 * c + 14)
                else:
                    pe.wait_ge(mixed_out, BLK * c + blk + 1)
                for h in range(H):
                    last = pe.matmul(ps[:, 6 + h // 4, (h % 4) * P:(h % 4 + 1) * P],
                                     val[:, blk, h, :, :].rearrange("p r d -> p (r d)"), wide_t[:, h, :],
                                     start=True, stop=True)
                last.then_inc(mixed, 1)

            def chunk(c):
                project(c, 0)
                for mt in range(1, 4):
                    project(c, mt)
                    scores(c, mt - 1)
                values(c, 0)
                scores(c, 3)
                for blk in range(1, BLK):
                    values(c, blk)
                turn(c, 0)
                for blk in range(1, BLK):
                    turn(c, blk)
                    mix(c, blk - 1)
                mix(c, BLK - 1)

            chunk(0)
            with pe.Fori(1, CHUNKS) as c:
                chunk(c)


def out_proj(nc, io, scratch, keep, int_w):
    AHEAD = 6
    with ExitStack() as ctx:
        m = Mem(nc, ctx, "out_")
        stage = m.sb("stage", [P, 2, DK, TOK])
        w_hi = m.sb("w_hi", [P, 2, DK, D], F32R)
        w_lo = m.sb("w_lo", [P, 2, DK, D], F32R)
        x_hi = m.sb("x_hi", [P, 2, DK, TOK], F32R)
        x_lo = m.sb("x_lo", [P, 2, DK, TOK], F32R)
        out_st = m.sb("out_st", [P, 2, NT, DK, CB])
        int_stage = m.sb("int_stage", [P, 2, 2, D])
        bias = m.sb("bias", [P, 2, DK])
        ps = m.psum("ps", [P, 8, BANK])
        bias_in = m.sem("bias_in")
        tile_in = [m.sem(f"tile_in{i}") for i in range(2)]
        w_in = [m.sem(f"w_in{i}") for i in range(2)]
        hi_done = m.sem("hi_done")
        split_done = m.sem("split_done")
        ready = m.sem("ready")
        free = m.sem("free")
        stored = [m.sem(f"stored{i}") for i in range(2)]
        int_in = [m.sem(f"int_in{i}") for i in range(2)]
        int_hi = m.sem("int_hi")
        int_split = m.sem("int_split")
        block = ctx.enter_context(nc.Block())
        src, dst = scratch["mixed"], scratch["attn"]
        w_stage = lambda r: out_st[:, r, :, :, :].rearrange("p n k b -> p n (k b)")

        def place(c, r):
            return 2 * (r + 1) if isinstance(c, int) and c == 0 else 2 * c + r + 3

        @block.sync
        def _(sp):
            sp.dma_start(bias[:, :, :], io["b_o"]).then_inc(bias_in, 16)

            def load(c):
                for r in range(2):
                    if isinstance(c, int) and c == 0:
                        sp.dma_start(w_stage(r), io["w_o"][r]).then_inc(w_in[r], 16)
                    else:
                        sp.wait_ge(split_done, 2 * c + r + 1)
                    for odd in range(2):
                        for blk in range(NT):
                            sp.dma_start(stage[odd * HD:(odd + 1) * HD, r, :, blk * P:(blk + 1) * P],
                                         src[c, blk, r * HD:(r + 1) * HD, odd::2, :]).then_inc(tile_in[r], 16)

            def store(c):
                for r in range(2):
                    sp.wait_ge(free, 8 * c + 4 * r + 12)
                    sp.dma_start(dst[c, r].rearrange("n p x -> p n x"),
                                 out_st[:, r, :, :, :].rearrange("p n k b -> p n (k b)")).then_inc(stored[r], 16)

            sp.sem_inc(stored[0], 16)
            sp.sem_inc(stored[1], 16)
            load(0)
            with sp.Fori(0, AHEAD) as c:
                for i in range(2):
                    sp.wait_ge(int_split, 2 * c + i + 1)
                    sp.dma_start(int_stage[:, i, :, :], io["w_int"][2 * c + i]).then_inc(int_in[i], 16)
                load(c + 1)
                store(c)
            for c in range(AHEAD, CHUNKS - 1):
                load(c + 1)
                store(c)
            store(CHUNKS - 1)
            for r in range(2):
                sp.wait_ge(stored[r], 16 * (CHUNKS + 1))

        @block.scalar
        def _(act):
            act.sem_inc(free, 8)
            act.wait_ge(bias_in, 16)

            def split_x(c, r):
                act.wait_ge(tile_in[r], 128 * (c + 1))
                act.activation(x_hi[:, r, :, :], stage[:, r, :, :], ACT.Identity).then_inc(hi_done, 1)

            def evacuate(c, r):
                act.wait_ge(stored[r], 16 * (c + 1))
                for mt in range(DK):
                    act.wait_ge(ready, 8 * c + 4 * r + mt + 1)
                    act.activation(out_st[:, r, :, mt, :],
                                   ps[:, 4 * r + mt, :].rearrange("p (b n) -> p n b", n=NT),
                                   ACT.Identity, bias=bias[:, r, mt:mt + 1]).then_inc(free, 1)

            for r in range(2):
                act.wait_ge(w_in[r], 16)
                act.activation(w_hi[:, r, :, :], w_stage(r), ACT.Identity).then_inc(hi_done, 1)
                split_x(0, r)
            with act.Fori(0, CHUNKS - 1) as c:
                for r in range(2):
                    evacuate(c, r)
                    split_x(c + 1, r)
            for r in range(2):
                evacuate(CHUNKS - 1, r)

        @block.vector
        def _(dve):
            def split_x(c, r):
                dve.wait_ge(hi_done, place(c, r))
                dve.tensor_tensor(x_lo[:, r, :, :], stage[:, r, :, :], x_hi[:, r, :, :].bitcast(F32),
                                  ALU.subtract).then_inc(split_done, 1)

            def split_int(c, i):
                tile = (slice(None), bass.ds(2 * c + i, 1), slice(None), slice(None))
                staged = int_stage[:, i:i + 1, :, :]
                dve.wait_ge(int_in[i], 16 * c + 16)
                dve.tensor_scalar(int_w["hi"][tile], staged, 1.0, None, ALU.mult).then_inc(int_hi, 1)
                dve.wait_ge(int_hi, 2 * c + i + 1)
                dve.tensor_tensor(int_w["lo"][tile], staged, int_w["hi"][tile].bitcast(F32),
                                  ALU.subtract).then_inc(int_split, 1)

            dve.sem_inc(int_split, 2)
            for r in range(2):
                dve.wait_ge(hi_done, place(0, r) - 1)
                dve.tensor_tensor(w_lo[:, r, :, :], w_stage(r), w_hi[:, r, :, :].bitcast(F32),
                                  ALU.subtract).then_inc(split_done, 1)
                split_x(0, r)
            for r in range(2):
                split_int(0, r)
            with dve.Fori(1, AHEAD) as c:
                for r in range(2):
                    split_x(c, r)
                    split_int(c, r)
            for c in range(AHEAD, CHUNKS):
                for r in range(2):
                    split_x(c, r)

        @block.tensor
        def _(pe):
            def chunk(c):
                for r in range(2):
                    pe.wait_ge(split_done, place(c, r))
                    for mt in range(DK):
                        pe.wait_ge(free, 8 * c + 4 * r + mt + 1)
                        for kt in range(DK):
                            hi = w_hi[:, r, kt, mt * P:(mt + 1) * P]
                            lo = w_lo[:, r, kt, mt * P:(mt + 1) * P]
                            pe.matmul(ps[:, 4 * r + mt, :], hi, x_hi[:, r, kt, :], start=kt == 0, stop=False)
                            pe.matmul(ps[:, 4 * r + mt, :], hi, x_lo[:, r, kt, :], start=False, stop=False)
                            last = pe.matmul(ps[:, 4 * r + mt, :], lo, x_hi[:, r, kt, :], start=False,
                                             stop=kt == DK - 1)
                        last.then_inc(ready, 1)

            chunk(0)
            with pe.Fori(1, CHUNKS) as c:
                chunk(c)


def interference(nc, io, scratch, keep, int_w):
    RE, IM, NEG = range(3)
    PAIRS = [(0, 1), (0, 2), (1, 2), (0, 3), (1, 3), (2, 3)]
    ON_POOL = 3
    N_PAIRS = len(PAIRS)
    W_LOADS = 4
    TINY = 1e-36
    ZERO_MAG = 1.01e-18
    with ExitStack() as ctx:
        m = Mem(nc, ctx, "int_")
        stage = m.sb("stage", [P, 2, 2, D])
        a_hi = m.sb("a_hi", [P, 2, 3, D], F32R)
        a_lo = m.sb("a_lo", [P, 2, 3, D], F32R)
        unit = m.sb("unit", [P, 2, NT, D])
        mag = m.sb("mag", [P, NT, D])
        inv = m.sb("inv", [P, NT, D])
        is_zero = m.sb("is_zero", [P, NT, D], BF16)
        s_now = m.sb("s_now", [P, NT, NT])
        prod = m.sb("prod", [P, 2, D])
        sup = m.sb("sup", [P, 2, D])
        norm = m.sb("norm", [P, 1])
        tiny = m.sb("tiny", [P, 1])
        ps = m.psum("ps", [P, 8, BANK])
        slot = lambda p: sup if p % 2 else prod
        with ExitStack() as token_3:
            w = Mem(nc, token_3, "int_")
            w3_hi = w.sb("w3_hi", [P, W_LOADS, 2, D], F32R)
            w3_lo = w.sb("w3_lo", [P, W_LOADS, 2, D], F32R)
        HALF, HC = B // 2, CHUNKS // 2
        M_TILES = DK // 2
        as_tiles = lambda t: t.rearrange("p a b n -> p (a b) n")
        x_of = lambda part, comp: as_tiles(int_w[part][:, 2 * comp:2 * comp + 2, :, :])
        m_of = lambda part, t: int_w[part][:, 6 + t, :, :]
        half_sup = m.sb("half_sup", [P, HC, 2, D])
        amp = m.sb("amp", [P, DK, HALF])
        im_sq = m.sb("im_sq", [P, 2, HALF])

        tile_in = [m.sem(f"tile_in{i}") for i in range(2)]
        hi_done = m.sem("hi_done")
        w_split = m.sem("w_split")
        a_split = m.sem("a_split")
        neg_done = m.sem("neg_done")
        ready = m.sem("ready")
        free = m.sem("free")
        tiny_set = m.sem("tiny_set")
        squares = m.sem("squares")
        sq_sum = m.sem("sq_sum")
        rooted = m.sem("rooted")
        strength_set = m.sem("strength_set")
        inverted = m.sem("inverted")
        flagged = m.sem("flagged")
        units = m.sem("units")
        multiplied = m.sem("multiplied")
        dot_sum = m.sem("dot_sum")
        pool_step = m.sem("pool_step")
        cosine = m.sem("cosine")
        begun = m.sem("begun")
        weighted = m.sem("weighted")
        w_scaled = m.sem("w_scaled")
        applied = m.sem("applied")
        sup_sum = m.sem("sup_sum")
        norm_sum = m.sem("norm_sum")
        norm_root = m.sem("norm_root")
        norm_inv = m.sem("norm_inv")
        sup_scaled = m.sem("sup_scaled")
        stored = m.sem("stored")
        half_in = m.sem("half_in")
        meas_hi = m.sem("meas_hi")
        meas_split = m.sem("meas_split")
        turned = m.sem("turned")
        x_hi_done = m.sem("x_hi_done")
        x_split = m.sem("x_split")
        x_neg = m.sem("x_neg")
        measured = m.sem("measured")
        meas_sq = m.sem("meas_sq")
        amp_sq = m.sem("amp_sq")
        amp_stored = m.sem("amp_stored")
        block = ctx.enter_context(nc.Block())
        src, dst = scratch["attn"], scratch["sup"]
        strength = keep["strength"]

        def terms(p):
            return [(a, b, all(b not in q for q in PAIRS[:p])) for a, b in (PAIRS[p], PAIRS[p][::-1])]

        def before(p):
            new = sum(first for q in range(p) for _, _, first in terms(q))
            return new, 2 * p - new

        TERMS = before(N_PAIRS)[1]
        ahead = lambda s: [(s + 1, 1), (s + 1, 2), (s + 1, 3), (s + 2, 0)]

        def staged(c, n):
            early = isinstance(c, int) and NT * c + n < 2
            return NT * c + n + 1 + (0 if early else W_LOADS)

        @block.sync
        def _(sp):
            sp.sem_inc(stored, 16)

            def load(c, n):
                sp.dma_start(stage[:, n % 2, :, :], src[c, :, n].rearrange("r p x -> p r x")
                             ).then_inc(tile_in[n % 2], 16)

            def store(c):
                sp.wait_ge(sup_scaled, c + 1)
                sp.dma_start(dst[c], sup[:, :, :]).then_inc(stored, 16)

            load(0, 0)
            load(0, 1)
            for t in range(W_LOADS):
                if t < 2:
                    sp.wait_ge(neg_done, t + 1)
                else:
                    sp.wait_ge(w_split, t - 1)
                sp.dma_start(stage[:, t % 2, :, :], io["w_int"][12 + t]).then_inc(tile_in[t % 2], 16)
            for n in range(2, NT + 1):
                if n < 4:
                    sp.wait_ge(w_split, n + 1)
                else:
                    sp.wait_ge(neg_done, n - 1)
                load(n // NT, n % NT)

            def chunk(s, loads):
                for c, n in loads:
                    sp.wait_ge(neg_done, NT * c + n - 1)
                    load(c, n)
                store(s)

            with sp.Fori(0, CHUNKS - 2) as s:
                chunk(s, ahead(s))
            chunk(CHUNKS - 2, ahead(CHUNKS - 2)[:3])
            for t in range(2 * M_TILES):
                if t < 2:
                    sp.wait_ge(neg_done, NT * CHUNKS)
                else:
                    sp.wait_ge(meas_split, t - 1)
                sp.dma_start(stage[:, t % 2, :, :], io["w_head"][t]).then_inc(tile_in[t % 2], 16)
                if t == 1:
                    sp.wait_ge(ready, NT * CHUNKS)
                    sp.wait_ge(stored, 16 * CHUNKS)
                    for c in range(HC):
                        sp.dma_start(half_sup[:, c, :, :], dst[c]).then_inc(half_in, 16)
            store(CHUNKS - 1)
            for mt in range(DK):
                sp.wait_ge(amp_sq, mt + 1)
                sp.dma_start(scratch["amp"][mt], amp[:, mt, :]).then_inc(amp_stored, 16)
            sp.wait_ge(stored, 16 * (CHUNKS + 1))
            sp.wait_ge(amp_stored, 16 * DK)

        @block.gpsimd
        def _(pool):
            nc.gpsimd.memset(tiny[:, :], TINY).then_inc(tiny_set, 1)

            def split_attn(c, n):
                pool.wait_ge(hi_done, staged(c, n))
                nc.gpsimd.tensor_tensor(a_lo[:, n % 2, 0:2, :], stage[:, n % 2, :, :],
                                        a_hi[:, n % 2, 0:2, :].bitcast(F32), ALU.subtract).then_inc(a_split, 1)

            def add_squares(c, n):
                pool.wait_ge(squares, NT * c + n + 1)
                nc.gpsimd.tensor_tensor(mag[:, n, :], mag[:, n, :], prod[:, n % 2, :], ALU.add).then_inc(sq_sum, 1)

            def split_meas(t):
                pool.wait_ge(meas_hi, t + 1)
                nc.gpsimd.tensor_tensor(m_of("lo", t), stage[:, t % 2, :, :], m_of("hi", t).bitcast(F32),
                                        ALU.subtract).then_inc(meas_split, 1)

            def finish_pair(c, p):
                i, j = PAIRS[p]
                f = slot(p)[:, 0, :]
                steps = 2 * ON_POOL + N_PAIRS - ON_POOL
                done = 2 * p if p < ON_POOL else ON_POOL + p
                if p < ON_POOL:
                    pool.wait_ge(multiplied, N_PAIRS * c + p + 1)
                    nc.gpsimd.tensor_tensor(f, f, slot(p)[:, 1, :], ALU.add).then_inc(pool_step, 1)
                    done += 1
                    pool.wait_ge(pool_step, steps * c + done)
                else:
                    pool.wait_ge(dot_sum, (N_PAIRS - ON_POOL) * c + p - ON_POOL + 1)
                pool.wait_ge(flagged, NT * c + j + 1)
                nc.gpsimd.tensor_tensor(f, f, is_zero[:, i, :], ALU.add).then_inc(pool_step, 1)
                pool.wait_ge(pool_step, steps * c + done + 1)
                nc.gpsimd.tensor_tensor(f, f, is_zero[:, j, :], ALU.add).then_inc(cosine, 1)

            def chunk(s, splits, next_too):
                add_squares(s, 2)
                add_squares(s, 3)
                for c, n in splits[:1]:
                    split_attn(c, n)
                if not next_too:
                    split_meas(0)
                    split_meas(1)
                finish_pair(s, 0)
                finish_pair(s, 1)
                finish_pair(s, 2)
                for c, n in splits[1:2]:
                    split_attn(c, n)
                if not next_too:
                    split_meas(2)
                    split_meas(3)
                for p in range(3, N_PAIRS):
                    finish_pair(s, p)
                for c, n in splits[2:]:
                    split_attn(c, n)
                if next_too:
                    add_squares(s + 1, 0)
                    add_squares(s + 1, 1)

            for n in range(NT + 1):
                split_attn(n // NT, n % NT)
            add_squares(0, 0)
            add_squares(0, 1)
            with pool.Fori(0, CHUNKS - 2) as s:
                chunk(s, ahead(s), True)
            chunk(CHUNKS - 2, ahead(CHUNKS - 2)[:3], True)
            chunk(CHUNKS - 1, [], False)

        @block.scalar
        def _(act):
            act.sem_inc(free, NT)

            def split_attn(c, n):
                early = isinstance(c, int) and NT * c + n < 2
                act.wait_ge(tile_in[n % 2], 16 * (2 * c + n // 2 + 1 + (0 if early else W_LOADS // 2)))
                if not early:
                    act.wait_ge(ready, NT * c + n - 1)
                act.activation(a_hi[:, n % 2, 0:2, :], stage[:, n % 2, :, :], ACT.Identity).then_inc(hi_done, 1)
                act.activation(a_hi[:, n % 2, NEG, :], stage[:, n % 2, IM, :], ACT.Identity, scale=-1.0)
                act.wait_ge(a_split, NT * c + n + 1)
                act.activation(a_lo[:, n % 2, NEG, :], a_lo[:, n % 2, IM, :].bitcast(F32), ACT.Identity,
                               scale=-1.0).then_inc(neg_done, 1)

            def square(c, n):
                act.wait_ge(ready, NT * c + n + 1)
                act.wait_ge(w_scaled, 3 * c + (2 if n < 2 else 3))
                if not isinstance(c, int) or c > 0 or n >= 2:
                    act.wait_ge(sq_sum, NT * c + n - 1)
                act.activation(mag[:, n, :], ps[:, 2 * n, :], ACT.Square)
                act.activation(prod[:, n % 2, :], ps[:, 2 * n + 1, :], ACT.Square).then_inc(squares, 1)

            def root(c, n):
                act.wait_ge(sq_sum, NT * c + n + 1)
                act.activation(mag[:, n, :], mag[:, n, :], ACT.Sqrt, bias=tiny[:, 0:1]).then_inc(rooted, 1)

            def copy(c, n):
                act.wait_ge(sup_sum, 3 * c + max(n, 1))
                act.activation(unit[:, :, n, :], ps[:, 2 * n:2 * n + 2, :], ACT.Copy).then_inc(free, 1)

            def split_meas(t):
                act.wait_ge(tile_in[t % 2], 16 * ((NT * CHUNKS + W_LOADS) // 2 + t // 2 + 1))
                act.wait_ge(ready, NT * CHUNKS)
                act.activation(m_of("hi", t), stage[:, t % 2, :, :], ACT.Identity).then_inc(meas_hi, 1)

            def x_part(part):
                act.wait_ge(turned, part + 1)
                act.activation(x_of("hi", part), ps[:, 4 * part:4 * part + 4, :], ACT.Identity).then_inc(x_hi_done, 1)

            def negate():
                act.wait_ge(x_hi_done, 2)
                act.activation(x_of("hi", NEG), x_of("hi", IM).bitcast(F32), ACT.Identity,
                               scale=-1.0).then_inc(x_hi_done, 1)
                act.wait_ge(x_split, 2)
                act.activation(x_of("lo", NEG), x_of("lo", IM).bitcast(F32), ACT.Identity,
                               scale=-1.0).then_inc(x_neg, 1)

            def square_meas(mt):
                act.wait_ge(measured, 2 * mt + 1)
                if mt >= 2:
                    act.wait_ge(amp_sq, mt - 1)
                act.activation(im_sq[:, mt % 2, :], ps[:, 2 * (mt % 2) + 1, :], ACT.Square).then_inc(meas_sq, 1)
                act.wait_ge(measured, 2 * mt + 2)
                act.activation(amp[:, mt, :], ps[:, 2 * (mt % 2), :], ACT.Square).then_inc(meas_sq, 1)

            def begin_weights(c, p):
                act.wait_ge(cosine, N_PAIRS * c + p + 1)
                for a, b, first in terms(p):
                    if first:
                        act.wait_ge(units, NT * c + b + 1)
                        act.activation(inv[:, b, :], slot(p)[:, 0, :], ACT.Identity, scale=s_now[:, a, b:b + 1],
                                       bias=s_now[:, b, b:b + 1]).then_inc(begun, 1)

            def chunk(s, splits, next_too):
                square(s, 2)
                square(s, 3)
                for n in (2, 3):
                    root(s, n)
                    copy(s, n)
                for c, n in splits[:1]:
                    split_attn(c, n)
                if not next_too:
                    split_meas(0)
                    split_meas(1)
                act.wait_ge(strength_set, s + 1)
                begin_weights(s, 0)
                begin_weights(s, 1)
                for c, n in splits[1:2]:
                    split_attn(c, n)
                if not next_too:
                    split_meas(2)
                    split_meas(3)
                    x_part(RE)
                    x_part(IM)
                begin_weights(s, 3)
                for c, n in splits[2:]:
                    split_attn(c, n)
                if not next_too:
                    negate()
                    square_meas(0)
                    square_meas(1)
                if next_too:
                    for n in range(2):
                        square(s + 1, n)
                    for n in range(2):
                        root(s + 1, n)
                    copy(s + 1, 0)
                act.wait_ge(norm_sum, s + 1)
                act.activation(norm[:, :], norm[:, :], ACT.Sqrt).then_inc(norm_root, 1)
                if next_too:
                    copy(s + 1, 1)
                act.wait_ge(norm_inv, s + 1)
                act.activation(sup[:, :, :], sup[:, :, :], ACT.Identity, scale=norm[:, 0:1]).then_inc(sup_scaled, 1)

            split_attn(0, 0)
            split_attn(0, 1)
            for t in range(W_LOADS):
                act.wait_ge(tile_in[t % 2], 16 * (t // 2 + 2))
                act.activation(w3_hi[:, t, :, :], stage[:, t % 2, :, :], ACT.Identity).then_inc(hi_done, 1)
            act.wait_ge(tiny_set, 1)
            for n in range(2, NT + 1):
                split_attn(n // NT, n % NT)
            for n in range(2):
                square(0, n)
            for n in range(2):
                root(0, n)
                copy(0, n)
            with act.Fori(0, CHUNKS - 2) as s:
                chunk(s, ahead(s), True)
            chunk(CHUNKS - 2, ahead(CHUNKS - 2)[:3], True)
            chunk(CHUNKS - 1, [], False)
            square_meas(2)
            square_meas(3)

        @block.vector
        def _(dve):
            dve.sem_inc(w_scaled, 3)
            dve.sem_inc(sup_sum, 3)
            for t in range(W_LOADS):
                dve.wait_ge(hi_done, t + 3)
                dve.tensor_tensor(w3_lo[:, t, :, :], stage[:, t % 2, :, :], w3_hi[:, t, :, :].bitcast(F32),
                                  ALU.subtract).then_inc(w_split, 1)

            def unit_vector(c, n):
                dve.wait_ge(rooted, NT * c + n + 1)
                dve.tensor_scalar(is_zero[:, n, :], mag[:, n, :], ZERO_MAG, None, ALU.is_le).then_inc(flagged, 1)
                dve.reciprocal(inv[:, n, :], mag[:, n, :]).then_inc(inverted, 1)
                dve.wait_ge(inverted, NT * c + n + 1)
                dve.wait_ge(free, NT * c + n + NT + 1)
                dve.tensor_tensor(unit[:, :, n, :], unit[:, :, n, :],
                                  inv[:, n, :].unsqueeze(1).broadcast_to([P, 2, D]), ALU.mult).then_inc(units, 1)

            def multiply_pair(c, p):
                i, j = PAIRS[p]
                dve.wait_ge(units, NT * c + j + 1)
                if p == 0:
                    dve.wait_ge(sq_sum, NT * c + NT)
                elif p == 1:
                    dve.wait_ge(stored, 16 * c + 16)
                else:
                    dve.wait_ge(begun, NT * c + before(p - 1)[0])
                    if p > 2:
                        dve.wait_ge(weighted, TERMS * c + before(p - 1)[1])
                dve.tensor_tensor(slot(p)[:, :, :], unit[:, :, i, :], unit[:, :, j, :],
                                  ALU.mult).then_inc(multiplied, 1)
                if p >= ON_POOL:
                    dve.wait_ge(multiplied, N_PAIRS * c + p + 1)
                    dve.tensor_tensor(slot(p)[:, 0, :], slot(p)[:, 0, :], slot(p)[:, 1, :],
                                      ALU.add).then_inc(dot_sum, 1)

            def weigh_pair(c, p):
                dve.wait_ge(cosine, N_PAIRS * c + p + 1)
                new, old = before(p)
                for a, b, first in terms(p):
                    if first:
                        continue
                    dve.wait_ge(begun, NT * c + new)
                    if old:
                        dve.wait_ge(weighted, TERMS * c + old)
                    dve.scalar_tensor_tensor(out=inv[:, b, :], in0=slot(p)[:, 0, :], scalar=s_now[:, a, b:b + 1],
                                             in1=inv[:, b, :], op0=ALU.mult, op1=ALU.add).then_inc(weighted, 1)

            def apply(c, first, tokens, k):
                some = slice(first, first + tokens)
                dve.tensor_tensor(inv[:, some, :], inv[:, some, :], mag[:, some, :],
                                  ALU.mult).then_inc(w_scaled, 1)
                dve.wait_ge(w_scaled, 3 * c + 3 + k)
                for n in range(first, first + tokens):
                    dve.tensor_tensor(unit[:, :, n, :], unit[:, :, n, :],
                                      inv[:, n, :].unsqueeze(1).broadcast_to([P, 2, D]),
                                      ALU.mult).then_inc(applied, 1)

            def chunk(c, next_too):
                dve.tensor_scalar(s_now[:, :, :].rearrange("p i j -> p (i j)"),
                                  strength[:, bass.ds(c * NT * NT, NT * NT)], 1.0, None, ALU.mult
                                  ).then_inc(strength_set, 1)
                unit_vector(c, 1)
                multiply_pair(c, 0)
                unit_vector(c, 2)
                dve.wait_ge(strength_set, c + 1)
                multiply_pair(c, 1)
                multiply_pair(c, 2)
                unit_vector(c, 3)
                if not next_too:
                    for part in (RE, IM):
                        dve.wait_ge(x_hi_done, part + 1)
                        dve.tensor_tensor(x_of("lo", part), ps[:, 4 * part:4 * part + 4, :],
                                          x_of("hi", part).bitcast(F32), ALU.subtract).then_inc(x_split, 1)
                weigh_pair(c, 1)
                multiply_pair(c, 3)
                weigh_pair(c, 2)
                multiply_pair(c, 4)
                weigh_pair(c, 3)
                multiply_pair(c, 5)
                dve.wait_ge(weighted, TERMS * c + before(4)[1])
                apply(c, 0, 1, 1)
                weigh_pair(c, 4)
                dve.wait_ge(weighted, TERMS * c + before(5)[1])
                apply(c, 1, 1, 2)
                weigh_pair(c, 5)
                dve.wait_ge(weighted, TERMS * c + TERMS)
                dve.wait_ge(applied, NT * c + 2)
                dve.tensor_tensor(sup[:, :, :], unit[:, :, 0, :], unit[:, :, 1, :], ALU.add).then_inc(sup_sum, 1)
                apply(c, 2, 2, 3)
                for n in (2, 3):
                    dve.wait_ge(applied, NT * c + n + 1)
                    dve.wait_ge(sup_sum, 3 * c + n + 2)
                    dve.tensor_tensor(sup[:, :, :], sup[:, :, :], unit[:, :, n, :], ALU.add).then_inc(sup_sum, 1)
                dve.wait_ge(applied, NT * c + NT)
                dve.wait_ge(sup_sum, 3 * c + 6)
                dve.tensor_tensor_reduce(out=inv[:, 2:4, :], in0=sup[:, :, :], in1=sup[:, :, :], scale=1.0,
                                         scalar=EPS, op0=ALU.mult, op1=ALU.add,
                                         accum_out=norm[:, :]).then_inc(norm_sum, 1)
                if next_too:
                    unit_vector(c + 1, 0)
                dve.wait_ge(norm_root, c + 1)
                dve.reciprocal(norm[:, :], norm[:, :]).then_inc(norm_inv, 1)

            unit_vector(0, 0)
            with dve.Fori(0, CHUNKS - 1) as c:
                chunk(c, True)
            chunk(CHUNKS - 1, False)
            for mt in range(DK):
                dve.wait_ge(meas_sq, 2 * mt + 2)
                dve.tensor_tensor(amp[:, mt, :], amp[:, mt, :], im_sq[:, mt % 2, :], ALU.add).then_inc(amp_sq, 1)

        @block.tensor
        def _(pe):
            def weights(n, w, kt):
                if n < 3:
                    t = n * 4 + w * 2 + kt // 2
                    return int_w["hi"][:, t, kt % 2, :], int_w["lo"][:, t, kt % 2, :]
                return w3_hi[:, w * 2 + kt // 2, kt % 2, :], w3_lo[:, w * 2 + kt // 2, kt % 2, :]

            with pe.Fori(0, CHUNKS) as c:
                for n in range(NT):
                    pe.wait_ge(neg_done, NT * c + n + 1)
                    pe.wait_ge(free, NT * c + n + 1)
                    if n == 3:
                        pe.wait_ge(w_split, W_LOADS)
                    R, I = ps[:, 2 * n, :], ps[:, 2 * n + 1, :]
                    for kt in range(DK):
                        cols = slice(kt * CB, (kt + 1) * CB)
                        for out, comp, w in ((R, RE, 0), (I, RE, 1), (I, IM, 0), (R, NEG, 1)):
                            first = kt == 0 and comp == RE
                            end = kt == DK - 1 and comp in (IM, NEG)
                            hi, lo = a_hi[:, n % 2, comp, cols], a_lo[:, n % 2, comp, cols]
                            wh, wl = weights(n, w, kt)
                            pe.matmul(out, hi, wh, start=first, stop=False)
                            pe.matmul(out, hi, wl, start=False, stop=False)
                            last = pe.matmul(out, lo, wh, start=False, stop=end)
                    last.then_inc(ready, 1)

            pe.wait_ge(half_in, 16 * HC)
            for part in (RE, IM):
                pe.wait_ge(free, NT * CHUNKS + 2 * part + 2)
                for kt in range(DK):
                    for c in range(HC):
                        last = pe.transpose(ps[:, 4 * part + kt, c * P:(c + 1) * P],
                                            half_sup[:, c, part, kt * P:(kt + 1) * P], keep["ident"][:, :])
                last.then_inc(turned, 1)
            for mt in range(DK):
                real, imag = 2 * (mt % 2), 2 * (mt % 2) + 1
                if mt >= 2:
                    pe.wait_ge(meas_sq, 2 * mt - 2)
                for bank, w, comp in ((real, 0, RE), (imag, M_TILES, RE), (imag, 0, IM), (real, M_TILES, NEG)):
                    if comp == NEG:
                        pe.wait_ge(x_neg, 1)
                    else:
                        pe.wait_ge(x_split, comp + 1)
                    pe.wait_ge(meas_split, w + M_TILES)
                    for kt in range(DK):
                        cols = slice(mt * P, (mt + 1) * P)
                        hi, lo = m_of("hi", w + kt // 2)[:, kt % 2, cols], m_of("lo", w + kt // 2)[:, kt % 2, cols]
                        x_hi, x_lo = x_of("hi", comp)[:, kt, :], x_of("lo", comp)[:, kt, :]
                        pe.matmul(ps[:, bank, :], hi, x_hi, start=comp == RE and kt == 0, stop=False)
                        pe.matmul(ps[:, bank, :], hi, x_lo, start=False, stop=False)
                        last = pe.matmul(ps[:, bank, :], lo, x_hi, start=False, stop=comp != RE and kt == DK - 1)
                    if comp != RE:
                        last.then_inc(measured, 1)


def head(nc, io, scratch, keep):
    HALF = B // 2
    HC = HALF // CB
    RE, IM, NEG = range(3)
    MEAS_R, MEAS_I, POST, TOP1, TOP2, W_TILES = 0, 4, 8, 12, 16, 18
    W_LOADS = W_TILES // 2
    W_ORDER = [4, 5, 0, 1, 2, 3, 6, 7, 8]
    with ExitStack() as ctx:
        m = Mem(nc, ctx, "head_")
        w_stage = m.sb("w_stage", [P, 2, 2, D])
        w_hi = m.sb("w_hi", [P, W_TILES, D], F32R)
        w_lo = m.sb("w_lo", [P, W_TILES, D], F32R)
        sup = m.sb("sup", [P, HC, 2, D])
        x_hi = m.sb("x_hi", [P, 3, DK, HALF], F32R)
        x_lo = m.sb("x_lo", [P, 3, DK, HALF], F32R)
        amp = m.sb("amp", [P, DK, HALF])
        im_sq = m.sb("im_sq", [P, 2, HALF])
        c_hi = m.sb("c_hi", [P, DK, HALF], F32R)
        c_lo = m.sb("c_lo", [P, DK, HALF], F32R)
        act_a = m.sb("act_a", [P, DK, HALF])
        act_b = m.sb("act_b", [P, DK, HALF])
        sums = m.sb("sums", [P, 2, HALF])
        stat = m.sb("stat", [P, 3, HALF])
        h2 = m.sb("h2", [P, 2, HALF])
        y = m.sb("y", [1, 2, HALF])
        bias = m.sb("bias", [P, 5, DK])
        mean_w = m.sb("mean_w", [P, P])
        ps = m.psum("ps", [P, 8, BANK])

        bias_in = m.sem("bias_in")
        w_in = [m.sem(f"w_in{i}") for i in range(2)]
        w_hi_done = m.sem("w_hi_done")
        w_split = m.sem("w_split")
        sup_in = m.sem("sup_in")
        top_x_in = m.sem("top_x_in")
        mean_set = m.sem("mean_set")
        amp_in = m.sem("amp_in")
        turned = m.sem("turned")
        x_hi_done = m.sem("x_hi_done")
        x_split = m.sem("x_split")
        x_neg = m.sem("x_neg")
        measured = m.sem("measured")
        meas_sq = m.sem("meas_sq")
        amp_sq = m.sem("amp_sq")
        amp_root = m.sem("amp_root")
        c_hi_done = m.sem("c_hi_done")
        c_split = m.sem("c_split")
        posted = m.sem("posted")
        post_out = m.sem("post_out")
        summed = m.sem("summed")
        col_mean = m.sem("col_mean")
        var = m.sem("var")
        std = m.sem("std")
        centred = m.sem("centred")
        inverse = m.sem("inverse")
        normed = m.sem("normed")
        gelu = m.sem("gelu")
        top1 = m.sem("top1")
        top1_sum = m.sem("top1_sum")
        top2 = m.sem("top2")
        top2_out = m.sem("top2_out")
        top3 = m.sem("top3")
        top3_out = m.sem("top3_out")
        stored = m.sem("stored")
        block = ctx.enter_context(nc.Block())
        src, top_part, out = scratch["sup"], scratch["pre"], io["out"]
        T_AMP, T_Z, T_H1 = 0, DK, 2 * DK

        @block.sync
        def _(sp):
            def load_top_x(hb):
                sp.wait_ge(summed, 6 * hb + 6)
                sp.dma_start(act_b[:, :, :], top_part[8, :, :, hb * HALF:(hb + 1) * HALF].rearrange("k p b -> p k b")
                             ).then_inc(top_x_in, 16)

            for c in range(HC):
                sp.dma_start(sup[:, c, :, :], src[HC + c]).then_inc(sup_in, 16)
            for i, t in enumerate(W_ORDER):
                if i >= 2:
                    sp.wait_ge(w_split, i - 1)
                sp.dma_start(w_stage[:, i % 2, :, :], io["w_head"][t]).then_inc(w_in[i % 2], 16)
                if i == 1:
                    sp.dma_start(amp[:, :, :], scratch["amp"].rearrange("k p b -> p k b")).then_inc(amp_in, 16)
                    sp.dma_start(bias[:, :, :], io["b_head"]).then_inc(bias_in, 16)
            load_top_x(0)
            load_top_x(1)
            for hb in range(2):
                sp.wait_ge(top3_out, hb + 1)
                sp.dma_start(out[hb], y[0:1, hb, :]).then_inc(stored, 16)
            sp.wait_ge(stored, 32)

        @block.gpsimd
        def _(pool):
            nc.gpsimd.memset(mean_w[:, :], 1.0 / D).then_inc(mean_set, 1)
            for hb in range(2):
                for mt in range(DK):
                    pool.wait_ge(var, 4 * hb + 1)
                    nc.gpsimd.tensor_tensor(act_a[:, mt, :], act_a[:, mt, :], stat[:, 0, :],
                                            ALU.subtract).then_inc(centred, 1)

        @block.scalar
        def _(act):
            def split_w(i):
                act.wait_ge(w_in[i % 2], 16 * (i // 2 + 1))
                w = 2 * W_ORDER[i]
                act.activation(w_hi[:, w:w + 2, :], w_stage[:, i % 2, :, :], ACT.Identity).then_inc(w_hi_done, 1)

            def x_part(part):
                act.wait_ge(turned, part + 1)
                act.activation(x_hi[:, part, :, :], ps[:, 4 * part:4 * part + 4, :], ACT.Identity).then_inc(x_hi_done, 1)

            def negate():
                act.wait_ge(x_hi_done, 2)
                act.activation(x_hi[:, NEG, :, :], x_hi[:, IM, :, :].bitcast(F32), ACT.Identity,
                               scale=-1.0).then_inc(x_hi_done, 1)
                act.wait_ge(x_split, 2)
                act.activation(x_lo[:, NEG, :, :], x_lo[:, IM, :, :].bitcast(F32), ACT.Identity,
                               scale=-1.0).then_inc(x_neg, 1)

            def square(mt):
                act.wait_ge(measured, 2 * mt + 1)
                if mt >= 2:
                    act.wait_ge(amp_sq, mt - 1)
                act.activation(im_sq[:, mt % 2, :], ps[:, 2 * (mt % 2) + 1, :], ACT.Square).then_inc(meas_sq, 1)
                act.wait_ge(measured, 2 * mt + 2)
                act.wait_ge(c_split, T_AMP + mt + 1)
                act.activation(amp[:, mt, :], ps[:, 2 * (mt % 2), :], ACT.Square).then_inc(meas_sq, 1)

            def amplitude(hb, mt):
                if hb:
                    act.wait_ge(amp_sq, mt + 1)
                else:
                    act.wait_ge(amp_in, 16)
                act.activation(amp[:, mt, :], amp[:, mt, :], ACT.Sqrt).then_inc(amp_root, 1)
                act.wait_ge(amp_root, 4 * hb + mt + 1)
                if hb:
                    act.wait_ge(top2, 2)
                act.activation(c_hi[:, mt, :], amp[:, mt, :], ACT.Identity).then_inc(c_hi_done, 1)

            def post(hb):
                for mt in range(DK):
                    act.wait_ge(posted, 4 * hb + mt + 1)
                    act.activation(act_a[:, mt, :], ps[:, 4 + mt, :], ACT.Identity,
                                   bias=bias[:, 0, mt:mt + 1]).then_inc(post_out, 1)
                    act.activation(act_b[:, mt, :], ps[:, 4 + mt, :], ACT.Square,
                                   bias=bias[:, 0, mt:mt + 1]).then_inc(post_out, 1)

            def deviation(hb):
                act.wait_ge(var, 4 * hb + 4)
                act.activation(stat[:, 1, :], stat[:, 1, :], ACT.Sqrt).then_inc(std, 1)

            def z(hb):
                for mt in range(DK):
                    act.wait_ge(normed, 4 * hb + mt + 1)
                    act.activation(act_a[:, mt, :], act_a[:, mt, :], ACT.Gelu, scale=bias[:, 1, mt:mt + 1],
                                   bias=bias[:, 2, mt:mt + 1]).then_inc(gelu, 1)
                    act.wait_ge(gelu, 4 * hb + mt + 1)
                    act.activation(c_hi[:, mt, :], act_a[:, mt, :], ACT.Identity).then_inc(c_hi_done, 1)

            def h1(hb):
                for mt in range(DK):
                    act.wait_ge(top1_sum, 4 * hb + mt + 1)
                    act.activation(c_hi[:, mt, :], act_b[:, mt, :], ACT.Relu).then_inc(c_hi_done, 1)

            def h2_out(hb):
                for mt in range(2):
                    act.wait_ge(top2, 2 * hb + mt + 1)
                    act.activation(h2[:, mt, :], ps[:, 4 + mt, :], ACT.Relu,
                                   bias=bias[:, 3, mt:mt + 1]).then_inc(top2_out, 1)

            def result(hb):
                act.wait_ge(top3, hb + 1)
                act.activation(y[0:1, hb, :], ps[0:1, 6, :], ACT.Copy).then_inc(top3_out, 1)

            x_part(RE)
            x_part(IM)
            split_w(0)
            split_w(1)
            for mt in range(DK):
                amplitude(0, mt)
            split_w(2)
            split_w(3)
            negate()
            split_w(4)
            split_w(5)
            act.wait_ge(bias_in, 16)
            post(0)
            for i in range(6, W_LOADS):
                split_w(i)
            square(0)
            deviation(0)
            z(0)
            square(1)
            square(2)
            h1(0)
            h2_out(0)
            for mt in range(DK - 1):
                amplitude(1, mt)
            result(0)
            square(DK - 1)
            amplitude(1, DK - 1)
            post(1)
            deviation(1)
            z(1)
            h1(1)
            h2_out(1)
            result(1)

        @block.vector
        def _(dve):
            def split_w(i):
                dve.wait_ge(w_hi_done, i + 1)
                w = 2 * W_ORDER[i]
                dve.tensor_tensor(w_lo[:, w:w + 2, :], w_stage[:, i % 2, :, :],
                                  w_hi[:, w:w + 2, :].bitcast(F32), ALU.subtract).then_inc(w_split, 1)

            def x_part(part):
                dve.wait_ge(x_hi_done, part + 1)
                dve.tensor_tensor(x_lo[:, part, :, :], ps[:, 4 * part:4 * part + 4, :],
                                  x_hi[:, part, :, :].bitcast(F32), ALU.subtract).then_inc(x_split, 1)

            def add_squares(mt):
                dve.wait_ge(meas_sq, 2 * mt + 2)
                dve.tensor_tensor(amp[:, mt, :], amp[:, mt, :], im_sq[:, mt % 2, :], ALU.add).then_inc(amp_sq, 1)

            def split_c(hb, before, mt, x):
                dve.wait_ge(c_hi_done, 12 * hb + before + mt + 1)
                dve.tensor_tensor(c_lo[:, mt, :], x[:, mt, :], c_hi[:, mt, :].bitcast(F32),
                                  ALU.subtract).then_inc(c_split, 1)

            def sum_tiles(hb):
                for mt in range(1, DK):
                    for i, t in enumerate((act_a, act_b)):
                        dve.wait_ge(post_out, 8 * hb + 2 * mt + i + 1)
                        if mt > 1:
                            dve.wait_ge(summed, 6 * hb + 2 * mt - 3 + i)
                        dve.tensor_tensor(sums[:, i, :], t[:, 0, :] if mt == 1 else sums[:, i, :], t[:, mt, :],
                                          ALU.add).then_inc(summed, 1)

            def variance(hb):
                dve.wait_ge(col_mean, 2 * hb + 2)
                dve.tensor_copy(stat[:, 0, :], ps[:, 4, :]).then_inc(var, 1)
                dve.wait_ge(var, 4 * hb + 1)
                dve.tensor_tensor(stat[:, 2, :], stat[:, 0, :], stat[:, 0, :], ALU.mult).then_inc(var, 1)
                dve.wait_ge(var, 4 * hb + 2)
                dve.tensor_tensor(stat[:, 1, :], ps[:, 5, :], stat[:, 2, :], ALU.subtract).then_inc(var, 1)
                dve.wait_ge(var, 4 * hb + 3)
                dve.tensor_scalar(stat[:, 1, :], stat[:, 1, :], 0.0, LN_EPS, ALU.max, ALU.add).then_inc(var, 1)

            def normalise(hb):
                dve.wait_ge(std, hb + 1)
                dve.reciprocal(stat[:, 2, :], stat[:, 1, :]).then_inc(inverse, 1)
                dve.wait_ge(inverse, hb + 1)
                for mt in range(DK):
                    dve.wait_ge(centred, 4 * hb + mt + 1)
                    dve.tensor_tensor(act_a[:, mt, :], act_a[:, mt, :], stat[:, 2, :], ALU.mult).then_inc(normed, 1)
                    if mt:
                        split_c(hb, T_Z, mt - 1, act_a)
                split_c(hb, T_Z, DK - 1, act_a)

            def top1_out(hb):
                dve.wait_ge(top_x_in, 16 * (hb + 1))
                for mt in range(DK):
                    dve.wait_ge(top1, 4 * hb + mt + 1)
                    dve.tensor_tensor(act_b[:, mt, :], ps[:, 4 + mt, :], act_b[:, mt, :], ALU.add).then_inc(top1_sum, 1)
                for mt in range(DK):
                    dve.wait_ge(c_hi_done, 12 * hb + T_H1 + mt + 1)
                    dve.scalar_tensor_tensor(out=c_lo[:, mt, :], in0=act_b[:, mt, :], scalar=0.0,
                                             in1=c_hi[:, mt, :].bitcast(F32), op0=ALU.max,
                                             op1=ALU.subtract).then_inc(c_split, 1)

            x_part(RE)
            x_part(IM)
            split_w(0)
            split_w(1)
            for mt in range(DK):
                split_c(0, T_AMP, mt, amp)
            for i in range(2, 6):
                split_w(i)
            sum_tiles(0)
            for i in range(6, W_LOADS):
                split_w(i)
            add_squares(0)
            variance(0)
            normalise(0)
            add_squares(1)
            add_squares(2)
            top1_out(0)
            for mt in range(DK - 1):
                split_c(1, T_AMP, mt, amp)
            add_squares(DK - 1)
            split_c(1, T_AMP, DK - 1, amp)
            sum_tiles(1)
            variance(1)
            normalise(1)
            top1_out(1)

        @block.tensor
        def _(pe):
            def product(bank, w, cols, hi_x, lo_x, first, end):
                hi, lo = w_hi[:, w, cols], w_lo[:, w, cols]
                pe.matmul(ps[:, bank, :], hi, hi_x, start=first, stop=False)
                pe.matmul(ps[:, bank, :], hi, lo_x, start=False, stop=False)
                return pe.matmul(ps[:, bank, :], lo, hi_x, start=False, stop=end)

            def turn(part):
                for kt in range(DK):
                    for c in range(HC):
                        last = pe.transpose(ps[:, 4 * part + kt, c * P:(c + 1) * P],
                                            sup[:, c, part, kt * P:(kt + 1) * P], keep["ident"][:, :])
                last.then_inc(turned, 1)

            def measure(mt, steps):
                real, imag = 2 * (mt % 2), 2 * (mt % 2) + 1
                if 0 in steps and mt >= 2:
                    pe.wait_ge(meas_sq, 2 * mt - 2)
                order = ((real, MEAS_R, RE), (imag, MEAS_I, RE), (imag, MEAS_R, IM), (real, MEAS_I, NEG))
                for step in steps:
                    bank, w, comp = order[step]
                    if comp == NEG:
                        pe.wait_ge(x_neg, 1)
                    pe.wait_ge(w_split, 4 if w == MEAS_R else 6)
                    for kt in range(DK):
                        last = product(bank, w + kt, slice(mt * P, (mt + 1) * P), x_hi[:, comp, kt, :],
                                       x_lo[:, comp, kt, :], comp == RE and kt == 0, comp != RE and kt == DK - 1)
                    if comp != RE:
                        last.then_inc(measured, 1)

            def layer(hb, before, tile, tiles, done):
                for kt in range(DK):
                    pe.wait_ge(c_split, 12 * hb + before + kt + 1)
                    for mt in range(tiles):
                        w, cols = tile(kt, mt)
                        last = product(4 + mt, w, cols, c_hi[:, kt, :], c_lo[:, kt, :], kt == 0, kt == DK - 1)
                        if kt == DK - 1:
                            last.then_inc(done, 1)

            def post(hb):
                pe.wait_ge(w_split, 2)
                if hb:
                    pe.wait_ge(top3_out, 1)
                layer(hb, T_AMP, lambda kt, mt: (POST + kt, slice(mt * P, (mt + 1) * P)), DK, posted)

            def means(hb):
                pe.wait_ge(mean_set, 1)
                for i in range(2):
                    pe.wait_ge(summed, 6 * hb + 5 + i)
                    pe.matmul(ps[:, 4 + i, :], mean_w[:, :], sums[:, i, :], start=True, stop=True).then_inc(col_mean, 1)

            def top_1(hb):
                pe.wait_ge(var, 4 * hb + 3)
                pe.wait_ge(w_split, W_LOADS)
                layer(hb, T_Z, lambda kt, mt: (TOP1 + kt, slice(mt * P, (mt + 1) * P)), DK, top1)

            def top_2(hb):
                pe.wait_ge(top1_sum, 4 * hb + 4)
                layer(hb, T_H1, lambda kt, mt: (TOP2 + kt // 2, slice((kt % 2) * 256 + mt * P,
                                                                     (kt % 2) * 256 + (mt + 1) * P)), 2, top2)

            def top_3(hb):
                pe.wait_ge(top2_out, 2 * hb + 2)
                for mt in range(2):
                    last = pe.matmul(ps[0:1, 6, :], bias[:, 4, mt:mt + 1], h2[:, mt, :], start=mt == 0, stop=mt == 1)
                last.then_inc(top3, 1)

            pe.wait_ge(sup_in, 16 * HC)
            turn(RE)
            turn(IM)
            pe.wait_ge(x_split, 2)
            post(0)
            measure(0, range(4))
            means(0)
            measure(1, range(4))
            measure(2, range(4))
            top_1(0)
            measure(3, range(2))
            top_2(0)
            top_3(0)
            measure(3, range(2, 4))
            post(1)
            means(1)
            top_1(1)
            top_2(1)
            top_3(1)


def build(nc, io):
    scratch = {
        "pre": nc.dram_tensor("pre", (17, GROUP, P, B), F32).ap(),
        "mixed": nc.dram_tensor("mixed", (CHUNKS, NT, P, H, P), F32).ap(),
        "attn": nc.dram_tensor("attn", (CHUNKS, 2, NT, P, DK * CB), F32).ap(),
        "amp": nc.dram_tensor("amp", (DK, P, B // 2), F32).ap(),
        "sup": nc.dram_tensor("sup", (CHUNKS, P, 2, D), F32).ap(),
    }
    with ExitStack() as ctx:
        m = Mem(nc, ctx, "keep_")
        keep = {
            "ident": m.sb("ident", [P, P]),
            "ids": m.sb("ids", [P, CHUNKS, NT], I32),
            "strength": m.sb("strength", [P, CHUNKS * NT * NT]),
        }
        encoders(nc, io, scratch, keep)
        attention(nc, io, scratch, keep)
        with ExitStack() as later:
            w = Mem(nc, later, "int_")
            int_w = {part: w.sb("w_" + part, [P, 12, 2, D], F32R) for part in ("hi", "lo")}
            out_proj(nc, io, scratch, keep, int_w)
            interference(nc, io, scratch, keep, int_w)
        head(nc, io, scratch, keep)


def kernel(**inputs):
    import numpy as np
    import concourse.bacc as bacc
    from concourse.bass_utils import run_bass_kernel_spmd as run

    v = {k.replace("L0_rec_", ""): np.asarray(a) for k, a in inputs.items()}

    def rows(w):
        return w.reshape(-1, P, w.shape[1])

    def cols(*vectors):
        return np.concatenate([x.reshape(-1, P) for x in vectors]).T

    w_enc = np.concatenate([v["er_W1"].T, v["ei_W1"].T, v["W_top1"][D:], v["er_W2"].T, v["ei_W2"].T], axis=1)
    head_w = np.concatenate([
        rows(v["meas_Mr"].T), rows(v["meas_Mi"].T), rows(v["post_W"].T), rows(v["W_top1"][:D]),
        rows(v["W_top2"]).reshape(2, 2, P, 256).transpose(0, 2, 1, 3).reshape(2, P, D)])
    int_w = np.stack([v["int_Wr"], v["int_Wi"]], axis=1).transpose(0, 1, 3, 2)
    zero = np.zeros(256, np.float32)
    arrays = {
        "xT": v["r_x"].T.reshape(KT, P, B),
        "w_enc": w_enc.reshape(KT, P, 17, D).transpose(2, 0, 1, 3),
        "b_enc": cols(v["er_b1"], v["ei_b1"], v["b_top1"], v["er_b2"], v["ei_b2"]),
        "ln_g": cols(v["er_g1"], v["ei_g1"]),
        "ln_b": cols(v["er_be1"], v["ei_be1"]),
        "ids": v["ids"].reshape(CHUNKS, P, NT).transpose(1, 0, 2),
        "tbl_0": v["tbl_0"], "tbl_1": v["tbl_1"], "tbl_2": v["tbl_2"], "tbl_3": v["tbl_3"],
        "w_qkv": np.concatenate([rows(v[w].T) for w in ("Wq_r", "Wq_i", "Wk_r", "Wk_i", "Wv_r", "Wv_i")]),
        "b_qk": cols(v["bq_r"], v["bq_i"], v["bk_r"], v["bk_i"]).reshape(P, 4, DK),
        "b_v": np.stack([v["bv_r"].reshape(H, HD), v["bv_i"].reshape(H, HD)]).transpose(0, 2, 1).reshape(P, H),
        "w_o": np.stack([v["Wo_r"].T, v["Wo_i"].T]).reshape(2, DK, P, D).transpose(0, 2, 1, 3),
        "b_o": cols(v["bo_r"], v["bo_i"]).reshape(P, 2, DK),
        "w_int": int_w.reshape(16, 2, P, D).transpose(0, 2, 1, 3),
        "w_head": head_w.reshape(9, 2, P, D).transpose(0, 2, 1, 3),
        "b_head": cols(v["post_b"], v["post_g"], v["post_be"], v["b_top2"], zero, v["W_top3"][:, 0], zero
                       ).reshape(P, 5, DK),
    }
    arrays = {name: np.ascontiguousarray(a) for name, a in arrays.items()}
    nc = bacc.Bacc("TRN2", target_bir_lowering=False, num_devices=1)
    io = {name: nc.dram_tensor(name, a.shape, mybir.dt.from_np(a.dtype), kind="ExternalInput").ap()
          for name, a in arrays.items()}
    y = nc.dram_tensor("y", (2, 1, B // 2), F32, kind="ExternalOutput").ap()
    io["out"] = y
    build(nc, io)
    result = run(nc, [arrays], core_ids=[0])
    return result.results[0]["y"].reshape(B, 1)
```
